# Optimizing a Trainium2 kernel written in Bass

```python
import numpy as np
import jax
import jax.numpy as jnp

def _softmax(x, axis=-1):
    return jax.nn.softmax(x, axis=axis)

def _gelu(x):
    return jax.nn.gelu(x, approximate=True)

def _silu(x):
    return jax.nn.silu(x)

def _sigmoid(x):
    return jax.nn.sigmoid(x)

def _layernorm(x, axis=-1, eps=1e-05):
    m = jnp.mean(x, axis=axis, keepdims=True)
    v = jnp.var(x, axis=axis, keepdims=True)
    return (x - m) / jnp.sqrt(v + eps)

def _scatter_add(tgt, idx, src, axis=0):
    return tgt.at[idx].add(src)

def _segment_sum(src, seg, n):
    return jax.ops.segment_sum(src, seg, n)
kernel_name = 'mk_adaln_attn_ffn_d4_seqx_r8_5b091e'

def setup_inputs(seed: int=0):
    np.random.seed(seed)
    _w = jnp.asarray

    def _rec_inputs():
        import jax
        import jax.numpy as jnp
        _rk = jax.random.key(seed)
        x = -0.000125 + 0.9999 * jax.random.normal(jax.random.fold_in(_rk, 1), (4, 256, 256), jnp.float32)
        _lenS = 256 - jax.random.randint(jax.random.fold_in(_rk, 7), (4,), 0, max(1, 256 // 4) + 1, jnp.int32)
        _lenS2 = 256 - jax.random.randint(jax.random.fold_in(_rk, 8), (4,), 0, max(1, 256 // 4) + 1, jnp.int32)
        fside_BxSxS_0 = -1.52775e-05 + 0.999936 * jax.random.normal(jax.random.fold_in(_rk, 11), (4, 256, 256), jnp.float32)
        cond_512 = -5.03954e-05 + 1.00559 * jax.random.normal(jax.random.fold_in(_rk, 12), (4, 64), jnp.float32)
        return (x, fside_BxSxS_0, cond_512)
    x, fside_BxSxS_0, cond_512 = _rec_inputs()

    def _L0_cond_setup():
        import jax, jax.numpy as jnp
        from jax import lax
        import numpy as np
        B, T, C, TD = (8, 256, 256, 64)

        def _bi_wkv(r, k, v, w, u, time_emb):
            tf = jax.nn.sigmoid(jnp.sum(time_emb, axis=-1))[:, None, None]
            decay = jnp.exp(-jnp.exp(w.astype(jnp.float32)))[None, :] * (0.5 + 0.5 * tf[:, :, 0])
            kf = k.astype(jnp.float32)
            vf = v.astype(jnp.float32)
            ek = jnp.exp(jnp.minimum(kf, 30.0))
            ekv = ek * vf

            def step(carry, x):
                a, b = carry
                ekv_t, ek_t = x
                a = a * decay + ekv_t
                b = b * decay + ek_t
                return ((a, b), (a, b))
            ekv_t = jnp.swapaxes(ekv, 0, 1)
            ek_t = jnp.swapaxes(ek, 0, 1)
            init = (jnp.zeros_like(decay), jnp.zeros_like(decay))
            _, (nf, df) = lax.scan(step, init, (ekv_t, ek_t))
            _, (nb, db) = lax.scan(step, init, (ekv_t, ek_t), reverse=True)
            nf = jnp.swapaxes(nf, 0, 1)
            df = jnp.swapaxes(df, 0, 1)
            nb = jnp.swapaxes(nb, 0, 1)
            db = jnp.swapaxes(db, 0, 1)
            euk = jnp.exp(jnp.minimum(u.astype(jnp.float32)[None, None, :] + kf, 30.0))
            num = nf + nb - ekv + euk * vf
            den = df + db - ek + euk
            base = jax.nn.sigmoid(r.astype(jnp.float32)) * (num / jnp.maximum(den, 1e-08))
            out = base * (0.8 + 0.2 * tf)
            return out.astype(r.dtype)
        key = jax.random.key(seed)
        ks = jax.random.split(key, 6)
        return {'r': jax.random.normal(ks[0], (B, T, C), dtype=jnp.float32), 'k': jax.random.normal(ks[1], (B, T, C), dtype=jnp.float32), 'v': jax.random.normal(ks[2], (B, T, C), dtype=jnp.float32), 'w': jax.random.normal(ks[3], (C,), dtype=jnp.float32), 'u': jax.random.normal(ks[4], (C,), dtype=jnp.float32), 'time_emb': jax.random.normal(ks[5], (B, TD), dtype=jnp.float32)}
    _L0_cond_all = _L0_cond_setup()
    _L0_cond_in = {k: v for k, v in _L0_cond_all.items() if k in ('w', 'u')}
    del _L0_cond_all

    def _L0_attn_setup():
        import jax, jax.numpy as jnp
        import numpy as np
        EMBED_DIM = 256
        NUM_HEADS = 16
        HEAD_DIM = EMBED_DIM // NUM_HEADS
        SCALE = HEAD_DIM ** (-0.5)
        NEG = -9000000000000000.0

        def _act_quant(x):
            s = 127.0 / jnp.clip(jnp.max(jnp.abs(x), axis=-1, keepdims=True), 1e-05)
            return jnp.clip(jnp.round(x * s), -128.0, 127.0) / s

        def _weight_quant(w):
            s = 1.0 / jnp.clip(jnp.mean(jnp.abs(w)), 1e-05)
            return jnp.clip(jnp.round(w * s), -1.0, 1.0) / s

        def _bitlinear(x, w):
            xq = x + jax.lax.stop_gradient(_act_quant(x) - x)
            wq = w + jax.lax.stop_gradient(_weight_quant(w) - w)
            return jnp.einsum('bnc,oc->bno', xq, wq)
        key = jax.random.key(seed)
        k1, k2, k3 = jax.random.split(key, 3)
        x = jax.random.normal(k1, (2, 256, EMBED_DIM), dtype=jnp.float32)
        w_qkv = jax.random.normal(k2, (3 * EMBED_DIM, EMBED_DIM), dtype=jnp.float32) * EMBED_DIM ** (-0.5)
        w_proj = jax.random.normal(k3, (EMBED_DIM, EMBED_DIM), dtype=jnp.float32) * EMBED_DIM ** (-0.5)
        return {'x': x, 'w_qkv': w_qkv, 'w_proj': w_proj}
    _L0_attn_all = _L0_attn_setup()
    _L0_attn_in = {k: v for k, v in _L0_attn_all.items() if k in ('w_qkv', 'w_proj')}
    del _L0_attn_all

    def _L0_cond2_setup():
        import jax, jax.numpy as jnp
        from jax import lax
        import numpy as np
        B, T, C, TD = (8, 256, 256, 64)

        def _bi_wkv(r, k, v, w, u, time_emb):
            tf = jax.nn.sigmoid(jnp.sum(time_emb, axis=-1))[:, None, None]
            decay = jnp.exp(-jnp.exp(w.astype(jnp.float32)))[None, :] * (0.5 + 0.5 * tf[:, :, 0])
            kf = k.astype(jnp.float32)
            vf = v.astype(jnp.float32)
            ek = jnp.exp(jnp.minimum(kf, 30.0))
            ekv = ek * vf

            def step(carry, x):
                a, b = carry
                ekv_t, ek_t = x
                a = a * decay + ekv_t
                b = b * decay + ek_t
                return ((a, b), (a, b))
            ekv_t = jnp.swapaxes(ekv, 0, 1)
            ek_t = jnp.swapaxes(ek, 0, 1)
            init = (jnp.zeros_like(decay), jnp.zeros_like(decay))
            _, (nf, df) = lax.scan(step, init, (ekv_t, ek_t))
            _, (nb, db) = lax.scan(step, init, (ekv_t, ek_t), reverse=True)
            nf = jnp.swapaxes(nf, 0, 1)
            df = jnp.swapaxes(df, 0, 1)
            nb = jnp.swapaxes(nb, 0, 1)
            db = jnp.swapaxes(db, 0, 1)
            euk = jnp.exp(jnp.minimum(u.astype(jnp.float32)[None, None, :] + kf, 30.0))
            num = nf + nb - ekv + euk * vf
            den = df + db - ek + euk
            base = jax.nn.sigmoid(r.astype(jnp.float32)) * (num / jnp.maximum(den, 1e-08))
            out = base * (0.8 + 0.2 * tf)
            return out.astype(r.dtype)
        key = jax.random.key(seed)
        ks = jax.random.split(key, 6)
        return {'r': jax.random.normal(ks[0], (B, T, C), dtype=jnp.float32), 'k': jax.random.normal(ks[1], (B, T, C), dtype=jnp.float32), 'v': jax.random.normal(ks[2], (B, T, C), dtype=jnp.float32), 'w': jax.random.normal(ks[3], (C,), dtype=jnp.float32), 'u': jax.random.normal(ks[4], (C,), dtype=jnp.float32), 'time_emb': jax.random.normal(ks[5], (B, TD), dtype=jnp.float32)}
    _L0_cond2_all = _L0_cond2_setup()
    _L0_cond2_in = {k: v for k, v in _L0_cond2_all.items() if k in ('w', 'u')}
    del _L0_cond2_all

    def _L0_ffn_setup():
        import jax, jax.numpy as jnp
        import numpy as np
        B, S, D, R, E = (4, 256, 256, 64, 8)
        SCALING = 64.0 / 16.0
        key = jax.random.key(seed)
        k1, k2, k3, k4 = jax.random.split(key, 4)
        x = jax.random.normal(k1, (B, S, D), dtype=jnp.float32)
        A = jax.random.normal(k2, (E, R, D), dtype=jnp.float32) * 0.02
        Bw = jax.random.normal(k3, (E, D, R), dtype=jnp.float32) * 0.02
        Wg = jax.random.normal(k4, (E, D), dtype=jnp.float32) * 0.02
        return {'x': x, 'A': A, 'Bw': Bw, 'Wg': Wg}
    _L0_ffn_all = _L0_ffn_setup()
    _L0_ffn_in = {k: v for k, v in _L0_ffn_all.items() if k in ('A', 'Bw', 'Wg')}
    del _L0_ffn_all

    def _L1_cond_setup():
        import jax, jax.numpy as jnp
        from jax import lax
        import numpy as np
        B, T, C, TD = (8, 256, 256, 64)

        def _bi_wkv(r, k, v, w, u, time_emb):
            tf = jax.nn.sigmoid(jnp.sum(time_emb, axis=-1))[:, None, None]
            decay = jnp.exp(-jnp.exp(w.astype(jnp.float32)))[None, :] * (0.5 + 0.5 * tf[:, :, 0])
            kf = k.astype(jnp.float32)
            vf = v.astype(jnp.float32)
            ek = jnp.exp(jnp.minimum(kf, 30.0))
            ekv = ek * vf

            def step(carry, x):
                a, b = carry
                ekv_t, ek_t = x
                a = a * decay + ekv_t
                b = b * decay + ek_t
                return ((a, b), (a, b))
            ekv_t = jnp.swapaxes(ekv, 0, 1)
            ek_t = jnp.swapaxes(ek, 0, 1)
            init = (jnp.zeros_like(decay), jnp.zeros_like(decay))
            _, (nf, df) = lax.scan(step, init, (ekv_t, ek_t))
            _, (nb, db) = lax.scan(step, init, (ekv_t, ek_t), reverse=True)
            nf = jnp.swapaxes(nf, 0, 1)
            df = jnp.swapaxes(df, 0, 1)
            nb = jnp.swapaxes(nb, 0, 1)
            db = jnp.swapaxes(db, 0, 1)
            euk = jnp.exp(jnp.minimum(u.astype(jnp.float32)[None, None, :] + kf, 30.0))
            num = nf + nb - ekv + euk * vf
            den = df + db - ek + euk
            base = jax.nn.sigmoid(r.astype(jnp.float32)) * (num / jnp.maximum(den, 1e-08))
            out = base * (0.8 + 0.2 * tf)
            return out.astype(r.dtype)
        key = jax.random.key(seed)
        ks = jax.random.split(key, 6)
        return {'r': jax.random.normal(ks[0], (B, T, C), dtype=jnp.float32), 'k': jax.random.normal(ks[1], (B, T, C), dtype=jnp.float32), 'v': jax.random.normal(ks[2], (B, T, C), dtype=jnp.float32), 'w': jax.random.normal(ks[3], (C,), dtype=jnp.float32), 'u': jax.random.normal(ks[4], (C,), dtype=jnp.float32), 'time_emb': jax.random.normal(ks[5], (B, TD), dtype=jnp.float32)}
    _L1_cond_all = _L1_cond_setup()
    _L1_cond_in = {k: v for k, v in _L1_cond_all.items() if k in ('w', 'u')}
    del _L1_cond_all

    def _L1_attn_setup():
        import jax, jax.numpy as jnp
        import numpy as np
        HIDDEN = 256
        NUM_HEADS = 16
        HEAD_DIM = 128
        WINDOW = 128
        ROPE_THETA = 10000.0
        B, L = (1, 512)

        def _apply_rotary(x, cos, sin):
            d2 = x.shape[-1] // 2
            x1, x2 = (x[..., :d2], x[..., d2:])
            return jnp.concatenate([x1 * cos - x2 * sin, x2 * cos + x1 * sin], axis=-1)
        key = jax.random.key(seed)
        k0, k1, k2, k3, k4 = jax.random.split(key, 5)
        s = 1.0 / np.sqrt(HIDDEN)
        return {'hidden_states': jax.random.normal(k0, (B, L, HIDDEN), dtype=jnp.float32), 'wq': jax.random.normal(k1, (HIDDEN, NUM_HEADS * HEAD_DIM), dtype=jnp.float32) * s, 'wk': jax.random.normal(k2, (HIDDEN, NUM_HEADS * HEAD_DIM), dtype=jnp.float32) * s, 'wv': jax.random.normal(k3, (HIDDEN, NUM_HEADS * HEAD_DIM), dtype=jnp.float32) * s, 'wo': jax.random.normal(k4, (NUM_HEADS * HEAD_DIM, HIDDEN), dtype=jnp.float32) * s}
    _L1_attn_all = _L1_attn_setup()
    _L1_attn_in = {k: v for k, v in _L1_attn_all.items() if k in ('wq', 'wk', 'wv', 'wo')}
    del _L1_attn_all

    def _L1_cond2_setup():
        import jax, jax.numpy as jnp
        from jax import lax
        import numpy as np
        B, T, C, TD = (8, 256, 256, 64)

        def _bi_wkv(r, k, v, w, u, time_emb):
            tf = jax.nn.sigmoid(jnp.sum(time_emb, axis=-1))[:, None, None]
            decay = jnp.exp(-jnp.exp(w.astype(jnp.float32)))[None, :] * (0.5 + 0.5 * tf[:, :, 0])
            kf = k.astype(jnp.float32)
            vf = v.astype(jnp.float32)
            ek = jnp.exp(jnp.minimum(kf, 30.0))
            ekv = ek * vf

            def step(carry, x):
                a, b = carry
                ekv_t, ek_t = x
                a = a * decay + ekv_t
                b = b * decay + ek_t
                return ((a, b), (a, b))
            ekv_t = jnp.swapaxes(ekv, 0, 1)
            ek_t = jnp.swapaxes(ek, 0, 1)
            init = (jnp.zeros_like(decay), jnp.zeros_like(decay))
            _, (nf, df) = lax.scan(step, init, (ekv_t, ek_t))
            _, (nb, db) = lax.scan(step, init, (ekv_t, ek_t), reverse=True)
            nf = jnp.swapaxes(nf, 0, 1)
            df = jnp.swapaxes(df, 0, 1)
            nb = jnp.swapaxes(nb, 0, 1)
            db = jnp.swapaxes(db, 0, 1)
            euk = jnp.exp(jnp.minimum(u.astype(jnp.float32)[None, None, :] + kf, 30.0))
            num = nf + nb - ekv + euk * vf
            den = df + db - ek + euk
            base = jax.nn.sigmoid(r.astype(jnp.float32)) * (num / jnp.maximum(den, 1e-08))
            out = base * (0.8 + 0.2 * tf)
            return out.astype(r.dtype)
        key = jax.random.key(seed)
        ks = jax.random.split(key, 6)
        return {'r': jax.random.normal(ks[0], (B, T, C), dtype=jnp.float32), 'k': jax.random.normal(ks[1], (B, T, C), dtype=jnp.float32), 'v': jax.random.normal(ks[2], (B, T, C), dtype=jnp.float32), 'w': jax.random.normal(ks[3], (C,), dtype=jnp.float32), 'u': jax.random.normal(ks[4], (C,), dtype=jnp.float32), 'time_emb': jax.random.normal(ks[5], (B, TD), dtype=jnp.float32)}
    _L1_cond2_all = _L1_cond2_setup()
    _L1_cond2_in = {k: v for k, v in _L1_cond2_all.items() if k in ('w', 'u')}
    del _L1_cond2_all

    def _L1_ffn_setup():
        import jax, jax.numpy as jnp
        import numpy as np
        E = 64
        K = 6
        NG = 8
        TKG = 4
        SCALE = 2.5
        CAP = 64

        def _router(x, gate_w, e_bias):
            logits = x.astype(jnp.float32) @ gate_w.T
            scores = jax.nn.sigmoid(logits)
            sc = scores + e_bias[None, :]
            T = x.shape[0]
            gs = sc.reshape(T, NG, E // NG)
            grp_score = jax.lax.top_k(gs, 2)[0].sum(-1)
            _, gidx = jax.lax.top_k(grp_score, TKG)
            gmask = jax.nn.one_hot(gidx, NG, dtype=sc.dtype).sum(1)
            emask = jnp.repeat(gmask, E // NG, axis=1)
            masked = jnp.where(emask > 0, sc, -jnp.inf)
            _, idx = jax.lax.top_k(masked, K)
            w = jnp.take_along_axis(scores, idx, axis=1)
            w = w / (w.sum(-1, keepdims=True) + 1e-20) * SCALE
            return (idx, w)

        def _relu2(h):
            return jnp.square(jax.nn.relu(h))

        def _moe(x, idx, w, w1, w2):
            T, D = x.shape
            e_flat = idx.reshape(-1)
            tok = jnp.repeat(jnp.arange(T), K)
            oh = jax.nn.one_hot(e_flat, E, dtype=jnp.float32)
            pos = jnp.cumsum(oh, axis=0) - oh
            pos = (pos * oh).sum(-1).astype(jnp.int32)
            keep = pos < CAP
            slot = jnp.where(keep, pos, CAP)
            xd = jnp.zeros((E, CAP + 1, D), x.dtype).at[e_flat, slot].set(x[tok])
            h = _relu2(jnp.einsum('ecd,eid->eci', xd, w1))
            yd = jnp.einsum('eci,edi->ecd', h, w2)
            gate = w.reshape(-1)[:, None] * keep[:, None].astype(x.dtype)
            y_assign = yd[e_flat, slot] * gate
            return jnp.zeros((T, D), x.dtype).at[tok].add(y_assign)
        key = jax.random.key(seed)
        ks = jax.random.split(key, 6)
        D, I, SH, T = (256, 128, 512, 256)
        x = jax.random.normal(ks[0], (1, T, D), jnp.float32)
        gate_w = jax.random.normal(ks[1], (E, D), jnp.float32) * D ** (-0.5)
        e_bias = jnp.zeros((E,), jnp.float32)
        w1 = jax.random.normal(ks[2], (E, I, D), jnp.float32) * D ** (-0.5)
        w2 = jax.random.normal(ks[3], (E, D, I), jnp.float32) * I ** (-0.5)
        su = jax.random.normal(ks[4], (SH, D), jnp.float32) * D ** (-0.5)
        sd = jax.random.normal(ks[5], (D, SH), jnp.float32) * SH ** (-0.5)
        return {'hidden_states': x, 'gate_w': gate_w, 'e_bias': e_bias, 'w1': w1, 'w2': w2, 'shared_up_w': su, 'shared_down_w': sd}
    _L1_ffn_all = _L1_ffn_setup()
    _L1_ffn_in = {k: v for k, v in _L1_ffn_all.items() if k in ('gate_w', 'e_bias', 'w1', 'w2', 'shared_up_w', 'shared_down_w')}
    del _L1_ffn_all

    def _L2_cond_setup():
        import jax, jax.numpy as jnp
        from jax import lax
        import numpy as np
        B, T, C, TD = (8, 256, 256, 64)

        def _bi_wkv(r, k, v, w, u, time_emb):
            tf = jax.nn.sigmoid(jnp.sum(time_emb, axis=-1))[:, None, None]
            decay = jnp.exp(-jnp.exp(w.astype(jnp.float32)))[None, :] * (0.5 + 0.5 * tf[:, :, 0])
            kf = k.astype(jnp.float32)
            vf = v.astype(jnp.float32)
            ek = jnp.exp(jnp.minimum(kf, 30.0))
            ekv = ek * vf

            def step(carry, x):
                a, b = carry
                ekv_t, ek_t = x
                a = a * decay + ekv_t
                b = b * decay + ek_t
                return ((a, b), (a, b))
            ekv_t = jnp.swapaxes(ekv, 0, 1)
            ek_t = jnp.swapaxes(ek, 0, 1)
            init = (jnp.zeros_like(decay), jnp.zeros_like(decay))
            _, (nf, df) = lax.scan(step, init, (ekv_t, ek_t))
            _, (nb, db) = lax.scan(step, init, (ekv_t, ek_t), reverse=True)
            nf = jnp.swapaxes(nf, 0, 1)
            df = jnp.swapaxes(df, 0, 1)
            nb = jnp.swapaxes(nb, 0, 1)
            db = jnp.swapaxes(db, 0, 1)
            euk = jnp.exp(jnp.minimum(u.astype(jnp.float32)[None, None, :] + kf, 30.0))
            num = nf + nb - ekv + euk * vf
            den = df + db - ek + euk
            base = jax.nn.sigmoid(r.astype(jnp.float32)) * (num / jnp.maximum(den, 1e-08))
            out = base * (0.8 + 0.2 * tf)
            return out.astype(r.dtype)
        key = jax.random.key(seed)
        ks = jax.random.split(key, 6)
        return {'r': jax.random.normal(ks[0], (B, T, C), dtype=jnp.float32), 'k': jax.random.normal(ks[1], (B, T, C), dtype=jnp.float32), 'v': jax.random.normal(ks[2], (B, T, C), dtype=jnp.float32), 'w': jax.random.normal(ks[3], (C,), dtype=jnp.float32), 'u': jax.random.normal(ks[4], (C,), dtype=jnp.float32), 'time_emb': jax.random.normal(ks[5], (B, TD), dtype=jnp.float32)}
    _L2_cond_all = _L2_cond_setup()
    _L2_cond_in = {k: v for k, v in _L2_cond_all.items() if k in ('w', 'u')}
    del _L2_cond_all

    def _L2_attn_setup():
        import jax, jax.numpy as jnp
        import numpy as np
        NUM_HEADS = 32
        ROPE_BASE = 10000.0
        MASK_NEG = -66504.0

        def _rotate_half(x):
            d = x.shape[-1] // 2
            return jnp.concatenate([-x[..., d:], x[..., :d]], axis=-1)
        key = jax.random.key(seed)
        k1, k2, k3, k4 = jax.random.split(key, 4)
        S, B, E = (256, 2, 256)
        return {'hidden_states': jax.random.normal(k1, (S, B, E), dtype=jnp.float32) * 0.02, 'qkv_w': jax.random.normal(k2, (E, 3 * E), dtype=jnp.float32) * 0.02, 'qkv_b': jax.random.normal(k3, (3 * E,), dtype=jnp.float32) * 0.02, 'out_w': jax.random.normal(k4, (E, E), dtype=jnp.float32) * 0.02, 'out_b': jnp.zeros((E,), dtype=jnp.float32)}
    _L2_attn_all = _L2_attn_setup()
    _L2_attn_in = {k: v for k, v in _L2_attn_all.items() if k in ('qkv_w', 'qkv_b', 'out_w', 'out_b')}
    del _L2_attn_all

    def _L2_cond2_setup():
        import jax, jax.numpy as jnp
        from jax import lax
        import numpy as np
        B, T, C, TD = (8, 256, 256, 64)

        def _bi_wkv(r, k, v, w, u, time_emb):
            tf = jax.nn.sigmoid(jnp.sum(time_emb, axis=-1))[:, None, None]
            decay = jnp.exp(-jnp.exp(w.astype(jnp.float32)))[None, :] * (0.5 + 0.5 * tf[:, :, 0])
            kf = k.astype(jnp.float32)
            vf = v.astype(jnp.float32)
            ek = jnp.exp(jnp.minimum(kf, 30.0))
            ekv = ek * vf

            def step(carry, x):
                a, b = carry
                ekv_t, ek_t = x
                a = a * decay + ekv_t
                b = b * decay + ek_t
                return ((a, b), (a, b))
            ekv_t = jnp.swapaxes(ekv, 0, 1)
            ek_t = jnp.swapaxes(ek, 0, 1)
            init = (jnp.zeros_like(decay), jnp.zeros_like(decay))
            _, (nf, df) = lax.scan(step, init, (ekv_t, ek_t))
            _, (nb, db) = lax.scan(step, init, (ekv_t, ek_t), reverse=True)
            nf = jnp.swapaxes(nf, 0, 1)
            df = jnp.swapaxes(df, 0, 1)
            nb = jnp.swapaxes(nb, 0, 1)
            db = jnp.swapaxes(db, 0, 1)
            euk = jnp.exp(jnp.minimum(u.astype(jnp.float32)[None, None, :] + kf, 30.0))
            num = nf + nb - ekv + euk * vf
            den = df + db - ek + euk
            base = jax.nn.sigmoid(r.astype(jnp.float32)) * (num / jnp.maximum(den, 1e-08))
            out = base * (0.8 + 0.2 * tf)
            return out.astype(r.dtype)
        key = jax.random.key(seed)
        ks = jax.random.split(key, 6)
        return {'r': jax.random.normal(ks[0], (B, T, C), dtype=jnp.float32), 'k': jax.random.normal(ks[1], (B, T, C), dtype=jnp.float32), 'v': jax.random.normal(ks[2], (B, T, C), dtype=jnp.float32), 'w': jax.random.normal(ks[3], (C,), dtype=jnp.float32), 'u': jax.random.normal(ks[4], (C,), dtype=jnp.float32), 'time_emb': jax.random.normal(ks[5], (B, TD), dtype=jnp.float32)}
    _L2_cond2_all = _L2_cond2_setup()
    _L2_cond2_in = {k: v for k, v in _L2_cond2_all.items() if k in ('w', 'u')}
    del _L2_cond2_all

    def _L2_ffn_setup():
        import jax, jax.numpy as jnp
        import numpy as np
        from jax import lax
        E = 64
        H = 256
        I = 88
        G = 8
        TOPK_GROUP = 4
        K = 8
        B, S = (2, 256)
        N = B * S
        CAP = 2 * N * K // E
        SCALE = 2.5

        def _route(x, router_weight, e_bias):
            logits = x.astype(jnp.float32) @ router_weight.astype(jnp.float32).T
            scores = jax.nn.sigmoid(logits)
            sc = scores + e_bias
            n = x.shape[0]
            group_scores = lax.top_k(sc.reshape(n, G, E // G), 2)[0].sum(-1)
            grp_idx = lax.top_k(group_scores, TOPK_GROUP)[1]
            group_mask = jnp.zeros((n, G), jnp.float32).at[jnp.arange(n)[:, None], grp_idx].set(1.0)
            score_mask = jnp.repeat(group_mask, E // G, axis=1)
            masked = jnp.where(score_mask > 0, sc, 0.0)
            topk_idx = lax.top_k(masked, K)[1]
            topk_w = jnp.take_along_axis(scores, topk_idx, axis=1)
            topk_w = topk_w / (topk_w.sum(-1, keepdims=True) + 1e-20)
            return (topk_idx, topk_w * SCALE)

        def _moe_experts(x, topk_idx, topk_w, w_gate, w_up, w_down):
            n = x.shape[0]
            flat_e = topk_idx.reshape(-1)
            rows = jnp.repeat(jnp.arange(n), K)
            oh = jax.nn.one_hot(flat_e, E, dtype=jnp.int32)
            pos = jnp.cumsum(oh, axis=0) - oh
            pos = jnp.take_along_axis(pos, flat_e[:, None], axis=1)[:, 0]
            valid = (pos < CAP).astype(x.dtype)
            p = jnp.minimum(pos, CAP - 1)
            buf = jnp.zeros((E, CAP, H), x.dtype).at[flat_e, p].add(x[rows] * valid[:, None])
            g = jnp.einsum('ech,ehi->eci', buf, w_gate)
            u = jnp.einsum('ech,ehi->eci', buf, w_up)
            y = jnp.einsum('eci,eih->ech', jax.nn.silu(g) * u, w_down)
            y_tok = y[flat_e, p] * (topk_w.reshape(-1) * valid)[:, None]
            return jnp.zeros((n, H), x.dtype).at[rows].add(y_tok)

        def _shared_mlp(x, sh_gate, sh_up, sh_down):
            return jax.nn.silu(x @ sh_gate) * (x @ sh_up) @ sh_down
        key = jax.random.key(seed)
        ks = jax.random.split(key, 9)
        f32 = jnp.float32
        return {'hidden_states': jax.random.normal(ks[0], (B, S, H), f32), 'router_weight': jax.random.normal(ks[1], (E, H), f32) * (2.0 / H) ** 0.5, 'e_bias': jnp.zeros((E,), f32), 'w_gate': jax.random.normal(ks[2], (E, H, I), f32) * (1.0 / H) ** 0.5, 'w_up': jax.random.normal(ks[3], (E, H, I), f32) * (1.0 / H) ** 0.5, 'w_down': jax.random.normal(ks[4], (E, I, H), f32) * (1.0 / I) ** 0.5, 'sh_gate': jax.random.normal(ks[5], (H, I), f32) * (1.0 / H) ** 0.5, 'sh_up': jax.random.normal(ks[6], (H, I), f32) * (1.0 / H) ** 0.5, 'sh_down': jax.random.normal(ks[7], (I, H), f32) * (1.0 / I) ** 0.5}
    _L2_ffn_all = _L2_ffn_setup()
    _L2_ffn_in = {k: v for k, v in _L2_ffn_all.items() if k in ('router_weight', 'e_bias', 'w_gate', 'w_up', 'w_down', 'sh_gate', 'sh_up', 'sh_down')}
    del _L2_ffn_all

    def _L3_cond_setup():
        import jax, jax.numpy as jnp
        from jax import lax
        import numpy as np
        B, T, C, TD = (8, 256, 256, 64)

        def _bi_wkv(r, k, v, w, u, time_emb):
            tf = jax.nn.sigmoid(jnp.sum(time_emb, axis=-1))[:, None, None]
            decay = jnp.exp(-jnp.exp(w.astype(jnp.float32)))[None, :] * (0.5 + 0.5 * tf[:, :, 0])
            kf = k.astype(jnp.float32)
            vf = v.astype(jnp.float32)
            ek = jnp.exp(jnp.minimum(kf, 30.0))
            ekv = ek * vf

            def step(carry, x):
                a, b = carry
                ekv_t, ek_t = x
                a = a * decay + ekv_t
                b = b * decay + ek_t
                return ((a, b), (a, b))
            ekv_t = jnp.swapaxes(ekv, 0, 1)
            ek_t = jnp.swapaxes(ek, 0, 1)
            init = (jnp.zeros_like(decay), jnp.zeros_like(decay))
            _, (nf, df) = lax.scan(step, init, (ekv_t, ek_t))
            _, (nb, db) = lax.scan(step, init, (ekv_t, ek_t), reverse=True)
            nf = jnp.swapaxes(nf, 0, 1)
            df = jnp.swapaxes(df, 0, 1)
            nb = jnp.swapaxes(nb, 0, 1)
            db = jnp.swapaxes(db, 0, 1)
            euk = jnp.exp(jnp.minimum(u.astype(jnp.float32)[None, None, :] + kf, 30.0))
            num = nf + nb - ekv + euk * vf
            den = df + db - ek + euk
            base = jax.nn.sigmoid(r.astype(jnp.float32)) * (num / jnp.maximum(den, 1e-08))
            out = base * (0.8 + 0.2 * tf)
            return out.astype(r.dtype)
        key = jax.random.key(seed)
        ks = jax.random.split(key, 6)
        return {'r': jax.random.normal(ks[0], (B, T, C), dtype=jnp.float32), 'k': jax.random.normal(ks[1], (B, T, C), dtype=jnp.float32), 'v': jax.random.normal(ks[2], (B, T, C), dtype=jnp.float32), 'w': jax.random.normal(ks[3], (C,), dtype=jnp.float32), 'u': jax.random.normal(ks[4], (C,), dtype=jnp.float32), 'time_emb': jax.random.normal(ks[5], (B, TD), dtype=jnp.float32)}
    _L3_cond_all = _L3_cond_setup()
    _L3_cond_in = {k: v for k, v in _L3_cond_all.items() if k in ('w', 'u')}
    del _L3_cond_all

    def _L3_attn_setup():
        import jax, jax.numpy as jnp
        import numpy as np
        DIM = 256
        HEADS = 16
        HEAD_DIM = DIM // HEADS
        RANK = 16
        ALPHA = 8.0
        SCALING = ALPHA / RANK
        SCALE = HEAD_DIM ** (-0.5)

        def lora_linear(x, W, b, Bm, Am):
            out = jnp.einsum('bld,od->blo', x, W) + b
            upd = jnp.einsum('blr,or->blo', jnp.einsum('bld,rd->blr', x, Bm), Am)
            return out + SCALING * upd

        def _split(t):
            B, L, D = t.shape
            return t.reshape(B, L, HEADS, HEAD_DIM).transpose(0, 2, 1, 3)
        key = jax.random.key(seed)
        ks = jax.random.split(key, 20)
        B, L = (4, 256)
        x = jax.random.normal(ks[0], (B, L, DIM), dtype=jnp.float32)
        s = 0.02
        inp = {'x': x}
        for i, name in enumerate(['q', 'k', 'v', 'o']):
            inp[f'W{name}'] = jax.random.normal(ks[1 + 4 * i], (DIM, DIM), jnp.float32) * s
            inp[f'b{name}'] = jax.random.normal(ks[2 + 4 * i], (DIM,), jnp.float32) * s
            inp[f'B{name}'] = jax.random.normal(ks[3 + 4 * i], (RANK, DIM), jnp.float32) * s
            inp[f'A{name}'] = jax.random.uniform(ks[4 + 4 * i], (DIM, RANK), jnp.float32, -0.1, 0.1)
        return inp
    _L3_attn_all = _L3_attn_setup()
    _L3_attn_in = {k: v for k, v in _L3_attn_all.items() if k in ('Wq', 'bq', 'Bq', 'Aq', 'Wk', 'bk', 'Bk', 'Ak', 'Wv', 'bv', 'Bv', 'Av', 'Wo', 'bo', 'Bo', 'Ao')}
    del _L3_attn_all

    def _L3_cond2_setup():
        import jax, jax.numpy as jnp
        from jax import lax
        import numpy as np
        B, T, C, TD = (8, 256, 256, 64)

        def _bi_wkv(r, k, v, w, u, time_emb):
            tf = jax.nn.sigmoid(jnp.sum(time_emb, axis=-1))[:, None, None]
            decay = jnp.exp(-jnp.exp(w.astype(jnp.float32)))[None, :] * (0.5 + 0.5 * tf[:, :, 0])
            kf = k.astype(jnp.float32)
            vf = v.astype(jnp.float32)
            ek = jnp.exp(jnp.minimum(kf, 30.0))
            ekv = ek * vf

            def step(carry, x):
                a, b = carry
                ekv_t, ek_t = x
                a = a * decay + ekv_t
                b = b * decay + ek_t
                return ((a, b), (a, b))
            ekv_t = jnp.swapaxes(ekv, 0, 1)
            ek_t = jnp.swapaxes(ek, 0, 1)
            init = (jnp.zeros_like(decay), jnp.zeros_like(decay))
            _, (nf, df) = lax.scan(step, init, (ekv_t, ek_t))
            _, (nb, db) = lax.scan(step, init, (ekv_t, ek_t), reverse=True)
            nf = jnp.swapaxes(nf, 0, 1)
            df = jnp.swapaxes(df, 0, 1)
            nb = jnp.swapaxes(nb, 0, 1)
            db = jnp.swapaxes(db, 0, 1)
            euk = jnp.exp(jnp.minimum(u.astype(jnp.float32)[None, None, :] + kf, 30.0))
            num = nf + nb - ekv + euk * vf
            den = df + db - ek + euk
            base = jax.nn.sigmoid(r.astype(jnp.float32)) * (num / jnp.maximum(den, 1e-08))
            out = base * (0.8 + 0.2 * tf)
            return out.astype(r.dtype)
        key = jax.random.key(seed)
        ks = jax.random.split(key, 6)
        return {'r': jax.random.normal(ks[0], (B, T, C), dtype=jnp.float32), 'k': jax.random.normal(ks[1], (B, T, C), dtype=jnp.float32), 'v': jax.random.normal(ks[2], (B, T, C), dtype=jnp.float32), 'w': jax.random.normal(ks[3], (C,), dtype=jnp.float32), 'u': jax.random.normal(ks[4], (C,), dtype=jnp.float32), 'time_emb': jax.random.normal(ks[5], (B, TD), dtype=jnp.float32)}
    _L3_cond2_all = _L3_cond2_setup()
    _L3_cond2_in = {k: v for k, v in _L3_cond2_all.items() if k in ('w', 'u')}
    del _L3_cond2_all

    def _L3_ffn_setup():
        import jax, jax.numpy as jnp
        import numpy as np
        EPS = 1e-05
        RMS_EPS = 1e-06

        def activation_quant(x, num_bits=8):
            qn = -2 ** (num_bits - 1)
            qp = 2 ** (num_bits - 1) - 1
            xf = x.astype(jnp.float32)
            s = qp / jnp.clip(jnp.max(jnp.abs(xf), axis=-1, keepdims=True), EPS, None)
            return (jnp.clip(jnp.round(xf * s), qn, qp) / s).astype(x.dtype)

        def weight_quant(w):
            wf = w.astype(jnp.float32)
            s = 1.0 / jnp.clip(jnp.mean(jnp.abs(wf)), EPS, None)
            return (jnp.clip(jnp.round(wf * s), -1.0, 1.0) / s).astype(w.dtype)

        def bit_linear(x, w):
            qx = x + jax.lax.stop_gradient(activation_quant(x) - x)
            qw = w + jax.lax.stop_gradient(weight_quant(w) - w)
            return jnp.einsum('bsh,oh->bso', qx, qw)

        def rms_norm(x, weight, eps=RMS_EPS):
            xf = x.astype(jnp.float32)
            var = jnp.mean(xf * xf, axis=-1, keepdims=True)
            return weight * (xf * jax.lax.rsqrt(var + eps)).astype(x.dtype)
        key = jax.random.key(seed)
        k1, k2, k3, k4 = jax.random.split(key, 4)
        B, S, H, I = (2, 256, 256, 1024)
        scale = 1.0 / np.sqrt(H)
        return {'x': jax.random.normal(k1, (B, S, H), dtype=jnp.float32), 'w_gate': jax.random.normal(k2, (I, H), dtype=jnp.float32) * scale, 'w_up': jax.random.normal(k3, (I, H), dtype=jnp.float32) * scale, 'w_down': jax.random.normal(k4, (H, I), dtype=jnp.float32) * (1.0 / np.sqrt(I)), 'ln_weight': jnp.ones((I,), dtype=jnp.float32)}
    _L3_ffn_all = _L3_ffn_setup()
    _L3_ffn_in = {k: v for k, v in _L3_ffn_all.items() if k in ('w_gate', 'w_up', 'w_down', 'ln_weight')}
    del _L3_ffn_all
    return {'x': x, 'fside_BxSxS_0': fside_BxSxS_0, 'cond_512': cond_512, 'L0_cond_w': _L0_cond_in['w'], 'L0_cond_u': _L0_cond_in['u'], 'L0_attn_w_qkv': _L0_attn_in['w_qkv'], 'L0_attn_w_proj': _L0_attn_in['w_proj'], 'L0_cond2_w': _L0_cond2_in['w'], 'L0_cond2_u': _L0_cond2_in['u'], 'L0_ffn_A': _L0_ffn_in['A'], 'L0_ffn_Bw': _L0_ffn_in['Bw'], 'L0_ffn_Wg': _L0_ffn_in['Wg'], 'L1_cond_w': _L1_cond_in['w'], 'L1_cond_u': _L1_cond_in['u'], 'L1_attn_wq': _L1_attn_in['wq'], 'L1_attn_wk': _L1_attn_in['wk'], 'L1_attn_wv': _L1_attn_in['wv'], 'L1_attn_wo': _L1_attn_in['wo'], 'L1_cond2_w': _L1_cond2_in['w'], 'L1_cond2_u': _L1_cond2_in['u'], 'L1_ffn_gate_w': _L1_ffn_in['gate_w'], 'L1_ffn_e_bias': _L1_ffn_in['e_bias'], 'L1_ffn_w1': _L1_ffn_in['w1'], 'L1_ffn_w2': _L1_ffn_in['w2'], 'L1_ffn_shared_up_w': _L1_ffn_in['shared_up_w'], 'L1_ffn_shared_down_w': _L1_ffn_in['shared_down_w'], 'L2_cond_w': _L2_cond_in['w'], 'L2_cond_u': _L2_cond_in['u'], 'L2_attn_qkv_w': _L2_attn_in['qkv_w'], 'L2_attn_qkv_b': _L2_attn_in['qkv_b'], 'L2_attn_out_w': _L2_attn_in['out_w'], 'L2_attn_out_b': _L2_attn_in['out_b'], 'L2_cond2_w': _L2_cond2_in['w'], 'L2_cond2_u': _L2_cond2_in['u'], 'L2_ffn_router_weight': _L2_ffn_in['router_weight'], 'L2_ffn_e_bias': _L2_ffn_in['e_bias'], 'L2_ffn_w_gate': _L2_ffn_in['w_gate'], 'L2_ffn_w_up': _L2_ffn_in['w_up'], 'L2_ffn_w_down': _L2_ffn_in['w_down'], 'L2_ffn_sh_gate': _L2_ffn_in['sh_gate'], 'L2_ffn_sh_up': _L2_ffn_in['sh_up'], 'L2_ffn_sh_down': _L2_ffn_in['sh_down'], 'L3_cond_w': _L3_cond_in['w'], 'L3_cond_u': _L3_cond_in['u'], 'L3_attn_Wq': _L3_attn_in['Wq'], 'L3_attn_bq': _L3_attn_in['bq'], 'L3_attn_Bq': _L3_attn_in['Bq'], 'L3_attn_Aq': _L3_attn_in['Aq'], 'L3_attn_Wk': _L3_attn_in['Wk'], 'L3_attn_bk': _L3_attn_in['bk'], 'L3_attn_Bk': _L3_attn_in['Bk'], 'L3_attn_Ak': _L3_attn_in['Ak'], 'L3_attn_Wv': _L3_attn_in['Wv'], 'L3_attn_bv': _L3_attn_in['bv'], 'L3_attn_Bv': _L3_attn_in['Bv'], 'L3_attn_Av': _L3_attn_in['Av'], 'L3_attn_Wo': _L3_attn_in['Wo'], 'L3_attn_bo': _L3_attn_in['bo'], 'L3_attn_Bo': _L3_attn_in['Bo'], 'L3_attn_Ao': _L3_attn_in['Ao'], 'L3_cond2_w': _L3_cond2_in['w'], 'L3_cond2_u': _L3_cond2_in['u'], 'L3_ffn_w_gate': _L3_ffn_in['w_gate'], 'L3_ffn_w_up': _L3_ffn_in['w_up'], 'L3_ffn_w_down': _L3_ffn_in['w_down'], 'L3_ffn_ln_weight': _L3_ffn_in['ln_weight']}

def reference(x, fside_BxSxS_0, cond_512, L0_cond_w, L0_cond_u, L0_attn_w_qkv, L0_attn_w_proj, L0_cond2_w, L0_cond2_u, L0_ffn_A, L0_ffn_Bw, L0_ffn_Wg, L1_cond_w, L1_cond_u, L1_attn_wq, L1_attn_wk, L1_attn_wv, L1_attn_wo, L1_cond2_w, L1_cond2_u, L1_ffn_gate_w, L1_ffn_e_bias, L1_ffn_w1, L1_ffn_w2, L1_ffn_shared_up_w, L1_ffn_shared_down_w, L2_cond_w, L2_cond_u, L2_attn_qkv_w, L2_attn_qkv_b, L2_attn_out_w, L2_attn_out_b, L2_cond2_w, L2_cond2_u, L2_ffn_router_weight, L2_ffn_e_bias, L2_ffn_w_gate, L2_ffn_w_up, L2_ffn_w_down, L2_ffn_sh_gate, L2_ffn_sh_up, L2_ffn_sh_down, L3_cond_w, L3_cond_u, L3_attn_Wq, L3_attn_bq, L3_attn_Bq, L3_attn_Aq, L3_attn_Wk, L3_attn_bk, L3_attn_Bk, L3_attn_Ak, L3_attn_Wv, L3_attn_bv, L3_attn_Bv, L3_attn_Av, L3_attn_Wo, L3_attn_bo, L3_attn_Bo, L3_attn_Ao, L3_cond2_w, L3_cond2_u, L3_ffn_w_gate, L3_ffn_w_up, L3_ffn_w_down, L3_ffn_ln_weight):
    import jax
    import jax.numpy as jnp

    def _L0_cond_ref(r, k, v, w, u, time_emb):
        import jax, jax.numpy as jnp
        from jax import lax
        import numpy as np
        B, T, C, TD = (8, 256, 256, 64)

        def _bi_wkv(r, k, v, w, u, time_emb):
            tf = jax.nn.sigmoid(jnp.sum(time_emb, axis=-1))[:, None, None]
            decay = jnp.exp(-jnp.exp(w.astype(jnp.float32)))[None, :] * (0.5 + 0.5 * tf[:, :, 0])
            kf = k.astype(jnp.float32)
            vf = v.astype(jnp.float32)
            ek = jnp.exp(jnp.minimum(kf, 30.0))
            ekv = ek * vf

            def step(carry, x):
                a, b = carry
                ekv_t, ek_t = x
                a = a * decay + ekv_t
                b = b * decay + ek_t
                return ((a, b), (a, b))
            ekv_t = jnp.swapaxes(ekv, 0, 1)
            ek_t = jnp.swapaxes(ek, 0, 1)
            init = (jnp.zeros_like(decay), jnp.zeros_like(decay))
            _, (nf, df) = lax.scan(step, init, (ekv_t, ek_t))
            _, (nb, db) = lax.scan(step, init, (ekv_t, ek_t), reverse=True)
            nf = jnp.swapaxes(nf, 0, 1)
            df = jnp.swapaxes(df, 0, 1)
            nb = jnp.swapaxes(nb, 0, 1)
            db = jnp.swapaxes(db, 0, 1)
            euk = jnp.exp(jnp.minimum(u.astype(jnp.float32)[None, None, :] + kf, 30.0))
            num = nf + nb - ekv + euk * vf
            den = df + db - ek + euk
            base = jax.nn.sigmoid(r.astype(jnp.float32)) * (num / jnp.maximum(den, 1e-08))
            out = base * (0.8 + 0.2 * tf)
            return out.astype(r.dtype)
        return _bi_wkv(r, k, v, w, u, time_emb)

    def _L0_attn_ref(x, w_qkv, w_proj):
        import jax, jax.numpy as jnp
        import numpy as np
        EMBED_DIM = 256
        NUM_HEADS = 16
        HEAD_DIM = EMBED_DIM // NUM_HEADS
        SCALE = HEAD_DIM ** (-0.5)
        NEG = -9000000000000000.0

        def _act_quant(x):
            s = 127.0 / jnp.clip(jnp.max(jnp.abs(x), axis=-1, keepdims=True), 1e-05)
            return jnp.clip(jnp.round(x * s), -128.0, 127.0) / s

        def _weight_quant(w):
            s = 1.0 / jnp.clip(jnp.mean(jnp.abs(w)), 1e-05)
            return jnp.clip(jnp.round(w * s), -1.0, 1.0) / s

        def _bitlinear(x, w):
            xq = x + jax.lax.stop_gradient(_act_quant(x) - x)
            wq = w + jax.lax.stop_gradient(_weight_quant(w) - w)
            return jnp.einsum('bnc,oc->bno', xq, wq)
        B, N, C = x.shape
        H, D = (NUM_HEADS, HEAD_DIM)
        qkv = _bitlinear(x, w_qkv).reshape(B, N, 3, H, D)
        q, k, v = (qkv[:, :, 0], qkv[:, :, 1], qkv[:, :, 2])
        attn = jnp.einsum('bnhd,bmhd->bhnm', q, k) * SCALE
        causal = jnp.tril(jnp.ones((N, N), dtype=bool))
        attn = jnp.where(causal, attn, NEG)
        attn = jax.nn.softmax(attn, axis=-1)
        out = jnp.einsum('bhnm,bmhd->bnhd', attn, v).reshape(B, N, C)
        return _bitlinear(out, w_proj)

    def _L0_cond2_ref(r, k, v, w, u, time_emb):
        import jax, jax.numpy as jnp
        from jax import lax
        import numpy as np
        B, T, C, TD = (8, 256, 256, 64)

        def _bi_wkv(r, k, v, w, u, time_emb):
            tf = jax.nn.sigmoid(jnp.sum(time_emb, axis=-1))[:, None, None]
            decay = jnp.exp(-jnp.exp(w.astype(jnp.float32)))[None, :] * (0.5 + 0.5 * tf[:, :, 0])
            kf = k.astype(jnp.float32)
            vf = v.astype(jnp.float32)
            ek = jnp.exp(jnp.minimum(kf, 30.0))
            ekv = ek * vf

            def step(carry, x):
                a, b = carry
                ekv_t, ek_t = x
                a = a * decay + ekv_t
                b = b * decay + ek_t
                return ((a, b), (a, b))
            ekv_t = jnp.swapaxes(ekv, 0, 1)
            ek_t = jnp.swapaxes(ek, 0, 1)
            init = (jnp.zeros_like(decay), jnp.zeros_like(decay))
            _, (nf, df) = lax.scan(step, init, (ekv_t, ek_t))
            _, (nb, db) = lax.scan(step, init, (ekv_t, ek_t), reverse=True)
            nf = jnp.swapaxes(nf, 0, 1)
            df = jnp.swapaxes(df, 0, 1)
            nb = jnp.swapaxes(nb, 0, 1)
            db = jnp.swapaxes(db, 0, 1)
            euk = jnp.exp(jnp.minimum(u.astype(jnp.float32)[None, None, :] + kf, 30.0))
            num = nf + nb - ekv + euk * vf
            den = df + db - ek + euk
            base = jax.nn.sigmoid(r.astype(jnp.float32)) * (num / jnp.maximum(den, 1e-08))
            out = base * (0.8 + 0.2 * tf)
            return out.astype(r.dtype)
        return _bi_wkv(r, k, v, w, u, time_emb)

    def _L0_ffn_ref(x, A, Bw, Wg):
        import jax, jax.numpy as jnp
        import numpy as np
        B, S, D, R, E = (4, 256, 256, 64, 8)
        SCALING = 64.0 / 16.0
        bsz, seq_len, dim = x.shape
        xf = x.reshape(-1, dim)
        logits = jnp.einsum('nd,ed->ne', xf, Wg)
        prob = jax.nn.softmax(logits, axis=-1)
        gate = jnp.argmax(prob, axis=-1)
        prob_sel = jnp.take_along_axis(prob, gate[:, None], axis=1)
        mask = jax.nn.one_hot(gate, E, dtype=xf.dtype)
        h = jnp.einsum('nd,erd->ner', xf, A)
        h = h * mask[:, :, None]
        y = jnp.einsum('ner,eor->no', h, Bw)
        y = y * SCALING * prob_sel
        return y.reshape(bsz, seq_len, -1)

    def _L1_cond_ref(r, k, v, w, u, time_emb):
        import jax, jax.numpy as jnp
        from jax import lax
        import numpy as np
        B, T, C, TD = (8, 256, 256, 64)

        def _bi_wkv(r, k, v, w, u, time_emb):
            tf = jax.nn.sigmoid(jnp.sum(time_emb, axis=-1))[:, None, None]
            decay = jnp.exp(-jnp.exp(w.astype(jnp.float32)))[None, :] * (0.5 + 0.5 * tf[:, :, 0])
            kf = k.astype(jnp.float32)
            vf = v.astype(jnp.float32)
            ek = jnp.exp(jnp.minimum(kf, 30.0))
            ekv = ek * vf

            def step(carry, x):
                a, b = carry
                ekv_t, ek_t = x
                a = a * decay + ekv_t
                b = b * decay + ek_t
                return ((a, b), (a, b))
            ekv_t = jnp.swapaxes(ekv, 0, 1)
            ek_t = jnp.swapaxes(ek, 0, 1)
            init = (jnp.zeros_like(decay), jnp.zeros_like(decay))
            _, (nf, df) = lax.scan(step, init, (ekv_t, ek_t))
            _, (nb, db) = lax.scan(step, init, (ekv_t, ek_t), reverse=True)
            nf = jnp.swapaxes(nf, 0, 1)
            df = jnp.swapaxes(df, 0, 1)
            nb = jnp.swapaxes(nb, 0, 1)
            db = jnp.swapaxes(db, 0, 1)
            euk = jnp.exp(jnp.minimum(u.astype(jnp.float32)[None, None, :] + kf, 30.0))
            num = nf + nb - ekv + euk * vf
            den = df + db - ek + euk
            base = jax.nn.sigmoid(r.astype(jnp.float32)) * (num / jnp.maximum(den, 1e-08))
            out = base * (0.8 + 0.2 * tf)
            return out.astype(r.dtype)
        return _bi_wkv(r, k, v, w, u, time_emb)

    def _L1_attn_ref(hidden_states, wq, wk, wv, wo):
        import jax, jax.numpy as jnp
        import numpy as np
        HIDDEN = 256
        NUM_HEADS = 16
        HEAD_DIM = 128
        WINDOW = 128
        ROPE_THETA = 10000.0
        B, L = (1, 512)

        def _apply_rotary(x, cos, sin):
            d2 = x.shape[-1] // 2
            x1, x2 = (x[..., :d2], x[..., d2:])
            return jnp.concatenate([x1 * cos - x2 * sin, x2 * cos + x1 * sin], axis=-1)
        Bsz, Ln, _ = hidden_states.shape
        dtype = hidden_states.dtype
        scale = HEAD_DIM ** (-0.5)

        def split_heads(x):
            return x.reshape(Bsz, Ln, NUM_HEADS, HEAD_DIM).transpose(0, 2, 1, 3)
        q = split_heads(hidden_states @ wq)
        k = split_heads(hidden_states @ wk)
        v = split_heads(hidden_states @ wv)
        inv_freq = 1.0 / ROPE_THETA ** (jnp.arange(0, HEAD_DIM, 2, dtype=jnp.float32) / HEAD_DIM)
        pos = jnp.arange(Ln, dtype=jnp.float32)
        freqs = pos[:, None] * inv_freq[None, :]
        cos = jnp.cos(freqs).astype(dtype)
        sin = jnp.sin(freqs).astype(dtype)
        q = _apply_rotary(q, cos, sin)
        k = _apply_rotary(k, cos, sin)
        q_pos = jnp.arange(Ln)[:, None]
        k_pos = jnp.arange(Ln)[None, :]
        valid = (k_pos > q_pos - WINDOW) & (k_pos <= q_pos)
        neg = jnp.finfo(dtype).min
        attn = jnp.einsum('bhqd,bhkd->bhqk', q, k) * scale
        attn = jnp.where(valid, attn, neg)
        attn = jax.nn.softmax(attn, axis=-1)
        out = jnp.einsum('bhqk,bhkd->bhqd', attn, v)
        out = out.transpose(0, 2, 1, 3).reshape(Bsz, Ln, NUM_HEADS * HEAD_DIM)
        return out @ wo

    def _L1_cond2_ref(r, k, v, w, u, time_emb):
        import jax, jax.numpy as jnp
        from jax import lax
        import numpy as np
        B, T, C, TD = (8, 256, 256, 64)

        def _bi_wkv(r, k, v, w, u, time_emb):
            tf = jax.nn.sigmoid(jnp.sum(time_emb, axis=-1))[:, None, None]
            decay = jnp.exp(-jnp.exp(w.astype(jnp.float32)))[None, :] * (0.5 + 0.5 * tf[:, :, 0])
            kf = k.astype(jnp.float32)
            vf = v.astype(jnp.float32)
            ek = jnp.exp(jnp.minimum(kf, 30.0))
            ekv = ek * vf

            def step(carry, x):
                a, b = carry
                ekv_t, ek_t = x
                a = a * decay + ekv_t
                b = b * decay + ek_t
                return ((a, b), (a, b))
            ekv_t = jnp.swapaxes(ekv, 0, 1)
            ek_t = jnp.swapaxes(ek, 0, 1)
            init = (jnp.zeros_like(decay), jnp.zeros_like(decay))
            _, (nf, df) = lax.scan(step, init, (ekv_t, ek_t))
            _, (nb, db) = lax.scan(step, init, (ekv_t, ek_t), reverse=True)
            nf = jnp.swapaxes(nf, 0, 1)
            df = jnp.swapaxes(df, 0, 1)
            nb = jnp.swapaxes(nb, 0, 1)
            db = jnp.swapaxes(db, 0, 1)
            euk = jnp.exp(jnp.minimum(u.astype(jnp.float32)[None, None, :] + kf, 30.0))
            num = nf + nb - ekv + euk * vf
            den = df + db - ek + euk
            base = jax.nn.sigmoid(r.astype(jnp.float32)) * (num / jnp.maximum(den, 1e-08))
            out = base * (0.8 + 0.2 * tf)
            return out.astype(r.dtype)
        return _bi_wkv(r, k, v, w, u, time_emb)

    def _L1_ffn_ref(hidden_states, gate_w, e_bias, w1, w2, shared_up_w, shared_down_w):
        import jax, jax.numpy as jnp
        import numpy as np
        E = 64
        K = 6
        NG = 8
        TKG = 4
        SCALE = 2.5
        CAP = 64

        def _router(x, gate_w, e_bias):
            logits = x.astype(jnp.float32) @ gate_w.T
            scores = jax.nn.sigmoid(logits)
            sc = scores + e_bias[None, :]
            T = x.shape[0]
            gs = sc.reshape(T, NG, E // NG)
            grp_score = jax.lax.top_k(gs, 2)[0].sum(-1)
            _, gidx = jax.lax.top_k(grp_score, TKG)
            gmask = jax.nn.one_hot(gidx, NG, dtype=sc.dtype).sum(1)
            emask = jnp.repeat(gmask, E // NG, axis=1)
            masked = jnp.where(emask > 0, sc, -jnp.inf)
            _, idx = jax.lax.top_k(masked, K)
            w = jnp.take_along_axis(scores, idx, axis=1)
            w = w / (w.sum(-1, keepdims=True) + 1e-20) * SCALE
            return (idx, w)

        def _relu2(h):
            return jnp.square(jax.nn.relu(h))

        def _moe(x, idx, w, w1, w2):
            T, D = x.shape
            e_flat = idx.reshape(-1)
            tok = jnp.repeat(jnp.arange(T), K)
            oh = jax.nn.one_hot(e_flat, E, dtype=jnp.float32)
            pos = jnp.cumsum(oh, axis=0) - oh
            pos = (pos * oh).sum(-1).astype(jnp.int32)
            keep = pos < CAP
            slot = jnp.where(keep, pos, CAP)
            xd = jnp.zeros((E, CAP + 1, D), x.dtype).at[e_flat, slot].set(x[tok])
            h = _relu2(jnp.einsum('ecd,eid->eci', xd, w1))
            yd = jnp.einsum('eci,edi->ecd', h, w2)
            gate = w.reshape(-1)[:, None] * keep[:, None].astype(x.dtype)
            y_assign = yd[e_flat, slot] * gate
            return jnp.zeros((T, D), x.dtype).at[tok].add(y_assign)
        orig = hidden_states.shape
        x = hidden_states.reshape(-1, orig[-1])
        idx, wts = _router(x, gate_w, e_bias)
        shared = _relu2(x @ shared_up_w.T) @ shared_down_w.T
        routed = _moe(x, idx, wts.astype(x.dtype), w1, w2)
        return (shared + routed).reshape(orig)

    def _L2_cond_ref(r, k, v, w, u, time_emb):
        import jax, jax.numpy as jnp
        from jax import lax
        import numpy as np
        B, T, C, TD = (8, 256, 256, 64)

        def _bi_wkv(r, k, v, w, u, time_emb):
            tf = jax.nn.sigmoid(jnp.sum(time_emb, axis=-1))[:, None, None]
            decay = jnp.exp(-jnp.exp(w.astype(jnp.float32)))[None, :] * (0.5 + 0.5 * tf[:, :, 0])
            kf = k.astype(jnp.float32)
            vf = v.astype(jnp.float32)
            ek = jnp.exp(jnp.minimum(kf, 30.0))
            ekv = ek * vf

            def step(carry, x):
                a, b = carry
                ekv_t, ek_t = x
                a = a * decay + ekv_t
                b = b * decay + ek_t
                return ((a, b), (a, b))
            ekv_t = jnp.swapaxes(ekv, 0, 1)
            ek_t = jnp.swapaxes(ek, 0, 1)
            init = (jnp.zeros_like(decay), jnp.zeros_like(decay))
            _, (nf, df) = lax.scan(step, init, (ekv_t, ek_t))
            _, (nb, db) = lax.scan(step, init, (ekv_t, ek_t), reverse=True)
            nf = jnp.swapaxes(nf, 0, 1)
            df = jnp.swapaxes(df, 0, 1)
            nb = jnp.swapaxes(nb, 0, 1)
            db = jnp.swapaxes(db, 0, 1)
            euk = jnp.exp(jnp.minimum(u.astype(jnp.float32)[None, None, :] + kf, 30.0))
            num = nf + nb - ekv + euk * vf
            den = df + db - ek + euk
            base = jax.nn.sigmoid(r.astype(jnp.float32)) * (num / jnp.maximum(den, 1e-08))
            out = base * (0.8 + 0.2 * tf)
            return out.astype(r.dtype)
        return _bi_wkv(r, k, v, w, u, time_emb)

    def _L2_attn_ref(hidden_states, qkv_w, qkv_b, out_w, out_b):
        import jax, jax.numpy as jnp
        import numpy as np
        NUM_HEADS = 32
        ROPE_BASE = 10000.0
        MASK_NEG = -66504.0

        def _rotate_half(x):
            d = x.shape[-1] // 2
            return jnp.concatenate([-x[..., d:], x[..., :d]], axis=-1)
        S, B, E = hidden_states.shape
        H = NUM_HEADS
        D = E // H
        qkv = jnp.einsum('sbe,ef->sbf', hidden_states, qkv_w) + qkv_b
        q, k, v = jnp.split(qkv, 3, axis=-1)
        q = q.reshape(S, B, H, D)
        k = k.reshape(S, B, H, D)
        v = v.reshape(S, B, H, D)
        inv_freq = 1.0 / ROPE_BASE ** (jnp.arange(0, D, 2, dtype=jnp.float32) / D)
        freqs = jnp.arange(S, dtype=jnp.float32)[:, None] * inv_freq
        emb = jnp.concatenate([freqs, freqs], axis=-1)
        cos = jnp.cos(emb)[:, None, None, :].astype(hidden_states.dtype)
        sin = jnp.sin(emb)[:, None, None, :].astype(hidden_states.dtype)
        q = q * cos + _rotate_half(q) * sin
        k = k * cos + _rotate_half(k) * sin
        scale = 1.0 / jnp.sqrt(jnp.array(D, dtype=hidden_states.dtype))
        scores = jnp.einsum('sbhd,tbhd->bhst', q, k) * scale
        causal = jnp.tril(jnp.ones((S, S), dtype=scores.dtype))
        scores = scores + (1.0 - causal) * MASK_NEG
        attn = jax.nn.softmax(scores, axis=-1)
        ctx = jnp.einsum('bhst,tbhd->sbhd', attn, v).reshape(S, B, E)
        return jnp.einsum('sbe,ef->sbf', ctx, out_w) + out_b

    def _L2_cond2_ref(r, k, v, w, u, time_emb):
        import jax, jax.numpy as jnp
        from jax import lax
        import numpy as np
        B, T, C, TD = (8, 256, 256, 64)

        def _bi_wkv(r, k, v, w, u, time_emb):
            tf = jax.nn.sigmoid(jnp.sum(time_emb, axis=-1))[:, None, None]
            decay = jnp.exp(-jnp.exp(w.astype(jnp.float32)))[None, :] * (0.5 + 0.5 * tf[:, :, 0])
            kf = k.astype(jnp.float32)
            vf = v.astype(jnp.float32)
            ek = jnp.exp(jnp.minimum(kf, 30.0))
            ekv = ek * vf

            def step(carry, x):
                a, b = carry
                ekv_t, ek_t = x
                a = a * decay + ekv_t
                b = b * decay + ek_t
                return ((a, b), (a, b))
            ekv_t = jnp.swapaxes(ekv, 0, 1)
            ek_t = jnp.swapaxes(ek, 0, 1)
            init = (jnp.zeros_like(decay), jnp.zeros_like(decay))
            _, (nf, df) = lax.scan(step, init, (ekv_t, ek_t))
            _, (nb, db) = lax.scan(step, init, (ekv_t, ek_t), reverse=True)
            nf = jnp.swapaxes(nf, 0, 1)
            df = jnp.swapaxes(df, 0, 1)
            nb = jnp.swapaxes(nb, 0, 1)
            db = jnp.swapaxes(db, 0, 1)
            euk = jnp.exp(jnp.minimum(u.astype(jnp.float32)[None, None, :] + kf, 30.0))
            num = nf + nb - ekv + euk * vf
            den = df + db - ek + euk
            base = jax.nn.sigmoid(r.astype(jnp.float32)) * (num / jnp.maximum(den, 1e-08))
            out = base * (0.8 + 0.2 * tf)
            return out.astype(r.dtype)
        return _bi_wkv(r, k, v, w, u, time_emb)

    def _L2_ffn_ref(hidden_states, router_weight, e_bias, w_gate, w_up, w_down, sh_gate, sh_up, sh_down):
        import jax, jax.numpy as jnp
        import numpy as np
        from jax import lax
        E = 64
        H = 256
        I = 88
        G = 8
        TOPK_GROUP = 4
        K = 8
        B, S = (2, 256)
        N = B * S
        CAP = 2 * N * K // E
        SCALE = 2.5

        def _route(x, router_weight, e_bias):
            logits = x.astype(jnp.float32) @ router_weight.astype(jnp.float32).T
            scores = jax.nn.sigmoid(logits)
            sc = scores + e_bias
            n = x.shape[0]
            group_scores = lax.top_k(sc.reshape(n, G, E // G), 2)[0].sum(-1)
            grp_idx = lax.top_k(group_scores, TOPK_GROUP)[1]
            group_mask = jnp.zeros((n, G), jnp.float32).at[jnp.arange(n)[:, None], grp_idx].set(1.0)
            score_mask = jnp.repeat(group_mask, E // G, axis=1)
            masked = jnp.where(score_mask > 0, sc, 0.0)
            topk_idx = lax.top_k(masked, K)[1]
            topk_w = jnp.take_along_axis(scores, topk_idx, axis=1)
            topk_w = topk_w / (topk_w.sum(-1, keepdims=True) + 1e-20)
            return (topk_idx, topk_w * SCALE)

        def _moe_experts(x, topk_idx, topk_w, w_gate, w_up, w_down):
            n = x.shape[0]
            flat_e = topk_idx.reshape(-1)
            rows = jnp.repeat(jnp.arange(n), K)
            oh = jax.nn.one_hot(flat_e, E, dtype=jnp.int32)
            pos = jnp.cumsum(oh, axis=0) - oh
            pos = jnp.take_along_axis(pos, flat_e[:, None], axis=1)[:, 0]
            valid = (pos < CAP).astype(x.dtype)
            p = jnp.minimum(pos, CAP - 1)
            buf = jnp.zeros((E, CAP, H), x.dtype).at[flat_e, p].add(x[rows] * valid[:, None])
            g = jnp.einsum('ech,ehi->eci', buf, w_gate)
            u = jnp.einsum('ech,ehi->eci', buf, w_up)
            y = jnp.einsum('eci,eih->ech', jax.nn.silu(g) * u, w_down)
            y_tok = y[flat_e, p] * (topk_w.reshape(-1) * valid)[:, None]
            return jnp.zeros((n, H), x.dtype).at[rows].add(y_tok)

        def _shared_mlp(x, sh_gate, sh_up, sh_down):
            return jax.nn.silu(x @ sh_gate) * (x @ sh_up) @ sh_down
        orig_shape = hidden_states.shape
        x = hidden_states.reshape(-1, H)
        topk_idx, topk_w = _route(x, router_weight, e_bias)
        moe_out = _moe_experts(x, topk_idx, topk_w.astype(x.dtype), w_gate, w_up, w_down)
        out = moe_out + _shared_mlp(x, sh_gate, sh_up, sh_down)
        return out.reshape(orig_shape)

    def _L3_cond_ref(r, k, v, w, u, time_emb):
        import jax, jax.numpy as jnp
        from jax import lax
        import numpy as np
        B, T, C, TD = (8, 256, 256, 64)

        def _bi_wkv(r, k, v, w, u, time_emb):
            tf = jax.nn.sigmoid(jnp.sum(time_emb, axis=-1))[:, None, None]
            decay = jnp.exp(-jnp.exp(w.astype(jnp.float32)))[None, :] * (0.5 + 0.5 * tf[:, :, 0])
            kf = k.astype(jnp.float32)
            vf = v.astype(jnp.float32)
            ek = jnp.exp(jnp.minimum(kf, 30.0))
            ekv = ek * vf

            def step(carry, x):
                a, b = carry
                ekv_t, ek_t = x
                a = a * decay + ekv_t
                b = b * decay + ek_t
                return ((a, b), (a, b))
            ekv_t = jnp.swapaxes(ekv, 0, 1)
            ek_t = jnp.swapaxes(ek, 0, 1)
            init = (jnp.zeros_like(decay), jnp.zeros_like(decay))
            _, (nf, df) = lax.scan(step, init, (ekv_t, ek_t))
            _, (nb, db) = lax.scan(step, init, (ekv_t, ek_t), reverse=True)
            nf = jnp.swapaxes(nf, 0, 1)
            df = jnp.swapaxes(df, 0, 1)
            nb = jnp.swapaxes(nb, 0, 1)
            db = jnp.swapaxes(db, 0, 1)
            euk = jnp.exp(jnp.minimum(u.astype(jnp.float32)[None, None, :] + kf, 30.0))
            num = nf + nb - ekv + euk * vf
            den = df + db - ek + euk
            base = jax.nn.sigmoid(r.astype(jnp.float32)) * (num / jnp.maximum(den, 1e-08))
            out = base * (0.8 + 0.2 * tf)
            return out.astype(r.dtype)
        return _bi_wkv(r, k, v, w, u, time_emb)

    def _L3_attn_ref(x, Wq, bq, Bq, Aq, Wk, bk, Bk, Ak, Wv, bv, Bv, Av, Wo, bo, Bo, Ao):
        import jax, jax.numpy as jnp
        import numpy as np
        DIM = 256
        HEADS = 16
        HEAD_DIM = DIM // HEADS
        RANK = 16
        ALPHA = 8.0
        SCALING = ALPHA / RANK
        SCALE = HEAD_DIM ** (-0.5)

        def lora_linear(x, W, b, Bm, Am):
            out = jnp.einsum('bld,od->blo', x, W) + b
            upd = jnp.einsum('blr,or->blo', jnp.einsum('bld,rd->blr', x, Bm), Am)
            return out + SCALING * upd

        def _split(t):
            B, L, D = t.shape
            return t.reshape(B, L, HEADS, HEAD_DIM).transpose(0, 2, 1, 3)
        q = _split(lora_linear(x, Wq, bq, Bq, Aq))
        k = _split(lora_linear(x, Wk, bk, Bk, Ak))
        v = _split(lora_linear(x, Wv, bv, Bv, Av))
        scores = jnp.einsum('bhqd,bhkd->bhqk', q, k) * SCALE
        attn = jax.nn.softmax(scores, axis=-1)
        out = jnp.einsum('bhqk,bhkd->bhqd', attn, v)
        B, H, L, hd = out.shape
        out = out.transpose(0, 2, 1, 3).reshape(B, L, H * hd)
        return lora_linear(out, Wo, bo, Bo, Ao)

    def _L3_cond2_ref(r, k, v, w, u, time_emb):
        import jax, jax.numpy as jnp
        from jax import lax
        import numpy as np
        B, T, C, TD = (8, 256, 256, 64)

        def _bi_wkv(r, k, v, w, u, time_emb):
            tf = jax.nn.sigmoid(jnp.sum(time_emb, axis=-1))[:, None, None]
            decay = jnp.exp(-jnp.exp(w.astype(jnp.float32)))[None, :] * (0.5 + 0.5 * tf[:, :, 0])
            kf = k.astype(jnp.float32)
            vf = v.astype(jnp.float32)
            ek = jnp.exp(jnp.minimum(kf, 30.0))
            ekv = ek * vf

            def step(carry, x):
                a, b = carry
                ekv_t, ek_t = x
                a = a * decay + ekv_t
                b = b * decay + ek_t
                return ((a, b), (a, b))
            ekv_t = jnp.swapaxes(ekv, 0, 1)
            ek_t = jnp.swapaxes(ek, 0, 1)
            init = (jnp.zeros_like(decay), jnp.zeros_like(decay))
            _, (nf, df) = lax.scan(step, init, (ekv_t, ek_t))
            _, (nb, db) = lax.scan(step, init, (ekv_t, ek_t), reverse=True)
            nf = jnp.swapaxes(nf, 0, 1)
            df = jnp.swapaxes(df, 0, 1)
            nb = jnp.swapaxes(nb, 0, 1)
            db = jnp.swapaxes(db, 0, 1)
            euk = jnp.exp(jnp.minimum(u.astype(jnp.float32)[None, None, :] + kf, 30.0))
            num = nf + nb - ekv + euk * vf
            den = df + db - ek + euk
            base = jax.nn.sigmoid(r.astype(jnp.float32)) * (num / jnp.maximum(den, 1e-08))
            out = base * (0.8 + 0.2 * tf)
            return out.astype(r.dtype)
        return _bi_wkv(r, k, v, w, u, time_emb)

    def _L3_ffn_ref(x, w_gate, w_up, w_down, ln_weight):
        import jax, jax.numpy as jnp
        import numpy as np
        EPS = 1e-05
        RMS_EPS = 1e-06

        def activation_quant(x, num_bits=8):
            qn = -2 ** (num_bits - 1)
            qp = 2 ** (num_bits - 1) - 1
            xf = x.astype(jnp.float32)
            s = qp / jnp.clip(jnp.max(jnp.abs(xf), axis=-1, keepdims=True), EPS, None)
            return (jnp.clip(jnp.round(xf * s), qn, qp) / s).astype(x.dtype)

        def weight_quant(w):
            wf = w.astype(jnp.float32)
            s = 1.0 / jnp.clip(jnp.mean(jnp.abs(wf)), EPS, None)
            return (jnp.clip(jnp.round(wf * s), -1.0, 1.0) / s).astype(w.dtype)

        def bit_linear(x, w):
            qx = x + jax.lax.stop_gradient(activation_quant(x) - x)
            qw = w + jax.lax.stop_gradient(weight_quant(w) - w)
            return jnp.einsum('bsh,oh->bso', qx, qw)

        def rms_norm(x, weight, eps=RMS_EPS):
            xf = x.astype(jnp.float32)
            var = jnp.mean(xf * xf, axis=-1, keepdims=True)
            return weight * (xf * jax.lax.rsqrt(var + eps)).astype(x.dtype)
        h = jax.nn.silu(bit_linear(x, w_gate)) * bit_linear(x, w_up)
        h = rms_norm(h, ln_weight)
        return bit_linear(h, w_down)
    x = x + _L0_attn_ref(_L0_cond_ref(x, fside_BxSxS_0, fside_BxSxS_0, L0_cond_w, L0_cond_u, cond_512), L0_attn_w_qkv, L0_attn_w_proj)
    x = x + _L0_ffn_ref(_L0_cond2_ref(x, fside_BxSxS_0, fside_BxSxS_0, L0_cond2_w, L0_cond2_u, cond_512), L0_ffn_A, L0_ffn_Bw, L0_ffn_Wg)
    x = x + _L1_attn_ref(_L1_cond_ref(x, fside_BxSxS_0, fside_BxSxS_0, L1_cond_w, L1_cond_u, cond_512), L1_attn_wq, L1_attn_wk, L1_attn_wv, L1_attn_wo)
    x = x + _L1_ffn_ref(_L1_cond2_ref(x, fside_BxSxS_0, fside_BxSxS_0, L1_cond2_w, L1_cond2_u, cond_512), L1_ffn_gate_w, L1_ffn_e_bias, L1_ffn_w1, L1_ffn_w2, L1_ffn_shared_up_w, L1_ffn_shared_down_w)
    x = x + _L2_attn_ref(_L2_cond_ref(x, fside_BxSxS_0, fside_BxSxS_0, L2_cond_w, L2_cond_u, cond_512), L2_attn_qkv_w, L2_attn_qkv_b, L2_attn_out_w, L2_attn_out_b)
    x = x + _L2_ffn_ref(_L2_cond2_ref(x, fside_BxSxS_0, fside_BxSxS_0, L2_cond2_w, L2_cond2_u, cond_512), L2_ffn_router_weight, L2_ffn_e_bias, L2_ffn_w_gate, L2_ffn_w_up, L2_ffn_w_down, L2_ffn_sh_gate, L2_ffn_sh_up, L2_ffn_sh_down)
    x = x + _L3_attn_ref(_L3_cond_ref(x, fside_BxSxS_0, fside_BxSxS_0, L3_cond_w, L3_cond_u, cond_512), L3_attn_Wq, L3_attn_bq, L3_attn_Bq, L3_attn_Aq, L3_attn_Wk, L3_attn_bk, L3_attn_Bk, L3_attn_Ak, L3_attn_Wv, L3_attn_bv, L3_attn_Bv, L3_attn_Av, L3_attn_Wo, L3_attn_bo, L3_attn_Bo, L3_attn_Ao)
    x = x + _L3_ffn_ref(_L3_cond2_ref(x, fside_BxSxS_0, fside_BxSxS_0, L3_cond2_w, L3_cond2_u, cond_512), L3_ffn_w_gate, L3_ffn_w_up, L3_ffn_w_down, L3_ffn_ln_weight)
    return x

_drawn_inputs = setup_inputs


def setup_inputs(seed=0):
    import zlib

    import numpy as np

    out = dict(_drawn_inputs(seed))
    spreads = {'L1_ffn_e_bias': (0.0, 0.1),
     'L2_attn_out_b': (0.0, 0.1),
     'L2_ffn_e_bias': (0.0, 0.1),
     'L3_ffn_ln_weight': (1.0, 0.2)}
    factors = {'L0_cond2_w': 3.096,
     'L0_cond2_u': 5.629,
     'L0_ffn_Wg': 2.852,
     'L2_cond_w': 3.517,
     'L2_cond_u': 6.983,
     'L2_attn_qkv_b': 5.75,
     'L3_cond_w': 4.482,
     'L3_cond_u': 8.0,
     'L3_attn_Wq': 8.0,
     'L3_attn_bq': 8.0,
     'L3_attn_Bq': 8.0,
     'L3_attn_Aq': 8.0,
     'L3_attn_Wk': 8.0,
     'L3_attn_bk': 8.0,
     'L3_attn_Bk': 8.0,
     'L3_attn_Ak': 8.0,
     'L3_attn_bv': 6.913,
     'L3_attn_Bv': 8.0,
     'L3_attn_Av': 8.0,
     'L3_attn_bo': 3.619,
     'L3_attn_Bo': 8.0,
     'L3_attn_Ao': 8.0}
    for name, (base, spread) in spreads.items():
        noise = np.random.default_rng([zlib.crc32(name.encode()), seed]).standard_normal(out[name].shape)
        drawn = base * np.exp(spread * noise) if base else spread * noise
        out[name] = jnp.asarray(drawn.astype(out[name].dtype))
    for name, factor in factors.items():
        out[name] = (out[name] * factor).astype(out[name].dtype)
    return out
```

```python
import numpy as np
from contextlib import ExitStack

import concourse.bass as bass
from concourse import mybir

F32 = mybir.dt.float32
BF16 = mybir.dt.bfloat16
I32 = mybir.dt.int32
U32 = mybir.dt.uint32
ALU = mybir.AluOpType
ACT = mybir.ActivationFunctionType
AX = mybir.AxisListType

P = 128
B, T, C = 4, 256, 256
NT = B * T
CT = C // P
TT = NT // P
HALF = 512
NH = 16
HG = 4
GROUPS = NH // HG
CONDS = 4
ROUND = 1.5 * 2.0 ** 23
MASKED = -1e30


class Tally:

    def __init__(self, eng, sem):
        self.eng, self.sem, self.n, self.base = eng, sem, 0, None

    def value(self):
        return self.n if self.base is None else self.base + self.n

    def link(self, ins):
        ins.then_inc(self.sem, 1)
        self.n += 1
        self.eng.wait_ge(self.sem, self.value())

    def enter(self, turn, per):
        self.before, self.per, self.base, self.n = self.n, per, turn * per + self.n, 0

    def leave(self, turns):
        assert self.n == self.per, (self.n, self.per)
        self.base, self.n = None, self.before + turns * self.per


class Stage:

    def __init__(self, nc, name):
        self.nc, self.name, self.stack, self.sems = nc, name, ExitStack(), []

    def __enter__(self):
        return self

    def __exit__(self, *e):
        for s in self.sems:
            self.nc.sync.sem_clear(s)
        self.stack.close()

    def sb(self, name, shape, dt=F32):
        return self.stack.enter_context(self.nc.sbuf_tensor(f"{self.name}_{name}", shape, dt))

    def ps(self, name, shape, dt=F32):
        return self.stack.enter_context(self.nc.psum_tensor(f"{self.name}_{name}", shape, dt))

    def sem(self, name):
        self.sems.append(self.stack.enter_context(self.nc.semaphore(f"{self.name}_{name}")))
        return self.sems[-1]


class Core:
    pass



def load_constants(nc, m, d):
    with Stage(nc, "start") as st:
        loaded, zeroed, filled = st.sem("loaded"), st.sem("zeroed"), st.sem("filled")
        zeros = st.sb("zeros", [P, 4096])
        pairs = [(m.xT, "xT"), (m.ident, "ident"), (m.ones, "ones"), (m.wu, "wu"), (m.condT, "condT"),
             (m.ident_b, "ident_b"), (m.mask_causal, "mask_causal"), (m.mask_window, "mask_window"),
             (m.ones_b, "ones_b"), (m.earlier, "earlier"), (m.iota, "iota")]
        with nc.Block() as block:
            @block.sync
            def _(sp):
                for tile, name in pairs:
                    sp.dma_start(tile[:], d[name]).then_inc(loaded, 16)
                sp.wait_ge(zeroed, 1)
                n = 0
                for slots in (m.slots_in_1, m.slots_in_2):
                    flat = slots.rearrange("(p r) c -> p (r c)", p=P)
                    for c in range(0, flat.shape[1], 4096):
                        sp.dma_start(flat[:, c:c + 4096], zeros[:, :]).then_inc(filled, 16)
                        n += 1
                sp.wait_ge(loaded, 16 * len(pairs))
                sp.wait_ge(filled, 16 * n)

            @block.vector
            def _(dve):
                nc.vector.memset(zeros[:, :], 0.0).then_inc(zeroed, 1)


def condition_gains(nc, m, d, name, first):
    with Stage(nc, name) as st:
        kT, ek, ekv = (st.sb(n, [P, CT, NT]) for n in ("kT", "ek", "ekv"))
        dec, dw, dw2 = st.sb("dec", [P, CONDS, CT, B]), st.sb("dw", [P, CONDS, CT]), st.sb("dw2", [P, CONDS, CT])
        tf, dfac, ofac = st.sb("tf", [P, B]), st.sb("dfac", [P, B]), st.sb("ofac", [P, B])
        uk, euk, z, zv, rd = (st.sb(n, [P, 2, NT]) for n in ("uk", "euk", "z", "zv", "rd"))
        lnd, seed, corr = (st.sb(n, [P, 2, NT]) for n in ("lnd", "seed", "corr"))
        sc = st.sb("sc", [P, 2, 4, NT])
        num, den = st.ps("num", [P, 2, NT]), st.ps("den", [P, 2, NT])
        (loaded, own_dve, capped, ek_ready, ekv_ready, dw_ready, w_ready, tf_sum, tf_ready, uk_ready, euk_ready,
         z_ready, zv_ready, scans_ready, sums_ready, clamped, seeded, gain_ready, own_act) = (
            st.sem(n) for n in ("loaded", "own_dve", "capped", "ek", "ekv", "dw", "w", "tf_sum", "tf", "uk", "euk",
                                "z", "zv", "scans", "sums", "clamped", "seeded", "gain", "own_act"))
        w = m.wu[:, 0, first:first + CONDS, :]
        with nc.Block() as block:
            @block.sync
            def _(sp):
                sp.dma_start(kT[:], d["fsideT"]).then_inc(loaded, 16)

            @block.tensor
            def _(pe):
                nc.tensor.matmul(num[:, 0, 0:B], m.ones[0:64, :], m.condT[:, :], start=True, stop=True).then_inc(tf_sum, 1)
                pe.wait_ge(tf_ready, 1)

                def add_up(i, ct, early):
                    s = i * CT + ct
                    pe.wait_ge(scans_ready, s + 1)
                    pe.wait_ge(zv_ready, s + 1)
                    if not early:
                        pe.wait_ge(gain_ready, s - 1)
                    for acc, terms in ((num, (sc[:, ct, 0], sc[:, ct, 1], zv[:, ct])),
                                       (den, (sc[:, ct, 2], sc[:, ct, 3], z[:, ct]))):
                        for c in range(0, NT, HALF):
                            for n, t in enumerate(terms):
                                last = nc.tensor.matmul(acc[:, ct, c:c + HALF], m.ident[:, :], t[:, c:c + HALF],
                                                        start=n == 0, stop=n == 2)
                    last.then_inc(sums_ready, 1)
                add_up(0, 0, True)
                add_up(0, 1, True)
                with pe.Fori(1, CONDS, 1) as i:
                    add_up(i, 0, False)
                    add_up(i, 1, False)

            @block.scalar
            def _(act):
                nc.scalar.activation(dw[:, :, :], w, ACT.Exp).then_inc(dw_ready, 1)
                act.wait_ge(dw_ready, 1)
                nc.scalar.activation(dw2[:, :, :], dw[:, :, :], ACT.Exp, scale=-1.0).then_inc(w_ready, 1)
                act.wait_ge(tf_sum, 1)
                nc.scalar.activation(tf[:, :], num[:, 0, 0:B], ACT.Sigmoid).then_inc(tf_ready, 1)
                act.wait_ge(capped, 1)
                nc.scalar.activation(ek[:, :, :], ek[:, :, :], ACT.Exp).then_inc(ek_ready, 1)

                def exp_uk(i, ct, early):
                    s = i * CT + ct
                    act.wait_ge(uk_ready, s + 1)
                    if not early:
                        act.wait_ge(z_ready, s - 1)
                    nc.scalar.activation(euk[:, ct], uk[:, ct], ACT.Exp).then_inc(euk_ready, 1)

                def seed_inverse(i, ct):
                    s = i * CT + ct
                    act.wait_ge(clamped, s + 1)
                    nc.scalar.activation(lnd[:, ct], rd[:, ct], ACT.Ln).then_inc(own_act, 1)
                    act.wait_ge(own_act, s + 1)
                    nc.scalar.activation(seed[:, ct], lnd[:, ct], ACT.Exp, scale=-1.0).then_inc(seeded, 1)
                exp_uk(0, 0, True)
                exp_uk(0, 1, True)
                seed_inverse(0, 0)
                with act.Fori(1, CONDS, 1) as i:
                    exp_uk(i, 0, False)
                    seed_inverse(i - 1, 1)
                    exp_uk(i, 1, False)
                    seed_inverse(i, 0)
                seed_inverse(CONDS - 1, 1)

            @block.gpsimd
            def _(pool):
                pool.wait_ge(ek_ready, 1)
                nc.gpsimd.tensor_tensor(ekv[:, :, :], ek[:, :, :], kT[:, :, :], ALU.mult).then_inc(ekv_ready, 1)

                def own_token(i, ct, early):
                    s = i * CT + ct
                    pool.wait_ge(euk_ready, s + 1)
                    if not early:
                        pool.wait_ge(sums_ready, s - 1)
                    nc.gpsimd.tensor_tensor(z[:, ct], euk[:, ct], ek[:, ct], ALU.subtract).then_inc(z_ready, 1)
                    pool.wait_ge(z_ready, s + 1)
                    nc.gpsimd.tensor_tensor(zv[:, ct], z[:, ct], kT[:, ct], ALU.mult).then_inc(zv_ready, 1)
                own_token(0, 0, True)
                own_token(0, 1, True)
                with pool.Fori(1, CONDS, 1) as i:
                    own_token(i, 0, False)
                    own_token(i, 1, False)

            @block.vector
            def _(dve):
                own = Tally(dve, own_dve)
                dve.wait_ge(loaded, 16)
                nc.vector.tensor_scalar(ek[:, :, :], kT[:, :, :], 30.0, None, ALU.min).then_inc(capped, 1)
                dve.wait_ge(tf_ready, 1)
                nc.vector.tensor_scalar(ofac[:, :], tf[:, :], 0.2, 0.8, ALU.mult, ALU.add)
                own.link(nc.vector.tensor_scalar(dfac[:, :], tf[:, :], 0.5, 0.5, ALU.mult, ALU.add))
                dve.wait_ge(w_ready, 1)
                for b in range(B):
                    last = nc.vector.tensor_scalar(dec[:, :, :, b], dw2[:, :, :], dfac[:, b:b + 1], None, ALU.mult)
                own.link(last)
                dve.wait_ge(ekv_ready, 1)

                def scans(i, ct, early):
                    s = i * CT + ct
                    if not early:
                        dve.wait_ge(euk_ready, s - 1)
                    nc.vector.tensor_scalar(uk[:, ct], kT[:, ct], m.wu[:, 1, bass.ds(first + i, 1), ct], 30.0,
                                            ALU.add, ALU.min).then_inc(uk_ready, 1)
                    if not early:
                        dve.wait_ge(sums_ready, s - 1)
                    for b in range(B):
                        decay = dec[:, bass.ds(i, 1), ct, b].broadcast_to([P, T])
                        ahead = slice(b * T, b * T + T)
                        back = slice(b * T + T - 1, b * T - 1 if b else None, -1)
                        for n, src in enumerate((ekv, ek)):
                            nc.vector.tensor_tensor_scan(sc[:, ct, 2 * n, ahead], decay, src[:, ct, ahead], 0.0,
                                                         ALU.mult, ALU.add)
                            last = nc.vector.tensor_tensor_scan(sc[:, ct, 2 * n + 1, back], decay, src[:, ct, back],
                                                                0.0, ALU.mult, ALU.add)
                    last.then_inc(scans_ready, 1)

                def clamp(i, ct, early):
                    dve.wait_ge(sums_ready, i * CT + ct + 1)
                    nc.vector.tensor_scalar(rd[:, ct], den[:, ct], 1e-8, None, ALU.max).then_inc(clamped, 1)

                def gains(i, ct):
                    s = i * CT + ct
                    dve.wait_ge(seeded, s + 1)
                    own.link(nc.vector.tensor_tensor(corr[:, ct], rd[:, ct], seed[:, ct], ALU.mult))
                    own.link(nc.vector.scalar_tensor_tensor(out=corr[:, ct], in0=corr[:, ct], scalar=2.0, in1=seed[:, ct],
                                                            op0=ALU.subtract, op1=ALU.mult))
                    for b in range(B):
                        t = slice(b * T, b * T + T)
                        last = nc.vector.scalar_tensor_tensor(
                            out=m.gain[:, bass.ds(i, 1), ct, t], in0=num[:, ct, t], scalar=ofac[:, b:b + 1],
                            in1=corr[:, ct, t], op0=ALU.mult, op1=ALU.mult)
                    last.then_inc(gain_ready, 1)
                own.link(nc.vector.tensor_scalar(ofac[:, :], ofac[:, :], -1.0, None, ALU.mult))
                scans(0, 0, True)
                scans(0, 1, True)
                clamp(0, 0, True)
                gains(0, 0)
                with dve.Fori(1, CONDS, 1) as i:
                    own.enter(i - 1, 4)
                    clamp(i - 1, 1, False)
                    scans(i, 0, False)
                    gains(i - 1, 1)
                    scans(i, 1, False)
                    clamp(i, 0, False)
                    gains(i, 0)
                own.leave(CONDS - 1)
                clamp(CONDS - 1, 1, False)
                gains(CONDS - 1, 1)


def apply_condition(nc, m, name, i, tok=False):
    with Stage(nc, name) as st:
        sig = st.sb("sig", [P, CT, NT])
        sig_ready, h_ready, turned = st.sem("sig"), st.sem("h"), st.sem("turned")
        tp = st.ps("tp", [P, TT, C]) if tok else None
        with nc.Block() as block:
            @block.scalar
            def _(act):
                for ct in range(CT):
                    nc.scalar.activation(sig[:, ct], m.xT[:, ct], ACT.Sigmoid).then_inc(sig_ready, 1)
                if tok:
                    for half in range(2):
                        act.wait_ge(turned, half + 1)
                        j = slice(half * TT // 2, (half + 1) * TT // 2)
                        nc.scalar.activation(m.tok[:, j, :], tp[:, j, :], ACT.Copy)

            @block.vector
            def _(dve):
                for ct in range(CT):
                    dve.wait_ge(sig_ready, ct + 1)
                    nc.vector.tensor_tensor(m.hT[:, ct], sig[:, ct], m.gain[:, i, ct], ALU.mult).then_inc(h_ready, 1)

            @block.tensor
            def _(pe):
                if tok:
                    pe.wait_ge(h_ready, CT)
                    for j in range(TT):
                        for ct in range(CT):
                            last = nc.tensor.transpose(tp[:, j, ct * P:(ct + 1) * P], m.hT[:, ct, j * P:(j + 1) * P],
                                                       m.ident[:, :])
                        if j % (TT // 2) == TT // 2 - 1:
                            last.then_inc(turned, 1)



def quantize_tokens(nc, m, name, tok, qT, feats):
    KT = feats // P
    per = HALF // P
    with Stage(nc, name) as st:
        amax, inv, s = st.sb("amax", [P, TT]), st.sb("inv", [P, TT]), st.sb("s", [P, TT])
        tp = st.ps("tp", [P, 4, HALF])
        own_dve, quantized, turned = (st.sem(n) for n in ("own_dve", "quantized", "turned"))
        moved = [st.sem("moved_by_dve"), st.sem("moved_by_act")]
        banks = [(k, h) for h in range(TT // per) for k in range(KT)]
        with nc.Block() as block:
            @block.vector
            def _(dve):
                own = Tally(dve, own_dve)
                own.link(nc.vector.tensor_reduce(amax[:, :], tok[:, :, :], AX.X, ALU.max, apply_absolute_value=True))
                own.link(nc.vector.tensor_scalar(amax[:, :], amax[:, :], 1e-5, None, ALU.max))
                own.link(nc.vector.reciprocal(s[:, :], amax[:, :]))
                own.link(nc.vector.tensor_scalar(s[:, :], s[:, :], 127.0, None, ALU.mult))
                own.link(nc.vector.tensor_scalar(inv[:, :], amax[:, :], 1.0 / 127.0, None, ALU.mult))
                for j in range(TT):
                    last = nc.vector.tensor_scalar(tok[:, j, :], tok[:, j, :], s[:, j:j + 1], ROUND, ALU.mult, ALU.add)
                own.link(last)
                for j in range(TT):
                    nc.vector.tensor_scalar(tok[:, j, :], tok[:, j, :], ROUND, inv[:, j:j + 1], ALU.subtract,
                                            ALU.mult).then_inc(quantized, 1)
                for n, (k, h) in enumerate(banks):
                    if n % 2 == 0:
                        dve.wait_ge(turned, n + 1)
                        nc.vector.tensor_copy(qT[:, k, h * HALF:(h + 1) * HALF], tp[:, n % 4, :]).then_inc(moved[0], 1)

            @block.scalar
            def _(act):
                for n, (k, h) in enumerate(banks):
                    if n % 2:
                        act.wait_ge(turned, n + 1)
                        nc.scalar.activation(qT[:, k, h * HALF:(h + 1) * HALF], tp[:, n % 4, :], ACT.Copy).then_inc(moved[1], 1)

            @block.tensor
            def _(pe):
                for n, (k, h) in enumerate(banks):
                    pe.wait_ge(quantized, (h + 1) * per)
                    if n >= 4:
                        pe.wait_ge(moved[n % 2], (n - 4) // 2 + 1)
                    for j in range(per):
                        last = nc.tensor.transpose(tp[:, n % 4, j * P:(j + 1) * P],
                                                   tok[:, h * per + j, k * P:(k + 1) * P], m.ident[:, :])
                    last.then_inc(turned, 1)


def quantize_weights(nc, m, name, groups):
    with Stage(nc, name) as st:
        views = [(w, g) for g, (ws, _) in enumerate(groups) for w in ws]
        part = st.sb("part", [P, len(views)])
        mean, s = st.sb("mean", [P, len(groups)]), st.sb("s", [P, len(groups)])
        total = st.ps("total", [P, len(groups)])
        own_dve, parts, summed = (st.sem(k) for k in ("own_dve", "parts", "summed"))
        with nc.Block() as block:
            @block.vector
            def _(dve):
                own = Tally(dve, own_dve)
                for i, (w, _) in enumerate(views):
                    last = dve.tensor_reduce(part[:, i:i + 1], w, AX.XY, ALU.add, apply_absolute_value=True)
                last.then_inc(parts, 1)
                dve.wait_ge(summed, 1)
                for g, (_, count) in enumerate(groups):
                    last = dve.tensor_scalar(mean[:, g:g + 1], total[:, g:g + 1], 1.0 / count, 1e-5, ALU.mult, ALU.max)
                own.link(last)
                own.link(dve.reciprocal(s[:, :], mean[:, :]))
                for step in range(3):
                    for w, g in views:
                        if step == 0:
                            last = dve.tensor_scalar(w, w, s[:, g:g + 1], ROUND, ALU.mult, ALU.add)
                        elif step == 1:
                            last = dve.tensor_scalar(w, w, ROUND, 1.0, ALU.subtract, ALU.min)
                        else:
                            last = dve.tensor_scalar(w, w, -1.0, mean[:, g:g + 1], ALU.max, ALU.mult)
                    own.link(last)

            @block.tensor
            def _(pe):
                pe.wait_ge(parts, 1)
                for g in range(len(groups)):
                    mine = [i for i, (_, g_) in enumerate(views) if g_ == g]
                    for i in mine:
                        last = pe.matmul(total[:, g:g + 1], m.ones[:, :], part[:, i:i + 1], start=i == mine[0], stop=i == mine[-1])
                last.then_inc(summed, 1)


def load(nc, name, pairs):
    with Stage(nc, name) as st:
        loaded = st.sem("loaded")
        with nc.Block() as block:
            @block.sync
            def _(sp):
                for tile, src in pairs:
                    sp.dma_start(tile, src).then_inc(loaded, 16)
                sp.wait_ge(loaded, 16 * len(pairs))



class Heads:

    def __init__(self, st, causal):
        self.blocks = [(0, 0), (1, 0), (1, 1)] if causal else [(0, 0), (0, 1), (1, 0), (1, 1)]
        self.causal = causal
        self.split = P if causal else 2 * P
        self.width = len(self.blocks) * P
        self.scores = st.ps("scores", [P, 2, HALF])
        self.turned = st.ps("turned", [P, 2, HALF])
        self.probs = st.sb("probs", [P, 2, HALF])
        self.probsT = st.sb("probsT", [P, 2, HALF])
        self.top = st.sb("top", [P, NH, 2])
        self.bias = st.sb("bias", [P, NH, 2])
        self.total = st.sb("total", [P, NH, 2])
        (self.s_scores, self.s_bias, self.s_turned, self.s_out, self.s_norm) = (
            st.sem(n) for n in ("scores_ready", "bias_ready", "turned_ready", "out_ready", "norm_ready"))
        self.s_moved = [st.sem("moved_by_dve"), st.sem("moved_by_act")]

    def tiles(self):
        return ((0, slice(0, self.split)), (1, slice(self.split, self.width)))

    def score(self, pe, turn, h, q, k, ident=None, mask=None):
        if h >= 2:
            pe.wait_ge(self.s_norm, turn + h - 1)
        for nt, cols in self.tiles():
            into = self.scores[:, h % 2, cols]
            if self.causal:
                pe.matmul(into, ident, mask[:, cols], start=True, stop=False)
            last = pe.matmul(into, q[:, nt * P:(nt + 1) * P], k[:, 0:cols.stop - cols.start],
                             start=not self.causal, stop=True)
        last.then_inc(self.s_scores, 1)

    def turn(self, pe, turn, h, ident):
        pe.wait_ge(self.s_norm, turn + h + 1)
        if h >= 2:
            pe.wait_ge(self.s_moved[h % 2], turn // 2 + (h - 2) // 2 + 1)
        for n in range(len(self.blocks)):
            last = pe.transpose(self.turned[:, h % 2, n * P:(n + 1) * P], self.probs[:, h % 2, n * P:(n + 1) * P], ident)
        last.then_inc(self.s_turned, 1)

    def top_of(self, dve, own, turn, h, scale):
        dve.wait_ge(self.s_scores, turn + h + 1)
        if self.causal:
            for nt, cols in self.tiles():
                last = dve.tensor_reduce(self.top[:, h, nt:nt + 1], self.scores[:, h % 2, cols], AX.X, ALU.max)
            own.link(last)
        else:
            own.link(dve.tensor_reduce(self.top[:, h, :], self.scores[:, h % 2, :].rearrange("p (n k) -> p n k", n=2),
                                       AX.X, ALU.max))
        dve.tensor_scalar(self.bias[:, h, :], self.top[:, h, :], -scale, None, ALU.mult).then_inc(self.s_bias, 1)

    def move(self, eng, copy, turn, h):
        eng.wait_ge(self.s_turned, turn + h + 1)
        if h >= 2:
            eng.wait_ge(self.s_out, turn + h - 1)
        copy(self.probsT[:, h % 2, 0:self.width], self.turned[:, h % 2, 0:self.width]).then_inc(self.s_moved[h % 2], 1)

    def exp(self, act, turn, h, scale, ready):
        act.wait_ge(self.s_bias, turn + h + 1)
        if h >= 2:
            act.wait_ge(self.s_turned, turn + h - 1)
        for nt, cols in self.tiles():
            last = act.activation(self.probs[:, h % 2, cols], self.scores[:, h % 2, cols], ACT.Exp, bias=self.bias[:, h, nt:nt + 1],
                                  scale=scale, accum_out=self.total[:, h, nt:nt + 1])
        last.then_inc(ready, 1)


def attention_small_heads(nc, m, d, name, x, w_qk, w_v, causal, scale, qk_bias=None, lora=None):
    with Stage(nc, name) as st:
        hd = Heads(st, causal)
        xb = st.sb("xb", [P, CT, T])
        qk = st.sb("qk", [P, 2 * GROUPS, T])
        v = st.sb("v", [P, 2, C])
        rtot = st.sb("rtot", [P, NH, 2])
        out = st.ps("out", [P, 2, C])
        prj = st.ps("prj", [P, 2, HALF])
        own_dve, s_xb, s_prj, s_xfree = (st.sem(n) for n in ("own_dve", "xb_ready", "prj_ready", "x_free"))
        s_low, s_lowready = st.sem("low_sum"), st.sem("low_ready")
        s_kept = [st.sem("kept_by_dve"), st.sem("kept_by_act")]
        NB = GROUPS + 1
        low = st.sb("low", [P, T]) if lora else None

        with nc.Block() as block:
            def kept(n):
                return (1, n // 2) if n % 2 else (0, n // 2)

            @block.tensor
            def _(pe):
                def batch(b, first):
                    turn = b * NH
                    pe.wait_ge(s_xb, b + 1)
                    if lora:
                        for ct in range(CT):
                            last = pe.matmul(prj[:, 1, 0:T], lora[0][:, ct], xb[:, ct], start=ct == 0, stop=ct == CT - 1)
                        last.then_inc(s_low, 1)
                        pe.wait_ge(s_lowready, b + 1)
                    for n in range(NB):
                        if n >= 2:
                            pe.wait_ge(s_kept[n % 2], b * ((NB + 1 - n % 2) // 2) + (n - 2) // 2 + 1)
                        for half in range(2):
                            into = prj[:, n % 2, half * T:(half + 1) * T]
                            for ct in range(CT):
                                if n < GROUPS:
                                    g = 2 * n + half
                                    last = pe.matmul(into, w_qk[:, ct, g * P:(g + 1) * P], xb[:, ct],
                                                     start=ct == 0, stop=ct == CT - 1 and not lora)
                                else:
                                    last = pe.matmul(into, xb[:, ct, half * P:(half + 1) * P], w_v[:, ct],
                                                     start=ct == 0, stop=ct == CT - 1 and not lora)
                            if lora and n < GROUPS:
                                r = 32 * (g // GROUPS)
                                last = pe.matmul(into, lora[1][r:r + 16, (g % GROUPS) * P:(g % GROUPS + 1) * P],
                                                 low[r:r + 16, :], start=False, stop=True)
                            elif lora:
                                last = pe.matmul(into, low[64:64 + 17, half * P:(half + 1) * P], lora[2][64:64 + 17, :],
                                                 start=False, stop=True)
                        last.then_inc(s_prj, 1)
                    pe.wait_ge(s_kept[0], (b + 1) * ((NB + 1) // 2))
                    pe.wait_ge(s_kept[1], (b + 1) * (NB // 2))
                    if not first:
                        pe.wait_ge(s_xfree, b)

                    def weigh(h):
                        pe.wait_ge(hd.s_moved[h % 2], turn // 2 + h // 2 + 1)
                        for nt in range(2):
                            mine = [(i, mt) for i, (n_, mt) in enumerate(hd.blocks) if n_ == nt]
                            for i, mt in mine:
                                last = pe.matmul(out[:, nt, h * 16:(h + 1) * 16], hd.probsT[:, h % 2, i * P:(i + 1) * P],
                                                 v[:, mt, h * 16:(h + 1) * 16], start=i == mine[0][0], stop=i == mine[-1][0])
                        last.then_inc(hd.s_out, 1)
                    for i in range(NH + 2):
                        if i < NH:
                            r = 32 * (i % HG)
                            hd.score(pe, turn, i, qk[r:r + 16, i // HG, :], qk[r:r + 16, GROUPS + i // HG, :], m.ident_b[:, :], m.mask_causal)
                        if 1 <= i <= NH:
                            hd.turn(pe, turn, i - 1, m.ident[:, :])
                        if i >= 2:
                            weigh(i - 2)
                batch(0, True)
                with pe.Fori(1, B, 1) as b:
                    batch(b, False)

            def keep(eng, copy, b, n):
                eng.wait_ge(s_prj, b * NB + n + 1)
                if n < GROUPS:
                    src = prj[:, n % 2, :].rearrange("p (g t) -> p g t", g=2)
                    if qk_bias is None:
                        copy(qk[:, 2 * n:2 * n + 2, :], src).then_inc(s_kept[n % 2], 1)
                    else:
                        for half in range(2):
                            g = 2 * n + half
                            last = eng.tensor_scalar(qk[:, g, :], src[:, half], qk_bias[:, g:g + 1], None, ALU.add) \
                                if n % 2 == 0 else \
                                eng.activation(qk[:, g, :], src[:, half], ACT.Identity, bias=qk_bias[:, g:g + 1])
                        last.then_inc(s_kept[n % 2], 1)
                else:
                    copy(v[:, :, :], prj[:, n % 2, :].rearrange("p (g t) -> p g t", g=2)).then_inc(s_kept[n % 2], 1)

            @block.scalar
            def _(act):
                def copy(o, i):
                    return nc.scalar.activation(o, i, ACT.Copy)

                def batch(b, first):
                    turn = b * NH
                    if lora:
                        act.wait_ge(s_low, b + 1)
                        act.activation(low[:, :], prj[:, 1, 0:T], ACT.Identity, scale=0.5,
                                       bias=m.low_bias[:, 0:1]).then_inc(s_lowready, 1)
                    for n in range(1, NB, 2):
                        keep(act, copy, b, n)
                    for i in range(NH + 1):
                        if i < NH:
                            hd.exp(act, turn, i, scale, hd.s_norm)
                        if i >= 1 and (i - 1) % 2:
                            hd.move(act, copy, turn, i - 1)
                batch(0, True)
                with act.Fori(1, B, 1) as b:
                    batch(b, False)

            @block.vector
            def _(dve):
                own = Tally(dve, own_dve)

                def copy(o, i):
                    return nc.vector.tensor_copy(o, i)

                def batch(b, first):
                    turn = b * NH
                    if not first:
                        dve.wait_ge(s_prj, b * NB)
                    dve.tensor_copy(xb[:, :, :], x[:, :, bass.ds(b * T, T)]).then_inc(s_xb, 1)
                    for n in range(0, NB, 2):
                        keep(dve, copy, b, n)
                    for i in range(NH + 1):
                        if i < NH:
                            hd.top_of(dve, own, turn, i, scale)
                        if i >= 1 and (i - 1) % 2 == 0:
                            hd.move(dve, copy, turn, i - 1)
                    dve.wait_ge(hd.s_norm, turn + NH)
                    own.link(dve.reciprocal(rtot[:, :, :], hd.total[:, :, :]))
                    dve.wait_ge(hd.s_out, turn + NH)
                    for nt in range(2):
                        last = dve.tensor_tensor(m.tok[:, bass.ds(2 * b + nt, 1), :].rearrange("p o (h c) -> p (o h) c", h=NH),
                                                 out[:, nt, :].rearrange("p (h c) -> p h c", h=NH),
                                                 rtot[:, :, nt:nt + 1].broadcast_to([P, NH, 16]), ALU.mult)
                    last.then_inc(s_xfree, 1)
                batch(0, True)
                with dve.Fori(1, B, 1) as b:
                    own.enter(b - 1, NH + 1)
                    batch(b, False)
                own.leave(B - 1)


def add_product(nc, m, name, w, x, bias=None, low=None):
    kts = w.shape[1]
    with Stage(nc, name) as st:
        acc = st.ps("acc", [P, CT, NT])
        s_sum = st.sem("sum")
        with nc.Block() as block:
            @block.tensor
            def _(pe):
                for o in range(CT):
                    for h in range(NT // HALF):
                        t = slice(h * HALF, (h + 1) * HALF)
                        for k in range(kts):
                            last = pe.matmul(acc[:, o, t], w[:, k, o * P:(o + 1) * P], x[:, k, t],
                                             start=k == 0, stop=k == kts - 1 and low is None)
                        if low is not None:
                            last = pe.matmul(acc[:, o, t], low[0][:, o * P:(o + 1) * P], low[1][:, t], start=False, stop=True)
                        last.then_inc(s_sum, 1)

            @block.vector
            def _(dve):
                for o in range(CT):
                    for h in range(NT // HALF):
                        t = slice(h * HALF, (h + 1) * HALF)
                        dve.wait_ge(s_sum, o * (NT // HALF) + h + 1)
                        if bias is None:
                            dve.tensor_tensor(m.xT[:, o, t], m.xT[:, o, t], acc[:, o, t], ALU.add)
                        else:
                            dve.scalar_tensor_tensor(out=m.xT[:, o, t], in0=acc[:, o, t], scalar=bias[:, o:o + 1],
                                                     in1=m.xT[:, o, t], op0=ALU.add, op1=ALU.add)



L0_E, L0_R = 8, 64


def argmax_gates(nc, m, d, name, w_g, select, gates):
    with Stage(nc, name) as st:
        lg, ex = st.sb("lg", [P, TT, L0_E]), st.sb("ex", [P, TT, L0_E])
        top, tot = st.sb("top", [P, TT, 1]), st.sb("tot", [P, TT, 1])
        rank = st.sb("rank", [P, L0_E])
        gateT = st.sb("gateT", [L0_E, NT])
        logits = st.ps("logits", [P, TT, L0_E])
        turned = st.ps("turned", [L0_E, NT])
        wide = st.ps("wide", [P, 4, HALF])
        (own_dve, s_logits, s_shift, s_exp, s_gate, s_turned, s_copied, s_wide, loaded) = (st.sem(n) for n in (
            "own_dve", "logits", "shifted", "exp", "gate", "turned", "copied", "wide", "loaded"))
        s_moved = [st.sem("moved_by_dve"), st.sem("moved_by_act")]
        banks = [(g, h) for g in range(4) for h in range(2)]
        with nc.Block() as block:
            @block.sync
            def _(sp):
                sp.dma_start(rank[:, :], d["rank8"]).then_inc(loaded, 16)

            @block.tensor
            def _(pe):
                for j in range(TT):
                    for ct in range(CT):
                        last = pe.matmul(logits[:, j, :], m.hT[:, ct, j * P:(j + 1) * P], w_g[:, ct, :],
                                         start=ct == 0, stop=ct == CT - 1)
                last.then_inc(s_logits, 1)
                pe.wait_ge(s_gate, 1)
                for j in range(TT):
                    last = pe.transpose(turned[:, j * P:(j + 1) * P], ex[:, j, :], m.ident[:, :])
                last.then_inc(s_turned, 1)
                pe.wait_ge(s_copied, 1)
                for n, (g, h) in enumerate(banks):
                    if n >= 4:
                        pe.wait_ge(s_moved[n % 2], (n - 4) // 2 + 1)
                    pe.matmul(wide[:, n % 4, :], select[:, g, :], gateT[:, h * HALF:(h + 1) * HALF],
                              start=True, stop=True).then_inc(s_wide, 1)

            @block.scalar
            def _(act):
                act.wait_ge(s_shift, 1)
                act.activation(ex[:, :, :], lg[:, :, :], ACT.Exp).then_inc(s_exp, 1)
                for n, (g, h) in enumerate(banks):
                    if n % 2:
                        act.wait_ge(s_wide, n + 1)
                        act.activation(gates[:, g, h * HALF:(h + 1) * HALF], wide[:, n % 4, :], ACT.Copy).then_inc(s_moved[1], 1)

            @block.vector
            def _(dve):
                own = Tally(dve, own_dve)
                dve.wait_ge(s_logits, 1)
                own.link(dve.tensor_reduce(top[:, :, :], logits[:, :, :], AX.X, ALU.max))
                dve.tensor_tensor(lg[:, :, :], logits[:, :, :], top[:, :, :].broadcast_to([P, TT, L0_E]),
                                  ALU.subtract).then_inc(s_shift, 1)
                dve.wait_ge(s_exp, 1)
                own.link(dve.tensor_reduce(tot[:, :, :], ex[:, :, :], AX.X, ALU.add))
                own.link(dve.reciprocal(tot[:, :, :], tot[:, :, :]))
                own.link(dve.tensor_scalar(tot[:, :, :], tot[:, :, :], 64.0 / 16.0, None, ALU.mult))
                dve.wait_ge(loaded, 16)
                own.link(dve.tensor_scalar(ex[:, :, :], lg[:, :, :], 0.0, None, ALU.is_equal))
                own.link(dve.tensor_tensor(ex[:, :, :], ex[:, :, :], rank[:, :].unsqueeze(1).broadcast_to([P, TT, L0_E]), ALU.mult))
                own.link(dve.tensor_reduce(top[:, :, :], ex[:, :, :], AX.X, ALU.max))
                own.link(dve.tensor_tensor(ex[:, :, :], ex[:, :, :], top[:, :, :].broadcast_to([P, TT, L0_E]), ALU.is_equal))
                dve.tensor_tensor(ex[:, :, :], ex[:, :, :], tot[:, :, :].broadcast_to([P, TT, L0_E]), ALU.mult).then_inc(s_gate, 1)
                dve.wait_ge(s_turned, 1)
                dve.tensor_copy(gateT[:, :], turned[:, :]).then_inc(s_copied, 1)
                for n, (g, h) in enumerate(banks):
                    if n % 2 == 0:
                        dve.wait_ge(s_wide, n + 1)
                        dve.tensor_copy(gates[:, g, h * HALF:(h + 1) * HALF], wide[:, n % 4, :]).then_inc(s_moved[0], 1)


def gated_inner(nc, m, name, w_a, gates, inner):
    with Stage(nc, name) as st:
        acc = st.ps("acc", [P, 4, HALF])
        s_sum, s_kept = st.sem("sum"), st.sem("kept")
        banks = [(g, h) for g in range(4) for h in range(2)]
        with nc.Block() as block:
            @block.tensor
            def _(pe):
                for n, (g, h) in enumerate(banks):
                    if n >= 4:
                        pe.wait_ge(s_kept, n - 3)
                    for ct in range(CT):
                        last = pe.matmul(acc[:, n % 4, :], w_a[:, ct, g * P:(g + 1) * P],
                                         m.hT[:, ct, h * HALF:(h + 1) * HALF], start=ct == 0, stop=ct == CT - 1)
                    last.then_inc(s_sum, 1)

            @block.vector
            def _(dve):
                for n, (g, h) in enumerate(banks):
                    t = slice(h * HALF, (h + 1) * HALF)
                    dve.wait_ge(s_sum, n + 1)
                    dve.tensor_tensor(inner[:, g, t], acc[:, n % 4, :], gates[:, g, t], ALU.mult).then_inc(s_kept, 1)



L1_CHUNKS = NH * P // HALF


def attention_wide_heads(nc, m, d, name, w_q, w_k, w_v, w_o):
    scale = 128 ** -0.5
    with Stage(nc, name) as st:
        hd = Heads(st, True)
        xb = st.sb("xb", [P, CT, T])
        qk = [st.sb("q", [P, NH, T]), st.sb("k", [P, NH, T])]
        v = st.sb("v", [P, 2, NH * P])
        oT = qk[0]
        cos, sin = st.sb("cos", [P, T]), st.sb("sin", [P, T])
        straight, crossed = st.sb("straight", [P, 2, HALF]), st.sb("crossed", [P, 2, HALF])
        rtot = st.sb("rtot", [P, NH, 2])
        prj = st.ps("prj", [P, 2, HALF])
        out = st.ps("out", [P, 2, HALF])
        own_dve, own_act, loaded, s_xb, s_prj, s_rot, s_turned_pos, s_vkept, s_exp, s_okept, s_sum, s_added = (
            st.sem(n) for n in ("own_dve", "own_act", "loaded", "xb_ready", "prj_ready", "rotated_parts", "rotated",
                                "v_kept", "exp_ready", "o_kept", "sum", "added"))
        NR = NH
        NV = 2 * L1_CHUNKS
        with nc.Block() as block:
            @block.sync
            def _(sp):
                sp.dma_start(cos[:, :], d["l1_cos"]).then_inc(loaded, 16)
                sp.dma_start(sin[:, :], d["l1_sin"]).then_inc(loaded, 16)

            @block.tensor
            def _(pe):
                def batch(b, first):
                    turn = b * NH
                    pe.wait_ge(s_xb, b + 1)
                    for n in range(NR):
                        if n >= 2:
                            pe.wait_ge(s_rot, b * NR + n - 1)
                        elif not first:
                            pe.wait_ge(s_vkept, b * NV - 1 + n)
                        w = w_q if n < NR // 2 else w_k
                        for half in range(2):
                            h = 2 * (n % (NR // 2)) + half
                            for ct in range(CT):
                                last = pe.matmul(prj[:, n % 2, half * T:(half + 1) * T], w[:, ct, h * P:(h + 1) * P],
                                                 xb[:, ct], start=ct == 0, stop=ct == CT - 1)
                        last.then_inc(s_prj, 1)
                    for n in range(NV):
                        if n < 2:
                            pe.wait_ge(s_rot, b * NR + NR - 1 + n)
                        else:
                            pe.wait_ge(s_vkept, b * NV + n - 1)
                        mt, c = n // L1_CHUNKS, n % L1_CHUNKS
                        for ct in range(CT):
                            last = pe.matmul(prj[:, n % 2, :], xb[:, ct, mt * P:(mt + 1) * P],
                                             w_v[:, ct, c * HALF:(c + 1) * HALF], start=ct == 0, stop=ct == CT - 1)
                        last.then_inc(s_prj, 1)
                    pe.wait_ge(s_turned_pos, (b + 1) * NR)
                    pe.wait_ge(s_vkept, (b + 1) * NV)

                    def weigh(h):
                        pe.wait_ge(hd.s_moved[h % 2], turn // 2 + h // 2 + 1)
                        if h >= 2:
                            pe.wait_ge(s_okept, turn + h - 1)
                        elif not first:
                            pe.wait_ge(s_added, b)
                        for nt in range(2):
                            mine = [(i, mt) for i, (n_, mt) in enumerate(hd.blocks) if n_ == nt]
                            for i, mt in mine:
                                last = pe.matmul(out[:, h % 2, nt * P:(nt + 1) * P], v[:, mt, h * P:(h + 1) * P],
                                                 hd.probsT[:, h % 2, i * P:(i + 1) * P],
                                                 start=i == mine[0][0], stop=i == mine[-1][0])
                        last.then_inc(hd.s_out, 1)
                    for i in range(NH + 2):
                        if i < NH:
                            hd.score(pe, turn, i, qk[0][:, i, :], qk[1][:, i, :], m.ident_b[:, :], m.mask_window)
                        if 1 <= i <= NH:
                            hd.turn(pe, turn, i - 1, m.ident[:, :])
                        if i >= 2:
                            weigh(i - 2)
                    pe.wait_ge(s_okept, turn + NH)
                    for o in range(CT):
                        for h in range(NH):
                            last = pe.matmul(out[:, o, 0:T], w_o[:, h, o * P:(o + 1) * P], oT[:, h, :],
                                             start=h == 0, stop=h == NH - 1)
                    last.then_inc(s_sum, 1)
                batch(0, True)
                with pe.Fori(1, B, 1) as b:
                    batch(b, False)

            @block.scalar
            def _(act):
                def copy(o, i):
                    return act.activation(o, i, ACT.Copy)

                def batch(b, first):
                    turn = b * NH
                    for n in range(NV):
                        mt, c = n // L1_CHUNKS, n % L1_CHUNKS
                        act.wait_ge(s_prj, b * (NR + NV) + NR + n + 1)
                        copy(v[:, mt, c * HALF:(c + 1) * HALF], prj[:, n % 2, :]).then_inc(s_vkept, 1)
                    for i in range(NH + 2):
                        if i < NH:
                            hd.exp(act, turn, i, scale, s_exp)
                        if 1 <= i <= NH and (i - 1) % 2:
                            hd.move(act, copy, turn, i - 1)
                        if i >= 2:
                            act.wait_ge(hd.s_out, turn + i - 1)
                            copy(oT[:, i - 2, :], out[:, i % 2, 0:T]).then_inc(s_okept, 1)
                batch(0, True)
                with act.Fori(1, B, 1) as b:
                    batch(b, False)

            @block.gpsimd
            def _(pool):
                with pool.Fori(0, B, 1) as b:
                    for n in range(NR):
                        pool.wait_ge(s_rot, b * NR + n + 1)
                        h = 2 * (n % (NR // 2))
                        pool.tensor_tensor(qk[n // (NR // 2)][:, h:h + 2, :], straight[:, n % 2, :].rearrange("p (h t) -> p h t", h=2),
                                           crossed[:, n % 2, :].rearrange("p (h t) -> p h t", h=2), ALU.add).then_inc(s_turned_pos, 1)

            @block.vector
            def _(dve):
                own = Tally(dve, own_dve)
                dve.wait_ge(loaded, 32)

                def copy(o, i):
                    return dve.tensor_copy(o, i)

                def batch(b, first):
                    turn = b * NH
                    dve.tensor_copy(xb[:, :, :], m.hT[:, :, bass.ds(b * T, T)]).then_inc(s_xb, 1)
                    for n in range(NR):
                        dve.wait_ge(s_prj, b * (NR + NV) + n + 1)
                        if n >= 2 or not first:
                            dve.wait_ge(s_turned_pos, b * NR + n - 1)
                        x = prj[:, n % 2, :].rearrange("p (h t) -> p h t", h=2)
                        cr = crossed[:, n % 2, :].rearrange("p (h t) -> p h t", h=2)
                        dve.tensor_tensor(straight[:, n % 2, :].rearrange("p (h t) -> p h t", h=2), x,
                                          cos[:, :].unsqueeze(1).broadcast_to([P, 2, T]), ALU.mult)
                        for src, dst in ((slice(64, P), slice(0, 64)), (slice(0, 64), slice(64, P))):
                            last = dve.tensor_tensor(cr[dst], x[src], sin[src, :].unsqueeze(1).broadcast_to([64, 2, T]), ALU.mult)
                        last.then_inc(s_rot, 1)

                    def normalise(h):
                        dve.wait_ge(s_exp, turn + h + 1)
                        own.link(dve.reciprocal(rtot[:, h, :], hd.total[:, h, :]))
                        for nt, cols in hd.tiles():
                            last = dve.tensor_scalar(hd.probs[:, h % 2, cols], hd.probs[:, h % 2, cols], rtot[:, h, nt:nt + 1],
                                                     None, ALU.mult)
                        last.then_inc(hd.s_norm, 1)
                    for i in range(NH + 1):
                        if i < NH:
                            hd.top_of(dve, own, turn, i, scale)
                            normalise(i)
                        if i >= 1 and (i - 1) % 2 == 0:
                            hd.move(dve, copy, turn, i - 1)
                    dve.wait_ge(s_sum, b + 1)
                    for o in range(CT):
                        t = bass.ds(b * T, T)
                        last = dve.tensor_tensor(m.xT[:, o, t], m.xT[:, o, t], out[:, o, 0:T], ALU.add)
                    last.then_inc(s_added, 1)
                batch(0, True)
                with dve.Fori(1, B, 1) as b:
                    own.enter(b - 1, 2 * NH)
                    batch(b, False)
                own.leave(B - 1)



E, GROUPS_E = 64, 8
GE = E // GROUPS_E
TOP_GROUPS = 4
ROUTED_SCALE = 2.5


class Routing:

    def __init__(self, st, K):
        self.K = K
        self.put = st.sb("slot_put", [P, TT, K], U32)
        self.get = st.sb("slot_get", [P, TT, K], U32)
        self.gate = st.sb("gate", [P, TT, K])


def route(nc, m, d, name, w_g, bias, r, cap, fill):
    K = r.K
    with Stage(nc, name) as st:
        score, biased, masked = (st.sb(n, [P, TT, E]) for n in ("score", "biased", "masked"))
        hi, lo, hi2, lo2, mid = (st.sb(n, [P, TT * GROUPS_E, 4]) for n in ("hi", "lo", "hi2", "lo2", "mid"))
        gsum, gin, pen = (st.sb(n, [P, TT, GROUPS_E]) for n in ("gsum", "gin", "pen"))
        best, idx, idxf = st.sb("best", [P, TT, 8]), st.sb("idx", [P, TT, 8], U32), st.sb("idxf", [P, TT, 8])
        geq = st.sb("geq", [P, TT, TOP_GROUPS, GROUPS_E])
        chosen, prod = st.sb("chosen", [P, TT, K, E]), st.sb("prod", [P, TT, K, E])
        sel = st.sb("sel", [P, TT, E], BF16)
        pos, wk, keep, slot, tmp = (st.sb(n, [P, TT, K]) for n in ("pos", "wk", "keep", "slot", "tmp"))
        wsum = st.sb("wsum", [P, TT, 1])
        logits, before = st.ps("logits", [P, TT, E]), st.ps("before", [P, TT, E])
        own_dve, s_logits, s_score, s_sel, s_before = (st.sem(n) for n in ("own_dve", "logits", "score", "sel", "before"))
        with nc.Block() as block:
            @block.tensor
            def _(pe):
                for j in range(TT):
                    for ct in range(CT):
                        last = pe.matmul(logits[:, j, :], m.hT[:, ct, j * P:(j + 1) * P], w_g[:, ct, :],
                                         start=ct == 0, stop=ct == CT - 1)
                last.then_inc(s_logits, 1)
                pe.wait_ge(s_sel, 1)
                pe.matmul(before[:, :, :], m.earlier[:, :], sel[:, :, :], start=True, stop=False)
                for j in range(TT - 1):
                    last = pe.matmul(before[:, j + 1:, :], m.ones_b[:, :], sel[:, j:j + 1, :].broadcast_to([P, TT - 1 - j, E]),
                                     start=False, stop=j == TT - 2)
                last.then_inc(s_before, 1)

            @block.scalar
            def _(act):
                act.wait_ge(s_logits, 1)
                act.activation(score[:, :, :], logits[:, :, :], ACT.Sigmoid).then_inc(s_score, 1)

            @block.vector
            def _(dve):
                own = Tally(dve, own_dve)

                def both(o, a, b, op):
                    own.link(dve.tensor_tensor(o, a, b, op))
                dve.wait_ge(s_score, 1)
                both(biased[:, :, :], score[:, :, :], bias[:, :].unsqueeze(1).broadcast_to([P, TT, E]), ALU.add)
                v = biased[:, :, :].rearrange("p t (g e) -> p (t g) e", e=GE)
                both(hi[:, :, :], v[:, :, 0:4], v[:, :, 4:8], ALU.max)
                both(lo[:, :, :], v[:, :, 0:4], v[:, :, 4:8], ALU.min)
                h, l, h_, l_ = hi, lo, hi2, lo2
                for n in (2, 1):
                    both(mid[:, :, 0:n], h[:, :, 0:n], h[:, :, n:2 * n], ALU.min)
                    both(h_[:, :, 0:n], h[:, :, 0:n], h[:, :, n:2 * n], ALU.max)
                    both(l_[:, :, 0:n], l[:, :, 0:n], l[:, :, n:2 * n], ALU.max)
                    both(l_[:, :, 0:n], l_[:, :, 0:n], mid[:, :, 0:n], ALU.max)
                    h, l, h_, l_ = h_, l_, h, l
                both(gsum[:, :, :], h[:, :, 0:1].rearrange("p (t g) o -> p t (g o)", g=GROUPS_E),
                     l[:, :, 0:1].rearrange("p (t g) o -> p t (g o)", g=GROUPS_E), ALU.add)
                for j in range(TT):
                    last = dve.max(best[:, j, :], gsum[:, j, :])
                own.link(last)
                for j in range(TT):
                    last = dve.max_index(idx[:, j, :], best[:, j, :], gsum[:, j, :])
                own.link(last)
                own.link(dve.tensor_copy(idxf[:, :, :], idx[:, :, :]))
                both(geq[:, :, :, :], m.iota[:, 0:GROUPS_E].unsqueeze(1).unsqueeze(1).broadcast_to([P, TT, TOP_GROUPS, GROUPS_E]),
                     idxf[:, :, 0:TOP_GROUPS].unsqueeze(3).broadcast_to([P, TT, TOP_GROUPS, GROUPS_E]), ALU.is_equal)
                own.link(dve.tensor_reduce(gin[:, :, :], geq[:, :, :, :].rearrange("p t k g -> p t g k"), AX.X, ALU.add))
                own.link(dve.tensor_scalar(pen[:, :, :], gin[:, :, :], -fill, fill, ALU.mult, ALU.add))
                mk = masked[:, :, :].rearrange("p t (g e) -> p (t g) e", e=GE)
                both(mk, v, gin[:, :, :].rearrange("p t g -> p (t g)").unsqueeze(2).broadcast_to([P, TT * GROUPS_E, GE]), ALU.mult)
                both(mk, mk, pen[:, :, :].rearrange("p t g -> p (t g)").unsqueeze(2).broadcast_to([P, TT * GROUPS_E, GE]), ALU.add)
                for j in range(TT):
                    last = dve.max(best[:, j, :], masked[:, j, :])
                own.link(last)
                for j in range(TT):
                    last = dve.max_index(idx[:, j, :], best[:, j, :], masked[:, j, :])
                own.link(last)
                own.link(dve.tensor_copy(idxf[:, :, :], idx[:, :, :]))
                full = [P, TT, K, E]
                both(chosen[:, :, :, :], m.iota[:, :].unsqueeze(1).unsqueeze(1).broadcast_to(full),
                     idxf[:, :, 0:K].unsqueeze(3).broadcast_to(full), ALU.is_equal)
                dve.tensor_reduce(sel[:, :, :], chosen[:, :, :, :].rearrange("p t k e -> p t e k"), AX.X, ALU.max).then_inc(s_sel, 1)
                both(prod[:, :, :, :], chosen[:, :, :, :], score[:, :, :].unsqueeze(2).broadcast_to(full), ALU.mult)
                own.link(dve.tensor_reduce(wk[:, :, :], prod[:, :, :, :], AX.X, ALU.add))
                dve.wait_ge(s_before, 1)
                both(prod[:, :, :, :], chosen[:, :, :, :], before[:, :, :].unsqueeze(2).broadcast_to(full), ALU.mult)
                own.link(dve.tensor_reduce(pos[:, :, :], prod[:, :, :, :], AX.X, ALU.add))
                own.link(dve.tensor_scalar(keep[:, :, :], pos[:, :, :], float(cap), None, ALU.is_lt))
                own.link(dve.scalar_tensor_tensor(out=slot[:, :, :], in0=idxf[:, :, 0:K], scalar=float(cap), in1=pos[:, :, :],
                                                  op0=ALU.mult, op1=ALU.add))
                own.link(dve.tensor_scalar(tmp[:, :, :], keep[:, :, :], -1048576.0, 1048576.0, ALU.mult, ALU.add))
                both(tmp[:, :, :], tmp[:, :, :], slot[:, :, :], ALU.add)
                own.link(dve.tensor_copy(r.put[:, :, :], tmp[:, :, :]))
                both(slot[:, :, :], slot[:, :, :], keep[:, :, :], ALU.mult)
                dve.tensor_copy(r.get[:, :, :], slot[:, :, :])
                own.link(dve.tensor_reduce(wsum[:, :, :], wk[:, :, :], AX.X, ALU.add))
                own.link(dve.tensor_scalar(wsum[:, :, :], wsum[:, :, :], 1e-20, None, ALU.add))
                own.link(dve.reciprocal(wsum[:, :, :], wsum[:, :, :]))
                both(wk[:, :, :], wk[:, :, :], wsum[:, :, :].broadcast_to([P, TT, K]), ALU.mult)
                dve.scalar_tensor_tensor(out=r.gate[:, :, :], in0=wk[:, :, :], scalar=ROUTED_SCALE, in1=keep[:, :, :],
                                         op0=ALU.mult, op1=ALU.mult)


def dispatch(nc, m, name, r, slots_in, w_up, w_gate, inner, rows_i):
    n_slots = slots_in.shape[0]
    tiles = w_up.shape[2] // rows_i
    with Stage(nc, name) as st:
        acc = st.ps("acc", [P, 4, HALF])
        side = st.sb("side", [P, 2, HALF])
        scattered, s_sum, s_act, s_kept = (st.sem(n) for n in ("scattered", "sum", "activated", "kept"))
        banks = [(i, h) for i in range(tiles) for h in range(NT // HALF)]
        with nc.Block() as block:
            @block.gpsimd
            def _(pool):
                for j in range(TT):
                    for k in range(r.K):
                        pool.indirect_dma_start(slots_in, bass.IndirectOffsetOnAxis(ap=r.put[:, j, k:k + 1], axis=0),
                                                m.tok[:, j, :], None, bounds_check=n_slots - 1,
                                                oob_is_err=False).then_inc(scattered, 16)
                pool.wait_ge(scattered, 16 * TT * r.K)

            @block.tensor
            def _(pe):
                for n, (i, h) in enumerate(banks):
                    if n >= 2:
                        pe.wait_ge(s_kept, n - 1)
                    for g, w in enumerate((w_up, w_gate)):
                        for ct in range(CT if w is not None else 0):
                            last = pe.matmul(acc[0:rows_i, 2 * (n % 2) + g, :], w[:, ct, i * rows_i:(i + 1) * rows_i],
                                             m.hT[:, ct, h * HALF:(h + 1) * HALF], start=ct == 0, stop=ct == CT - 1)
                    last.then_inc(s_sum, 1)

            @block.scalar
            def _(act):
                for n in range(len(banks)):
                    act.wait_ge(s_sum, n + 1)
                    if n >= 2:
                        act.wait_ge(s_kept, n - 1)
                    if w_gate is None:
                        ins = act.activation(side[0:rows_i, n % 2, :], acc[0:rows_i, 2 * (n % 2), :], ACT.Relu)
                    else:
                        ins = act.activation(side[0:rows_i, n % 2, :], acc[0:rows_i, 2 * (n % 2) + 1, :], ACT.Silu)
                    ins.then_inc(s_act, 1)

            @block.vector
            def _(dve):
                for n, (i, h) in enumerate(banks):
                    dve.wait_ge(s_act, n + 1)
                    other = side[0:rows_i, n % 2, :] if w_gate is None else acc[0:rows_i, 2 * (n % 2), :]
                    dve.tensor_tensor(inner[0:rows_i, i, h * HALF:(h + 1) * HALF], side[0:rows_i, n % 2, :], other,
                                      ALU.mult).then_inc(s_kept, 1)


RING = 4


def experts(nc, m, name, slots_in, slots_out, weights, per, rows_i, gated):
    units = slots_in.shape[0] // P
    cap = P // per
    n_in = 2 if gated else 1
    with Stage(nc, name) as st:
        xs = st.sb("xs", [P, RING, C])
        wi = [st.sb(f"wi{g}", [P, RING, per, CT, rows_i]) for g in range(n_in)]
        wo = st.sb("wo", [P, RING, per, C])
        xsT = st.sb("xsT", [P, 2, CT, P])
        half = st.sb("half", [P, 2, P])
        inner = st.sb("inner", [P, 2, P])
        y = st.sb("y", [P, 2, C])
        xs_t, up, ys = st.ps("xs_t", [P, 2, HALF]), st.ps("up", [P, 2, HALF]), st.ps("ys", [P, 2, HALF])
        loaded = [st.sem(f"loaded{i}") for i in range(RING)]
        stored = [st.sem(f"stored{i}") for i in range(2)]
        s_turned, s_copied, s_up, s_half, s_inner, s_ys, s_kept = (
            st.sem(n) for n in ("turned", "copied", "up", "half", "inner", "ys", "kept"))
        n_loads = 2 + n_in

        def pipeline(eng, steps, depth):
            for i in range(RING):
                steps(i, i)
            with eng.Fori(1, units // RING, 1) as it:
                for c in range(RING):
                    steps(it * RING + c, RING + c)
            for i in range(units, units + depth):
                steps(i, i)
        with nc.Block() as block:
            @block.sync
            def _(sp):
                def load_unit(u, r, seen):
                    if seen >= RING:
                        sp.wait_ge(s_ys, u - RING + 1)
                    sp.dma_start(xs[:, r, :], slots_in[bass.ds(u * P, P), :]).then_inc(loaded[r], 16)
                    for g in range(n_in):
                        sp.dma_start(wi[g][:, r], weights[g][bass.ds(u, 1)]).then_inc(loaded[r], 16)
                    sp.dma_start(wo[0:rows_i, r], weights[-1][bass.ds(u, 1)]).then_inc(loaded[r], 16)

                def store_unit(u, r):
                    sp.wait_ge(s_kept, u + 1)
                    sp.dma_start(slots_out[bass.ds(u * P, P), :], y[:, r % 2, :]).then_inc(stored[r % 2], 16)

                for u in range(RING):
                    load_unit(u, u, u)
                with sp.Fori(1, units // RING, 1) as it:
                    for c in range(RING):
                        store_unit(it * RING + c - RING, c)
                        load_unit(it * RING + c, c, RING)
                for c in range(RING):
                    store_unit(units - RING + c, c)
                for s in stored:
                    sp.wait_ge(s, 16 * units // 2)

            @block.tensor
            def _(pe):
                def steps(i, seen):
                    c = seen % RING
                    if isinstance(i, int) and i >= units:
                        pass
                    else:
                        pe.wait_ge(loaded[c], 16 * n_loads * (i // RING + 1) if isinstance(i, int) else 16 * n_loads * (i // RING + 1))
                        if seen >= 2:
                            pe.wait_ge(s_copied, i - 1)
                        for ct in range(CT):
                            last = pe.transpose(xs_t[:, c % 2, ct * P:(ct + 1) * P], xs[:, c, ct * P:(ct + 1) * P], m.ident[:, :])
                        last.then_inc(s_turned, 1)
                    if seen >= 1 and not (isinstance(i, int) and i - 1 >= units):
                        r = (c - 1) % RING
                        pe.wait_ge(s_copied, i)
                        if seen >= 3:
                            pe.wait_ge(s_inner, i - 2)
                        for e in range(per):
                            for g in range(n_in):
                                for ct in range(CT):
                                    last = pe.matmul(up[0:rows_i, r % 2, g * P + e * cap:g * P + (e + 1) * cap], wi[g][:, r, e, ct],
                                                     xsT[:, r % 2, ct, e * cap:(e + 1) * cap], start=ct == 0, stop=ct == CT - 1)
                        last.then_inc(s_up, 1)
                    if seen >= 2:
                        r = (c - 2) % RING
                        pe.wait_ge(s_inner, i - 1)
                        if seen >= 4:
                            pe.wait_ge(s_kept, i - 3)
                        for e in range(per):
                            last = pe.matmul(ys[e * cap:(e + 1) * cap, r % 2, 0:C], inner[0:rows_i, r % 2, e * cap:(e + 1) * cap],
                                             wo[0:rows_i, r, e, :], start=True, stop=True)
                        last.then_inc(s_ys, 1)
                pipeline(pe, steps, 2)

            @block.scalar
            def _(act):
                def steps(i, seen):
                    c = seen % RING
                    if not (isinstance(i, int) and i >= units):
                        act.wait_ge(s_turned, i + 1)
                        if seen >= 2:
                            act.wait_ge(s_up, i - 1)
                        act.activation(xsT[:, c % 2].rearrange("p a b -> p (a b)"), xs_t[:, c % 2, 0:C], ACT.Copy).then_inc(s_copied, 1)
                    if seen >= 1:
                        r = (c - 1) % RING
                        act.wait_ge(s_up, i)
                        if seen >= 3:
                            act.wait_ge(s_inner, i - 2)
                        if gated:
                            ins = act.activation(half[0:rows_i, r % 2, :], up[0:rows_i, r % 2, P:2 * P], ACT.Silu)
                        else:
                            ins = act.activation(half[0:rows_i, r % 2, :], up[0:rows_i, r % 2, 0:P], ACT.Relu)
                        ins.then_inc(s_half, 1)
                pipeline(act, steps, 1)

            @block.vector
            def _(dve):
                def steps(i, seen):
                    c = seen % RING
                    if seen >= 1 and not (isinstance(i, int) and i - 1 >= units):
                        r = (c - 1) % RING
                        dve.wait_ge(s_half, i)
                        if seen >= 3:
                            dve.wait_ge(s_ys, i - 2)
                        other = up[0:rows_i, r % 2, 0:P] if gated else half[0:rows_i, r % 2, :]
                        dve.tensor_tensor(inner[0:rows_i, r % 2, :], half[0:rows_i, r % 2, :], other, ALU.mult).then_inc(s_inner, 1)
                    if seen >= 2:
                        r = (c - 2) % RING
                        dve.wait_ge(s_ys, i - 1)
                        if seen >= 4:
                            dve.wait_ge(stored[r % 2], 16 * ((i - 2) // 2))
                        dve.tensor_copy(y[:, r % 2, :], ys[:, r % 2, 0:C]).then_inc(s_kept, 1)
                pipeline(dve, steps, 2)


def combine(nc, m, name, r, slots_out):
    GATHERS = 8
    with Stage(nc, name) as st:
        got = st.sb("got", [P, TT, C])
        turned = st.ps("turned", [P, CT, NT])
        gathered = [st.sem(f"gathered{j}") for j in range(TT)]
        s_added, s_turned = st.sem("added"), st.sem("turned")
        with nc.Block() as block:
            @block.gpsimd
            def _(pool):
                def gather(k, first):
                    for j in range(TT):
                        if not first:
                            pool.wait_ge(s_added, (k - 1) * TT + j + 1)
                        pool.indirect_dma_start(got[:, j, :], None, slots_out,
                                                bass.IndirectOffsetOnAxis(ap=r.get[:, j, k:k + 1], axis=0)
                                                ).then_inc(gathered[j], 16)
                for k in range(r.K):
                    gather(k, k == 0)

            @block.vector
            def _(dve):
                def add(k, first):
                    for j in range(TT):
                        dve.wait_ge(gathered[j], 16 * (k + 1))
                        if first:
                            dve.tensor_scalar(m.tok[:, j, :], got[:, j, :], r.gate[:, j, 0:1], None, ALU.mult).then_inc(s_added, 1)
                        else:
                            dve.wait_ge(s_added, (k - 1) * TT + j + 1)
                            dve.scalar_tensor_tensor(out=m.tok[:, j, :], in0=got[:, j, :], scalar=r.gate[:, j, bass.ds(k, 1)],
                                                     in1=m.tok[:, j, :], op0=ALU.mult, op1=ALU.add).then_inc(s_added, 1)
                add(0, True)
                with dve.Fori(1, r.K, 1) as k:
                    add(k, False)
                for h in range(2):
                    dve.wait_ge(s_turned, h + 1)
                    t = slice(h * HALF, (h + 1) * HALF)
                    for ct in range(CT):
                        dve.tensor_tensor(m.xT[:, ct, t], m.xT[:, ct, t], turned[:, ct, t], ALU.add)

            @block.tensor
            def _(pe):
                for j in range(TT):
                    pe.wait_ge(s_added, (r.K - 1) * TT + j + 1)
                    for ct in range(CT):
                        last = pe.transpose(turned[:, ct, j * P:(j + 1) * P], m.tok[:, j, ct * P:(ct + 1) * P], m.ident[:, :])
                    if j % (TT // 2) == TT // 2 - 1:
                        last.then_inc(s_turned, 1)



L2_H, L2_D = 32, 8
L2_HALF = TT // B


def qkv_tokens(nc, m, name, w, bias, qkv):
    cols = [slice(0, HALF), slice(HALF, 3 * C)]
    with Stage(nc, name) as st:
        acc = st.ps("acc", [P, 4, HALF])
        s_sum, s_kept = st.sem("sum"), st.sem("kept")
        banks = [(j, c) for j in range(TT) for c in cols]
        with nc.Block() as block:
            @block.tensor
            def _(pe):
                for n, (j, c) in enumerate(banks):
                    if n >= 4:
                        pe.wait_ge(s_kept, n - 3)
                    for ct in range(CT):
                        last = pe.matmul(acc[:, n % 4, 0:c.stop - c.start], m.hT[:, ct, j * P:(j + 1) * P], w[:, ct, c],
                                         start=ct == 0, stop=ct == CT - 1)
                    last.then_inc(s_sum, 1)

            @block.vector
            def _(dve):
                for n, (j, c) in enumerate(banks):
                    dve.wait_ge(s_sum, n + 1)
                    dve.tensor_tensor(qkv[:, j, c], acc[:, n % 4, 0:c.stop - c.start], bias[:, c], ALU.add).then_inc(s_kept, 1)


def attention_over_batch(nc, m, d, name, qkv):
    X = L2_HALF * L2_H
    scale = float(np.float32(1) / np.sqrt(np.float32(L2_D)))
    with Stage(nc, name) as st:
        cos, sin = st.sb("cos", [P, B, L2_D]), st.sb("sin", [P, B, L2_D])
        straight, crossed = st.sb("straight", [P, TT, 2 * C]), st.sb("crossed", [P, TT, 2 * C])
        vc = st.sb("vc", [P, TT, C])
        prod = st.sb("prod", [P, 2, B * L2_HALF * C])
        score, top, tot = st.sb("score", [P, B, B, X]), st.sb("top", [P, B, X]), st.sb("tot", [P, B, X])
        (loaded, own_dve, s_straight, s_crossed, s_rot, s_cleared, s_v, s_prod, s_red, s_shift, s_exp, s_norm, s_wprod,
         s_wred) = (st.sem(n) for n in ("loaded", "own_dve", "straight", "crossed", "rotated", "cleared", "v", "prod",
                                        "reduced", "shifted", "exp", "norm", "weighted", "summed"))
        x = qkv[:, :, 0:2 * C].rearrange("p t (h e) -> p t h e", e=L2_D)

        def heads(t):
            return t[:, :, :].rearrange("p t (h e) -> p t h e", e=L2_D)

        def table(t, b, part):
            n = part.stop - part.start
            return t[:, b, part].unsqueeze(1).unsqueeze(1).broadcast_to([P, L2_HALF, 2 * L2_H, n])
        lo, hi, both = slice(0, L2_D // 2), slice(L2_D // 2, L2_D), slice(0, L2_D)
        order = list(range(B))
        with nc.Block() as block:
            @block.sync
            def _(sp):
                sp.dma_start(cos[:, :, :], d["l2_cos"]).then_inc(loaded, 16)
                sp.dma_start(sin[:, :, :], d["l2_sin"]).then_inc(loaded, 16)

            @block.gpsimd
            def _(pool):
                pool.memset(score[:, :, :, :], MASKED).then_inc(s_cleared, 1)
                pool.wait_ge(loaded, 32)
                for b in range(B):
                    j = slice(b * L2_HALF, (b + 1) * L2_HALF)
                    for dst, src in ((lo, hi), (hi, lo)):
                        last = pool.tensor_tensor(heads(crossed)[:, j, :, dst], x[:, j, :, src], table(sin, b, dst), ALU.mult)
                    last.then_inc(s_crossed, 1)
                pool.tensor_copy(vc[:, :, :], qkv[:, :, 2 * C:3 * C]).then_inc(s_v, 1)
                for s in order:
                    pool.wait_ge(s_rot, B)
                    if s >= 2:
                        pool.wait_ge(s_red, s - 1)
                    o = prod[:, s % 2, 0:(s + 1) * L2_HALF * C].rearrange("p (k t c) -> p k t c", t=L2_HALF, c=C)
                    q = straight[:, s * L2_HALF:(s + 1) * L2_HALF, 0:C].unsqueeze(1).broadcast_to([P, s + 1, L2_HALF, C])
                    k = straight[:, 0:(s + 1) * L2_HALF, C:2 * C].rearrange("p (k t) c -> p k t c", t=L2_HALF)
                    pool.tensor_tensor(o, q, k, ALU.mult).then_inc(s_prod, 1)
                pool.wait_ge(s_v, 1)
                pool.wait_ge(s_norm, 1)
                for s in order:
                    if s < 2:
                        pool.wait_ge(s_red, B)
                    else:
                        pool.wait_ge(s_wred, s - 1)
                    o = prod[:, s % 2, 0:(s + 1) * L2_HALF * C].rearrange("p (k x e) -> p k x e", x=X, e=L2_D)
                    v = vc[:, 0:(s + 1) * L2_HALF, :].rearrange("p (k t) (h e) -> p k (t h) e", t=L2_HALF, e=L2_D)
                    p = score[:, s, 0:s + 1, :].unsqueeze(3).broadcast_to([P, s + 1, X, L2_D])
                    pool.tensor_tensor(o, v, p, ALU.mult).then_inc(s_wprod, 1)

            @block.scalar
            def _(act):
                act.wait_ge(s_shift, 1)
                act.activation(score[:, :, :, :], score[:, :, :, :], ACT.Exp, scale=scale).then_inc(s_exp, 1)

            @block.vector
            def _(dve):
                own = Tally(dve, own_dve)
                dve.wait_ge(loaded, 32)
                for b in range(B):
                    j = slice(b * L2_HALF, (b + 1) * L2_HALF)
                    dve.tensor_tensor(heads(straight)[:, j], x[:, j], table(cos, b, both), ALU.mult).then_inc(s_straight, 1)
                for b in range(B):
                    j = slice(b * L2_HALF, (b + 1) * L2_HALF)
                    dve.wait_ge(s_straight, b + 1)
                    dve.wait_ge(s_crossed, b + 1)
                    dve.tensor_tensor(straight[:, j, :], straight[:, j, :], crossed[:, j, :], ALU.add).then_inc(s_rot, 1)
                dve.wait_ge(s_cleared, 1)
                for s in order:
                    dve.wait_ge(s_prod, s + 1)
                    src = prod[:, s % 2, 0:(s + 1) * L2_HALF * C].rearrange("p (k x e) -> p k x e", x=X, e=L2_D)
                    dve.tensor_reduce(score[:, s, 0:s + 1, :], src, AX.X, ALU.add).then_inc(s_red, 1)
                dve.wait_ge(s_red, B)
                own.link(dve.tensor_reduce(top[:, :, :], score[:, :, :, :].rearrange("p s k x -> p s x k"), AX.X, ALU.max))
                full = [P, B, B, X]
                dve.tensor_tensor(score[:, :, :, :], score[:, :, :, :], top[:, :, :].unsqueeze(2).broadcast_to(full),
                                  ALU.subtract).then_inc(s_shift, 1)
                dve.wait_ge(s_exp, 1)
                own.link(dve.tensor_reduce(tot[:, :, :], score[:, :, :, :].rearrange("p s k x -> p s x k"), AX.X, ALU.add))
                own.link(dve.reciprocal(tot[:, :, :], tot[:, :, :]))
                dve.tensor_tensor(score[:, :, :, :], score[:, :, :, :], tot[:, :, :].unsqueeze(2).broadcast_to(full),
                                  ALU.mult).then_inc(s_norm, 1)
                for s in order:
                    dve.wait_ge(s_wprod, s + 1)
                    src = prod[:, s % 2, 0:(s + 1) * L2_HALF * C].rearrange("p (k x) -> p x k", x=L2_HALF * C)
                    out = m.tok[:, s * L2_HALF:(s + 1) * L2_HALF, :].rearrange("p t c -> p (t c)")
                    dve.tensor_reduce(out, src, AX.X, ALU.add).then_inc(s_wred, 1)


def turn_tokens(nc, m, name):
    with Stage(nc, name) as st:
        tp = st.ps("tp", [P, CT, NT])
        s_turned = st.sem("turned")
        with nc.Block() as block:
            @block.tensor
            def _(pe):
                for h in range(NT // HALF):
                    for ct in range(CT):
                        for j in range(h * HALF // P, (h + 1) * HALF // P):
                            last = pe.transpose(tp[:, ct, j * P:(j + 1) * P], m.tok[:, j, ct * P:(ct + 1) * P], m.ident[:, :])
                        last.then_inc(s_turned, 1)

            @block.vector
            def _(dve):
                for h in range(NT // HALF):
                    t = slice(h * HALF, (h + 1) * HALF)
                    dve.wait_ge(s_turned, 2 * h + 1)
                    dve.tensor_copy(m.hT[:, 0, t], tp[:, 0, t])

            @block.scalar
            def _(act):
                for h in range(NT // HALF):
                    t = slice(h * HALF, (h + 1) * HALF)
                    act.wait_ge(s_turned, 2 * h + 2)
                    act.activation(m.hT[:, 1, t], tp[:, 1, t], ACT.Copy)



def low_rank(nc, m, name, w, low):
    with Stage(nc, name) as st:
        acc = st.ps("acc", [16, NT])
        s_sum = st.sem("sum")
        with nc.Block() as block:
            @block.tensor
            def _(pe):
                for h in range(NT // HALF):
                    t = slice(h * HALF, (h + 1) * HALF)
                    for ct in range(CT):
                        last = pe.matmul(acc[:, t], w[:, ct, :], m.hT[:, ct, t], start=ct == 0, stop=ct == CT - 1)
                last.then_inc(s_sum, 1)

            @block.vector
            def _(dve):
                dve.wait_ge(s_sum, 1)
                dve.tensor_scalar(low[:, :], acc[:, :], 0.5, None, ALU.mult)


L3_I = 1024


def swiglu_rms(nc, m, name, w_gate, w_up, ln, h):
    with Stage(nc, name) as st:
        gate, up = st.ps("gate", [P, 2, HALF]), st.ps("up", [P, 2, HALF])
        act_out = st.sb("act_out", [P, 2, HALF])
        square = st.sb("square", [P, L3_I])
        ssum, rms, rinv = st.sb("ssum", [P, TT]), st.sb("rms", [P, TT]), st.sb("rinv", [P, TT])
        own_dve, s_sum, s_act, s_h, s_sq, s_var, s_rms = (st.sem(n) for n in ("own_dve", "sum", "act", "h", "sq", "var", "rms"))
        banks = [(j, c) for j in range(TT) for c in range(L3_I // HALF)]
        with nc.Block() as block:
            @block.tensor
            def _(pe):
                for n, (j, c) in enumerate(banks):
                    if n >= 2:
                        pe.wait_ge(s_h, n - 1)
                    for into, w in ((gate, w_gate), (up, w_up)):
                        for ct in range(CT):
                            last = pe.matmul(into[:, n % 2, :], m.hT[:, ct, j * P:(j + 1) * P], w[:, ct, c * HALF:(c + 1) * HALF],
                                             start=ct == 0, stop=ct == CT - 1)
                    last.then_inc(s_sum, 1)

            @block.scalar
            def _(act):
                for n, (j, c) in enumerate(banks):
                    act.wait_ge(s_sum, n + 1)
                    if n >= 2:
                        act.wait_ge(s_h, n - 1)
                    act.activation(act_out[:, n % 2, :], gate[:, n % 2, :], ACT.Silu).then_inc(s_act, 1)
                act.wait_ge(s_var, 1)
                act.activation(rms[:, :], rinv[:, :], ACT.Sqrt).then_inc(s_rms, 1)

            @block.vector
            def _(dve):
                own = Tally(dve, own_dve)
                for n, (j, c) in enumerate(banks):
                    dve.wait_ge(s_act, n + 1)
                    dve.tensor_tensor(h[:, j, c * HALF:(c + 1) * HALF], act_out[:, n % 2, :], up[:, n % 2, :], ALU.mult).then_inc(s_h, 1)
                for j in range(TT):
                    dve.wait_ge(s_h, 2 * j + 2)
                    own.link(dve.tensor_tensor_reduce(square[:, :], h[:, j, :], h[:, j, :], 1.0, 0.0, ALU.mult, ALU.add, ssum[:, j:j + 1]))
                dve.tensor_scalar(rinv[:, :], ssum[:, :], 1.0 / L3_I, 1e-6, ALU.mult, ALU.add).then_inc(s_var, 1)
                dve.wait_ge(s_rms, 1)
                own.link(dve.reciprocal(rinv[:, :], rms[:, :]))
                for j in range(TT):
                    dve.scalar_tensor_tensor(out=h[:, j, :], in0=h[:, j, :], scalar=rinv[:, j:j + 1], in1=ln[:, :],
                                             op0=ALU.mult, op1=ALU.mult)


def build(nc, m, d, out, stop=8):
    ctx = ExitStack()
    with ctx:
        def sb(name, shape, dt=F32):
            return ctx.enter_context(nc.sbuf_tensor(name, shape, dt))
        m.xT, m.hT = sb("xT", [P, CT, NT]), sb("hT", [P, CT, NT])
        m.tok = sb("tok", [P, TT, C])
        m.gain = sb("gain", [P, CONDS, CT, NT])
        m.ident, m.ones = sb("ident", [P, P]), sb("ones", [P, P])
        m.ident_b = sb("ident_b", [P, P], BF16)
        m.mask_causal, m.mask_window = sb("mask_causal", [P, 3 * P], BF16), sb("mask_window", [P, 3 * P], BF16)
        m.ones_b, m.earlier, m.iota = sb("ones_b", [P, P], BF16), sb("earlier", [P, P], BF16), sb("iota", [P, E])
        m.wu, m.condT = sb("wu", [P, 2, 2 * CONDS, CT]), sb("condT", [64, B])
        m.slots_in_1 = nc.dram_tensor("slots_in_1", (64 * 64, C), F32).ap()
        m.slots_in_2 = nc.dram_tensor("slots_in_2", (64 * 128, C), F32).ap()
        m.slots_out_1 = nc.dram_tensor("slots_out_1", (64 * 64, C), F32).ap()
        m.slots_out_2 = nc.dram_tensor("slots_out_2", (64 * 128, C), F32).ap()
        load_constants(nc, m, d)
        condition_gains(nc, m, d, "gains01", 0)
        layer0(nc, m, d, stop)
        layer1(nc, m, d, stop)
        if stop >= 5:
            condition_gains(nc, m, d, "gains23", CONDS)
            layer2(nc, m, d, stop)
        if stop >= 7:
            layer3(nc, m, d, stop)
        with Stage(nc, "end") as st:
            stored = st.sem("stored")
            with nc.Block() as block:
                @block.sync
                def _(sp):
                    sp.dma_start(out, m.xT[:]).then_inc(stored, 16)
                    sp.wait_ge(stored, 16)


def layer0(nc, m, d, stop):
    with ExitStack() as ctx:
        w_qk = ctx.enter_context(nc.sbuf_tensor("l0_w_qk", [P, CT, 2 * GROUPS * P], F32))
        w_v = ctx.enter_context(nc.sbuf_tensor("l0_w_v", [P, CT, C], F32))
        w_o = ctx.enter_context(nc.sbuf_tensor("l0_w_o", [P, CT, C], F32))
        load(nc, "l0_load", [(w_qk[:], d["l0_w_qk"]), (w_v[:], d["l0_w_v"]), (w_o[:], d["l0_w_o"])])
        quantize_weights(nc, m, "l0_ternary", [([w_qk[:], w_v[:]], 3 * C * C), ([w_o[:]], C * C)])
        apply_condition(nc, m, "l0_cond", 0, tok=True)
        quantize_tokens(nc, m, "l0_quant", m.tok, m.hT, C)
        attention_small_heads(nc, m, d, "l0_attn", m.hT, w_qk, w_v, True, 16 ** -0.5)
        quantize_tokens(nc, m, "l0_quant2", m.tok, m.hT, C)
        add_product(nc, m, "l0_out", w_o, m.hT)
    if stop < 2:
        return
    with Stage(nc, "l0f") as st:
        w_g, w_a, w_b = st.sb("w_g", [P, CT, L0_E]), st.sb("w_a", [P, CT, L0_E * L0_R]), st.sb("w_b", [P, 4, C])
        select = st.sb("select", [L0_E, 4, P])
        gates, inner = st.sb("gates", [P, 4, NT]), st.sb("inner", [P, 4, NT])
        load(nc, "l0_load2", [(w_g[:], d["l0_w_g"]), (w_a[:], d["l0_w_a"]), (w_b[:], d["l0_w_b"]), (select[:], d["l0_select"])])
        apply_condition(nc, m, "l0_cond2", 1)
        argmax_gates(nc, m, d, "l0_gates", w_g, select, gates)
        gated_inner(nc, m, "l0_inner", w_a, gates, inner)
        add_product(nc, m, "l0_down", w_b, inner)


L1_SH = 512


def layer1(nc, m, d, stop):
    if stop < 3:
        return
    with Stage(nc, "l1a") as st:
        w_q, w_k, w_v = (st.sb(n, [P, CT, NH * P]) for n in ("w_q", "w_k", "w_v"))
        w_o = st.sb("w_o", [P, NH, C])
        load(nc, "l1_load", [(w_q[:], d["l1_w_q"]), (w_k[:], d["l1_w_k"]), (w_v[:], d["l1_w_v"]), (w_o[:], d["l1_w_o"])])
        apply_condition(nc, m, "l1_cond", 2)
        attention_wide_heads(nc, m, d, "l1_attn", w_q, w_k, w_v, w_o)
    if stop < 4:
        return
    with Stage(nc, "l1f") as st:
        w_g, bias = st.sb("w_g", [P, CT, E]), st.sb("bias", [P, E])
        w_su, w_sd = st.sb("w_su", [P, CT, L1_SH]), st.sb("w_sd", [P, L1_SH // P, C])
        inner = st.sb("inner", [P, L1_SH // P, NT])
        r = Routing(st, 6)
        load(nc, "l1_load2", [(w_g[:], d["l1_w_g"]), (bias[:], d["l1_bias"]), (w_su[:], d["l1_w_su"]), (w_sd[:], d["l1_w_sd"])])
        apply_condition(nc, m, "l1_cond2", 3, tok=True)
        route(nc, m, d, "l1_route", w_g, bias, r, 64, MASKED)
        dispatch(nc, m, "l1_dispatch", r, m.slots_in_1, w_su, None, inner, P)
        add_product(nc, m, "l1_shared", w_sd, inner)
        experts(nc, m, "l1_experts", m.slots_in_1, m.slots_out_1, [d["l1_w_1"], d["l1_w_2"]], 2, P, False)
        combine(nc, m, "l1_combine", r, m.slots_out_1)


L2_I = 88


def layer2(nc, m, d, stop):
    with Stage(nc, "l2a") as st:
        w, bias, w_o, b_o = st.sb("w", [P, CT, 3 * C]), st.sb("bias", [P, 3 * C]), st.sb("w_o", [P, CT, C]), st.sb("b_o", [P, CT])
        qkv = st.sb("qkv", [P, TT, 3 * C])
        load(nc, "l2_load", [(w[:], d["l2_w"]), (bias[:], d["l2_bias"]), (w_o[:], d["l2_w_o"]), (b_o[:], d["l2_b_o"])])
        apply_condition(nc, m, "l2_cond", 0)
        qkv_tokens(nc, m, "l2_qkv", w, bias, qkv)
        attention_over_batch(nc, m, d, "l2_attn", qkv)
        turn_tokens(nc, m, "l2_turn")
        add_product(nc, m, "l2_out", w_o, m.hT, bias=b_o)
    if stop < 6:
        return
    with Stage(nc, "l2f") as st:
        w_g, bias = st.sb("w_g", [P, CT, E]), st.sb("bias", [P, E])
        w_sg, w_su = st.sb("w_sg", [P, CT, L2_I]), st.sb("w_su", [P, CT, L2_I])
        w_sd, inner = st.sb("w_sd", [L2_I, 1, C]), st.sb("inner", [L2_I, 1, NT])
        r = Routing(st, 8)
        load(nc, "l2_load2", [(w_g[:], d["l2_w_g"]), (bias[:], d["l2_ebias"]), (w_sg[:], d["l2_w_sg"]), (w_su[:], d["l2_w_su"]),
                              (w_sd[:], d["l2_w_sd"])])
        apply_condition(nc, m, "l2_cond2", 1, tok=True)
        route(nc, m, d, "l2_route", w_g, bias, r, 128, 0.0)
        dispatch(nc, m, "l2_dispatch", r, m.slots_in_2, w_su, w_sg, inner, L2_I)
        add_product(nc, m, "l2_shared", w_sd, inner)
        experts(nc, m, "l2_experts", m.slots_in_2, m.slots_out_2, [d["l2_w_up"], d["l2_w_gate"], d["l2_w_down"]], 1, L2_I, True)
        combine(nc, m, "l2_combine", r, m.slots_out_2)


def layer3(nc, m, d, stop):
    with Stage(nc, "l3a") as st:
        w_qk, w_v, w_o = st.sb("w_qk", [P, CT, 2 * GROUPS * P]), st.sb("w_v", [P, CT, C]), st.sb("w_o", [P, CT, C])
        low, up_qk, up_v = st.sb("low", [P, CT, P]), st.sb("up_qk", [P, GROUPS * P]), st.sb("up_v", [P, C])
        qk_bias, b_o = st.sb("qk_bias", [P, 2 * GROUPS]), st.sb("b_o", [P, CT])
        low_o, up_o, low_out = st.sb("low_o", [P, CT, 16]), st.sb("up_o", [16, C]), st.sb("low_out", [16, NT])
        m.low_bias = st.sb("low_bias", [P, 1])
        load(nc, "l3_load", [(t[:], d["l3_" + n]) for t, n in (
            (w_qk, "w_qk"), (w_v, "w_v"), (w_o, "w_o"), (low, "low"), (up_qk, "up_qk"), (up_v, "up_v"), (qk_bias, "qk_bias"),
            (b_o, "b_o"), (low_o, "low_o"), (up_o, "up_o"), (m.low_bias, "low_bias"))])
        apply_condition(nc, m, "l3_cond", 2)
        attention_small_heads(nc, m, d, "l3_attn", m.hT, w_qk, w_v, False, 16 ** -0.5, qk_bias, (low, up_qk, up_v))
        turn_tokens(nc, m, "l3_turn")
        low_rank(nc, m, "l3_low", low_o, low_out)
        add_product(nc, m, "l3_out", w_o, m.hT, bias=b_o, low=(up_o, low_out))
    if stop < 8:
        return
    with Stage(nc, "l3f") as st:
        w_g, w_u, w_d = st.sb("w_g", [P, CT, L3_I]), st.sb("w_u", [P, CT, L3_I]), st.sb("w_d", [P, L3_I // P, C])
        ln = st.sb("ln", [P, L3_I])
        h, hq = st.sb("h", [P, TT, L3_I]), st.sb("hq", [P, L3_I // P, NT])
        load(nc, "l3_load2", [(w_g[:], d["l3_w_g"]), (w_u[:], d["l3_w_u"]), (w_d[:], d["l3_w_d"]), (ln[:], d["l3_ln"])])
        quantize_weights(nc, m, "l3_ternary", [([w[:]], L3_I * C) for w in (w_g, w_u, w_d)])
        apply_condition(nc, m, "l3_cond2", 3, tok=True)
        quantize_tokens(nc, m, "l3_quant", m.tok, m.hT, C)
        swiglu_rms(nc, m, "l3_swiglu", w_g, w_u, ln, h)
        quantize_tokens(nc, m, "l3_quant2", h, hq, L3_I)
        add_product(nc, m, "l3_down", w_d, hq)



def rows(a):
    a = np.asarray(a)
    return np.ascontiguousarray(a.reshape(-1, P, a.shape[-1]).transpose(1, 0, 2))


def spread_heads(wT):
    a = np.zeros((wT.shape[0], NH, 32), wT.dtype)
    a[:, :, :16] = wT.reshape(-1, NH, 16)
    return a.reshape(wT.shape[0], -1)


def at_rows(*blocks):
    a = np.zeros((P, blocks[0][1].shape[1]), np.float32)
    for r, b in blocks:
        a[r:r + b.shape[0]] = b
    return a


def layouts(i):
    conds = [f"L{l}_cond{n}_" for l in range(4) for n in ("", "2")]
    i = {k: np.asarray(v) for k, v in i.items()}
    qkv = i["L0_attn_w_qkv"].T
    row, col = np.arange(P)[:, None], np.arange(P)[None, :]
    bf16 = np.dtype("bfloat16")
    freq = (np.float32(1) / np.float32(10000) ** (np.arange(0, P, 2, dtype=np.float32) / np.float32(P))).astype(np.float32)
    angle = np.tile((np.arange(T, dtype=np.float32)[:, None] * freq).T, (2, 1))
    freq2 = (np.float32(1) / np.float32(10000) ** (np.arange(0, L2_D, 2, dtype=np.float32) / np.float32(L2_D))).astype(np.float32)
    angle2 = np.tile(np.arange(B, dtype=np.float32)[:, None] * freq2, (1, 2))
    causal, window = np.where(col <= row, 0, MASKED), np.where(col > row, 0, MASKED)
    return {
        "xT": rows(i["x"].reshape(NT, C).T),
        "fsideT": rows(i["fside_BxSxS_0"].reshape(NT, C).T),
        "condT": np.ascontiguousarray(i["cond_512"].T),
        "wu": np.ascontiguousarray(np.stack([np.stack([i[c + k].reshape(CT, P).T for c in conds], 1) for k in "wu"], 1)),
        "ident": np.eye(P, dtype=np.float32), "ones": np.ones((P, P), np.float32),
        "ident_b": np.eye(P).astype(bf16),
        "mask_causal": np.concatenate([causal, 0 * causal, causal], 1).astype(bf16),
        "mask_window": np.concatenate([causal, window, causal], 1).astype(bf16),
        "l0_w_qk": rows(np.concatenate([spread_heads(qkv[:, :C]), spread_heads(qkv[:, C:2 * C])], 1)),
        "l0_w_v": rows(qkv[:, 2 * C:]),
        "l0_w_o": rows(i["L0_attn_w_proj"].T),
        "rank8": np.broadcast_to(np.arange(L0_E, 0, -1, dtype=np.float32), (P, L0_E)).copy(),
        "l0_w_g": rows(i["L0_ffn_Wg"].T),
        "l0_w_a": rows(i["L0_ffn_A"].reshape(L0_E * L0_R, C).T),
        "l0_w_b": rows(i["L0_ffn_Bw"].transpose(0, 2, 1).reshape(L0_E * L0_R, C)),
        "l0_select": (np.arange(L0_E)[:, None, None] == 2 * np.arange(4)[None, :, None] + np.arange(P)[None, None, :] // L0_R).astype(np.float32),
        "l1_w_q": rows(i["L1_attn_wq"]), "l1_w_k": rows(i["L1_attn_wk"]), "l1_w_v": rows(i["L1_attn_wv"]),
        "l1_w_o": rows(i["L1_attn_wo"]),
        "ones_b": np.ones((P, P), bf16), "earlier": (row < col).astype(bf16),
        "iota": np.broadcast_to(np.arange(E, dtype=np.float32), (P, E)).copy(),
        "l1_w_g": rows(i["L1_ffn_gate_w"].T), "l1_bias": np.broadcast_to(i["L1_ffn_e_bias"], (P, E)).copy(),
        "l1_w_su": rows(i["L1_ffn_shared_up_w"].T), "l1_w_sd": rows(i["L1_ffn_shared_down_w"].T),
        "l1_w_1": np.ascontiguousarray(i["L1_ffn_w1"].reshape(32, 2, P, CT, P).transpose(0, 4, 1, 3, 2)),
        "l1_w_2": np.ascontiguousarray(i["L1_ffn_w2"].reshape(32, 2, C, P).transpose(0, 3, 1, 2)),
        "l2_w": rows(i["L2_attn_qkv_w"]), "l2_bias": np.broadcast_to(i["L2_attn_qkv_b"], (P, 3 * C)).copy(),
        "l2_w_o": rows(i["L2_attn_out_w"]), "l2_b_o": np.ascontiguousarray(i["L2_attn_out_b"].reshape(CT, P).T),
        "l2_cos": np.broadcast_to(np.cos(angle2).astype(np.float32), (P, B, L2_D)).copy(),
        "l2_sin": np.broadcast_to((np.sin(angle2) * np.repeat([-1, 1], L2_D // 2)).astype(np.float32), (P, B, L2_D)).copy(),
        "l2_w_g": rows(i["L2_ffn_router_weight"].T), "l2_ebias": np.broadcast_to(i["L2_ffn_e_bias"], (P, E)).copy(),
        "l2_w_sg": rows(i["L2_ffn_sh_gate"]), "l2_w_su": rows(i["L2_ffn_sh_up"]), "l2_w_sd": i["L2_ffn_sh_down"][:, None, :],
        "l2_w_up": np.ascontiguousarray(i["L2_ffn_w_up"].reshape(E, CT, P, 1, L2_I).transpose(0, 2, 3, 1, 4)),
        "l2_w_gate": np.ascontiguousarray(i["L2_ffn_w_gate"].reshape(E, CT, P, 1, L2_I).transpose(0, 2, 3, 1, 4)),
        "l2_w_down": i["L2_ffn_w_down"][:, :, None, :],
        "l3_w_qk": rows(np.concatenate([spread_heads(i["L3_attn_Wq"].T), spread_heads(i["L3_attn_Wk"].T)], 1)),
        "l3_w_v": rows(i["L3_attn_Wv"].T), "l3_w_o": rows(i["L3_attn_Wo"].T),
        "l3_low": rows(np.concatenate([np.pad(i[f"L3_attn_B{k}"].T, ((0, 0), (0, 16))) for k in "qkv"] + [np.zeros((C, 32), np.float32)], 1)),
        "l3_up_qk": at_rows((0, spread_heads(i["L3_attn_Aq"].T)), (32, spread_heads(i["L3_attn_Ak"].T))),
        "l3_up_v": at_rows((64, i["L3_attn_Av"].T), (80, i["L3_attn_bv"][None])),
        "l3_qk_bias": np.concatenate([spread_heads(i[f"L3_attn_b{k}"][None]).reshape(GROUPS, P).T for k in "qk"], 1).copy(),
        "l3_b_o": np.ascontiguousarray(i["L3_attn_bo"].reshape(CT, P).T),
        "l3_low_o": rows(i["L3_attn_Bo"].T), "l3_up_o": np.ascontiguousarray(i["L3_attn_Ao"].T),
        "l3_low_bias": at_rows((80, np.ones((1, 1), np.float32))),
        "l3_w_g": rows(i["L3_ffn_w_gate"].T), "l3_w_u": rows(i["L3_ffn_w_up"].T), "l3_w_d": rows(i["L3_ffn_w_down"].T),
        "l3_ln": np.broadcast_to(i["L3_ffn_ln_weight"], (P, L3_I)).copy(),
        "l1_cos": np.cos(angle).astype(np.float32),
        "l1_sin": np.concatenate([np.sin(angle[:64]), -np.sin(angle[64:])]).astype(np.float32),
    }


def kernel(**inputs):
    import concourse.bacc as bacc
    from concourse.bass_utils import run_bass_kernel_spmd as run
    arrays = layouts(inputs)
    nc = bacc.Bacc("TRN2", target_bir_lowering=False, num_devices=1)
    d = {k: nc.dram_tensor("in_" + k, v.shape, mybir.dt.from_np(v.dtype), kind="ExternalInput").ap()
         for k, v in arrays.items()}
    out = nc.dram_tensor("out", (P, CT, NT), F32, kind="ExternalOutput").ap()
    build(nc, Core(), d, out)
    r = run(nc, [{"in_" + k: v for k, v in arrays.items()}], core_ids=[0])
    return np.ascontiguousarray(r.results[0]["out"].transpose(1, 0, 2).reshape(C, NT).T.reshape(B, T, C))
```

```python
import numpy as np
from contextlib import ExitStack

import concourse.bass as bass
from concourse import mybir

F32 = mybir.dt.float32
BF16 = mybir.dt.bfloat16
I32 = mybir.dt.int32
U32 = mybir.dt.uint32
ALU = mybir.AluOpType
ACT = mybir.ActivationFunctionType
AX = mybir.AxisListType

P = 128
B, T, C = 4, 256, 256
NT = B * T
CT = C // P
TT = NT // P
HALF = 512
NH = 16
HG = 4
GROUPS = NH // HG
CONDS = 4
ROUND = 1.5 * 2.0 ** 23
MASKED = -1e30


class Tally:

    def __init__(self, eng, sem):
        self.eng, self.sem, self.n, self.base = eng, sem, 0, None

    def value(self):
        return self.n if self.base is None else self.base + self.n

    def link(self, ins):
        ins.then_inc(self.sem, 1)
        self.n += 1
        self.eng.wait_ge(self.sem, self.value())

    def enter(self, turn, per):
        self.before, self.per, self.base, self.n = self.n, per, turn * per + self.n, 0

    def leave(self, turns):
        assert self.n == self.per, (self.n, self.per)
        self.base, self.n = None, self.before + turns * self.per


class Stage:

    def __init__(self, nc, name):
        self.nc, self.name, self.stack, self.sems = nc, name, ExitStack(), []

    def __enter__(self):
        return self

    def __exit__(self, *e):
        for s in self.sems:
            self.nc.sync.sem_clear(s)
        self.stack.close()

    def sb(self, name, shape, dt=F32):
        return self.stack.enter_context(self.nc.sbuf_tensor(f"{self.name}_{name}", shape, dt))

    def ps(self, name, shape, dt=F32):
        return self.stack.enter_context(self.nc.psum_tensor(f"{self.name}_{name}", shape, dt))

    def sem(self, name):
        self.sems.append(self.stack.enter_context(self.nc.semaphore(f"{self.name}_{name}")))
        return self.sems[-1]


class Core:
    pass



def load_constants(nc, m, d):
    with Stage(nc, "start") as st:
        loaded = st.sem("loaded")
        pairs = [(m.xT, "xT"), (m.ident, "ident"), (m.ones, "ones"), (m.wu, "wu"), (m.condT, "condT"),
             (m.ident_b, "ident_b"), (m.mask_causal, "mask_causal"), (m.mask_window, "mask_window"),
             (m.ones_b, "ones_b"), (m.earlier, "earlier"), (m.iota, "iota")]
        with nc.Block() as block:
            @block.sync
            def _(sp):
                for tile, name in pairs:
                    sp.dma_start(tile[:], d[name]).then_inc(loaded, 16)
                sp.wait_ge(loaded, 16 * len(pairs))


def condition_gains(nc, m, d, name, first):
    with Stage(nc, name) as st:
        if first == 0:
            zeros, zeroed, filled = st.sb("zeros", [P, 4096]), st.sem("zeroed"), st.sem("filled")
        kT, ek, ekv = (st.sb(n, [P, CT, NT]) for n in ("kT", "ek", "ekv"))
        dec, dw, dw2 = st.sb("dec", [P, CONDS, CT, B]), st.sb("dw", [P, CONDS, CT]), st.sb("dw2", [P, CONDS, CT])
        tf, dfac, ofac = st.sb("tf", [P, B]), st.sb("dfac", [P, B]), st.sb("ofac", [P, B])
        uk, euk, z, zv, rd = (st.sb(n, [P, 2, NT]) for n in ("uk", "euk", "z", "zv", "rd"))
        lnd, seed, corr = (st.sb(n, [P, 2, NT]) for n in ("lnd", "seed", "corr"))
        sc = st.sb("sc", [P, 2, 4, NT])
        num, den = st.ps("num", [P, 2, NT]), st.ps("den", [P, 2, NT])
        (loaded, own_dve, capped, ek_ready, ekv_ready, dw_ready, w_ready, tf_sum, tf_ready, uk_ready, euk_ready,
         z_ready, zv_ready, scans_ready, sums_ready, clamped, seeded, gain_ready, own_act) = (
            st.sem(n) for n in ("loaded", "own_dve", "capped", "ek", "ekv", "dw", "w", "tf_sum", "tf", "uk", "euk",
                                "z", "zv", "scans", "sums", "clamped", "seeded", "gain", "own_act"))
        w = m.wu[:, 0, first:first + CONDS, :]
        with nc.Block() as block:
            @block.sync
            def _(sp):
                sp.dma_start(kT[:], d["fsideT"]).then_inc(loaded, 16)
                if first == 0:
                    sp.wait_ge(zeroed, 1)
                    n = 0
                    for slots in (m.slots_in_1, m.slots_in_2):
                        flat = slots.rearrange("(p r) c -> p (r c)", p=P)
                        for c in range(0, flat.shape[1], zeros.shape[1]):
                            sp.dma_start(flat[:, c:c + zeros.shape[1]], zeros[:, :]).then_inc(filled, 16)
                            n += 1
                    sp.wait_ge(filled, 16 * n)

            @block.tensor
            def _(pe):
                nc.tensor.matmul(num[:, 0, 0:B], m.ones[0:64, :], m.condT[:, :], start=True, stop=True).then_inc(tf_sum, 1)
                pe.wait_ge(tf_ready, 1)

                def add_up(i, ct, early):
                    s = i * CT + ct
                    pe.wait_ge(scans_ready, s + 1)
                    pe.wait_ge(zv_ready, s + 1)
                    if not early:
                        pe.wait_ge(gain_ready, s - 1)
                    for acc, terms in ((num, (sc[:, ct, 0], sc[:, ct, 1], zv[:, ct])),
                                       (den, (sc[:, ct, 2], sc[:, ct, 3], z[:, ct]))):
                        for c in range(0, NT, HALF):
                            for n, t in enumerate(terms):
                                last = nc.tensor.matmul(acc[:, ct, c:c + HALF], m.ident[:, :], t[:, c:c + HALF],
                                                        start=n == 0, stop=n == 2)
                    last.then_inc(sums_ready, 1)
                add_up(0, 0, True)
                add_up(0, 1, True)
                with pe.Fori(1, CONDS, 1) as i:
                    add_up(i, 0, False)
                    add_up(i, 1, False)

            @block.scalar
            def _(act):
                nc.scalar.activation(dw[:, :, :], w, ACT.Exp).then_inc(dw_ready, 1)
                act.wait_ge(dw_ready, 1)
                nc.scalar.activation(dw2[:, :, :], dw[:, :, :], ACT.Exp, scale=-1.0).then_inc(w_ready, 1)
                act.wait_ge(tf_sum, 1)
                nc.scalar.activation(tf[:, :], num[:, 0, 0:B], ACT.Sigmoid).then_inc(tf_ready, 1)
                act.wait_ge(capped, 1)
                nc.scalar.activation(ek[:, :, :], ek[:, :, :], ACT.Exp).then_inc(ek_ready, 1)

                def exp_uk(i, ct, early):
                    s = i * CT + ct
                    act.wait_ge(uk_ready, s + 1)
                    if not early:
                        act.wait_ge(z_ready, s - 1)
                    nc.scalar.activation(euk[:, ct], uk[:, ct], ACT.Exp).then_inc(euk_ready, 1)

                def seed_inverse(i, ct):
                    s = i * CT + ct
                    act.wait_ge(clamped, s + 1)
                    nc.scalar.activation(lnd[:, ct], rd[:, ct], ACT.Ln).then_inc(own_act, 1)
                    act.wait_ge(own_act, s + 1)
                    nc.scalar.activation(seed[:, ct], lnd[:, ct], ACT.Exp, scale=-1.0).then_inc(seeded, 1)
                exp_uk(0, 0, True)
                exp_uk(0, 1, True)
                with act.Fori(1, CONDS, 1) as i:
                    seed_inverse(i - 1, 0)
                    exp_uk(i, 0, False)
                    seed_inverse(i - 1, 1)
                    exp_uk(i, 1, False)
                seed_inverse(CONDS - 1, 0)
                seed_inverse(CONDS - 1, 1)

            @block.gpsimd
            def _(pool):
                if first == 0:
                    nc.gpsimd.memset(zeros[:, :], 0.0).then_inc(zeroed, 1)
                pool.wait_ge(ek_ready, 1)
                nc.gpsimd.tensor_tensor(ekv[:, :, :], ek[:, :, :], kT[:, :, :], ALU.mult).then_inc(ekv_ready, 1)

                def own_token(i, ct, early):
                    s = i * CT + ct
                    pool.wait_ge(euk_ready, s + 1)
                    if not early:
                        pool.wait_ge(sums_ready, s - 1)
                    nc.gpsimd.tensor_tensor(z[:, ct], euk[:, ct], ek[:, ct], ALU.subtract).then_inc(z_ready, 1)
                    pool.wait_ge(z_ready, s + 1)
                    nc.gpsimd.tensor_tensor(zv[:, ct], z[:, ct], kT[:, ct], ALU.mult).then_inc(zv_ready, 1)
                own_token(0, 0, True)
                own_token(0, 1, True)
                with pool.Fori(1, CONDS, 1) as i:
                    own_token(i, 0, False)
                    own_token(i, 1, False)

            @block.vector
            def _(dve):
                own = Tally(dve, own_dve)
                dve.wait_ge(loaded, 16)
                nc.vector.tensor_scalar(ek[:, :, :], kT[:, :, :], 30.0, None, ALU.min).then_inc(capped, 1)
                dve.wait_ge(tf_ready, 1)
                nc.vector.tensor_scalar(ofac[:, :], tf[:, :], 0.2, 0.8, ALU.mult, ALU.add)
                own.link(nc.vector.tensor_scalar(dfac[:, :], tf[:, :], 0.5, 0.5, ALU.mult, ALU.add))
                dve.wait_ge(w_ready, 1)
                for b in range(B):
                    last = nc.vector.tensor_scalar(dec[:, :, :, b], dw2[:, :, :], dfac[:, b:b + 1], None, ALU.mult)
                own.link(last)
                dve.wait_ge(ekv_ready, 1)

                def scans(i, ct, early):
                    s = i * CT + ct
                    if not early:
                        dve.wait_ge(euk_ready, s - 1)
                    nc.vector.tensor_scalar(uk[:, ct], kT[:, ct], m.wu[:, 1, bass.ds(first + i, 1), ct], 30.0,
                                            ALU.add, ALU.min).then_inc(uk_ready, 1)
                    if not early:
                        dve.wait_ge(sums_ready, s - 1)
                    for b in range(B):
                        decay = dec[:, bass.ds(i, 1), ct, b].broadcast_to([P, T])
                        ahead = slice(b * T, b * T + T)
                        back = slice(b * T + T - 1, b * T - 1 if b else None, -1)
                        for n, src in enumerate((ekv, ek)):
                            nc.vector.tensor_tensor_scan(sc[:, ct, 2 * n, ahead], decay, src[:, ct, ahead], 0.0,
                                                         ALU.mult, ALU.add)
                            last = nc.vector.tensor_tensor_scan(sc[:, ct, 2 * n + 1, back], decay, src[:, ct, back],
                                                                0.0, ALU.mult, ALU.add)
                    last.then_inc(scans_ready, 1)

                def clamp(i, ct):
                    dve.wait_ge(sums_ready, i * CT + ct + 1)
                    nc.vector.tensor_scalar(rd[:, ct], den[:, ct], 1e-8, None, ALU.max).then_inc(clamped, 1)

                def gains(i, ct):
                    s = i * CT + ct
                    dve.wait_ge(seeded, s + 1)
                    own.link(nc.vector.tensor_tensor(corr[:, ct], rd[:, ct], seed[:, ct], ALU.mult))
                    own.link(nc.vector.scalar_tensor_tensor(out=corr[:, ct], in0=corr[:, ct], scalar=2.0, in1=seed[:, ct],
                                                            op0=ALU.subtract, op1=ALU.mult))
                    for b in range(B):
                        t = slice(b * T, b * T + T)
                        last = nc.vector.scalar_tensor_tensor(
                            out=m.gain[:, bass.ds(i, 1), ct, t], in0=num[:, ct, t], scalar=ofac[:, b:b + 1],
                            in1=corr[:, ct, t], op0=ALU.mult, op1=ALU.mult)
                    last.then_inc(gain_ready, 1)
                own.link(nc.vector.tensor_scalar(ofac[:, :], ofac[:, :], -1.0, None, ALU.mult))
                scans(0, 0, True)
                scans(0, 1, True)
                clamp(0, 0)
                with dve.Fori(1, CONDS, 1) as i:
                    own.enter(i - 1, 4)
                    scans(i, 0, False)
                    gains(i - 1, 0)
                    clamp(i - 1, 1)
                    scans(i, 1, False)
                    gains(i - 1, 1)
                    clamp(i, 0)
                own.leave(CONDS - 1)
                gains(CONDS - 1, 0)
                clamp(CONDS - 1, 1)
                gains(CONDS - 1, 1)


def apply_condition(nc, m, name, i, tok=False):
    with Stage(nc, name) as st:
        sig = st.sb("sig", [P, CT, NT])
        sig_ready, h_ready, turned = st.sem("sig"), st.sem("h"), st.sem("turned")
        tp = st.ps("tp", [P, TT, C]) if tok else None
        with nc.Block() as block:
            @block.scalar
            def _(act):
                for ct in range(CT):
                    nc.scalar.activation(sig[:, ct], m.xT[:, ct], ACT.Sigmoid).then_inc(sig_ready, 1)
                if tok:
                    for half in range(2):
                        act.wait_ge(turned, half + 1)
                        j = slice(half * TT // 2, (half + 1) * TT // 2)
                        nc.scalar.activation(m.tok[:, j, :], tp[:, j, :], ACT.Copy)

            @block.vector
            def _(dve):
                for ct in range(CT):
                    dve.wait_ge(sig_ready, ct + 1)
                    nc.vector.tensor_tensor(m.hT[:, ct], sig[:, ct], m.gain[:, i, ct], ALU.mult).then_inc(h_ready, 1)

            @block.tensor
            def _(pe):
                if tok:
                    pe.wait_ge(h_ready, CT)
                    for j in range(TT):
                        for ct in range(CT):
                            last = nc.tensor.transpose(tp[:, j, ct * P:(ct + 1) * P], m.hT[:, ct, j * P:(j + 1) * P],
                                                       m.ident[:, :])
                        if j % (TT // 2) == TT // 2 - 1:
                            last.then_inc(turned, 1)



def quantize_tokens(nc, m, name, tok, qT, feats):
    KT = feats // P
    per = HALF // P
    with Stage(nc, name) as st:
        amax, s = st.sb("amax", [P, TT]), st.sb("s", [P, TT])
        tp, row = st.ps("tp", [P, 4, HALF]), st.ps("row", [P, NT])
        own_dve, s_inv, s_row, quantized, turned = (st.sem(n) for n in ("own_dve", "inv", "row", "quantized", "turned"))
        moved = [st.sem("moved_by_dve"), st.sem("moved_by_act")]
        banks = [(k, h) for h in range(TT // per) for k in range(KT)]
        with nc.Block() as block:
            @block.vector
            def _(dve):
                own = Tally(dve, own_dve)
                own.link(nc.vector.tensor_reduce(amax[:, :], tok[:, :, :], AX.X, ALU.max, apply_absolute_value=True))
                own.link(nc.vector.tensor_scalar(amax[:, :], amax[:, :], 1e-5, None, ALU.max))
                nc.vector.tensor_scalar(m.inv[:, :], amax[:, :], 1.0 / 127.0, None, ALU.mult).then_inc(s_inv, 1)
                own.link(nc.vector.reciprocal(s[:, :], amax[:, :]))
                own.link(nc.vector.tensor_scalar(s[:, :], s[:, :], 127.0, None, ALU.mult))
                for j in range(TT):
                    nc.vector.tensor_scalar(tok[:, j, :], tok[:, j, :], s[:, j:j + 1], ROUND, ALU.mult,
                                            ALU.add).then_inc(quantized, 1)
                for n, (k, h) in enumerate(banks):
                    if n % 2 == 0:
                        dve.wait_ge(turned, n + 1)
                        nc.vector.tensor_scalar(qT[:, k, h * HALF:(h + 1) * HALF], tp[:, n % 4, :], ROUND, None,
                                                ALU.subtract).then_inc(moved[0], 1)

            @block.scalar
            def _(act):
                act.wait_ge(s_row, 1)
                nc.scalar.activation(m.inv_row[:, :], row[:, :], ACT.Copy)
                for n, (k, h) in enumerate(banks):
                    if n % 2:
                        act.wait_ge(turned, n + 1)
                        nc.scalar.activation(qT[:, k, h * HALF:(h + 1) * HALF], tp[:, n % 4, :], ACT.Copy,
                                             bias=-ROUND).then_inc(moved[1], 1)

            @block.tensor
            def _(pe):
                pe.wait_ge(s_inv, 1)
                for j in range(TT):
                    last = nc.tensor.matmul(row[:, j * P:(j + 1) * P], m.inv[:, j:j + 1].broadcast_to([P, P]), m.ident[:, :],
                                            start=True, stop=True)
                last.then_inc(s_row, 1)
                for n, (k, h) in enumerate(banks):
                    pe.wait_ge(quantized, (h + 1) * per)
                    if n >= 4:
                        pe.wait_ge(moved[n % 2], (n - 4) // 2 + 1)
                    for j in range(per):
                        last = nc.tensor.transpose(tp[:, n % 4, j * P:(j + 1) * P],
                                                   tok[:, h * per + j, k * P:(k + 1) * P], m.ident[:, :])
                    last.then_inc(turned, 1)


def quantize_weights(nc, m, name, groups, mean):
    with Stage(nc, name) as st:
        views = [(w, wq, g) for g, (ws, _) in enumerate(groups) for w, wq in ws]
        part = st.sb("part", [P, len(views)])
        s = st.sb("s", [P, len(groups)])
        total = st.ps("total", [P, len(groups)])
        own_dve, parts, summed = (st.sem(k) for k in ("own_dve", "parts", "summed"))
        with nc.Block() as block:
            @block.vector
            def _(dve):
                own = Tally(dve, own_dve)
                for i, (w, _, _) in enumerate(views):
                    last = dve.tensor_reduce(part[:, i:i + 1], w, AX.XY, ALU.add, apply_absolute_value=True)
                last.then_inc(parts, 1)
                dve.wait_ge(summed, 1)
                for g, (_, count) in enumerate(groups):
                    last = dve.tensor_scalar(mean[:, g:g + 1], total[:, g:g + 1], 1.0 / count, 1e-5, ALU.mult, ALU.max)
                own.link(last)
                own.link(dve.reciprocal(s[:, :], mean[:, :]))
                for step in range(3):
                    for w, wq, g in views:
                        if step == 0:
                            last = dve.tensor_scalar(w, w, s[:, g:g + 1], ROUND, ALU.mult, ALU.add)
                        elif step == 1:
                            last = dve.tensor_scalar(w, w, ROUND, 1.0, ALU.subtract, ALU.min)
                        else:
                            last = dve.tensor_scalar(wq, w, -1.0, None, ALU.max)
                    own.link(last)

            @block.tensor
            def _(pe):
                pe.wait_ge(parts, 1)
                for g in range(len(groups)):
                    mine = [i for i, (_, _, g_) in enumerate(views) if g_ == g]
                    for i in mine:
                        last = pe.matmul(total[:, g:g + 1], m.ones[:, :], part[:, i:i + 1], start=i == mine[0], stop=i == mine[-1])
                last.then_inc(summed, 1)


def load(nc, name, pairs):
    with Stage(nc, name) as st:
        loaded = st.sem("loaded")
        with nc.Block() as block:
            @block.sync
            def _(sp):
                for tile, src in pairs:
                    sp.dma_start(tile, src).then_inc(loaded, 16)
                sp.wait_ge(loaded, 16 * len(pairs))



IN_FLIGHT = 3
LAG = 2
WEIGH = 4


class Heads:

    def __init__(self, st, banks, causal):
        self.blocks = [(0, 0), (1, 0), (1, 1)] if causal else [(0, 0), (0, 1), (1, 0), (1, 1)]
        self.causal = causal
        self.split = P if causal else 2 * P
        self.width = len(self.blocks) * P
        self.turned, self.scores = banks[:, 0:2, :], banks[:, 2:2 + IN_FLIGHT, :]
        self.probs = st.sb("probs", [P, IN_FLIGHT, self.width])
        self.probsT = st.sb("probsT", [P, IN_FLIGHT, self.width])
        self.top = st.sb("top", [P, NH, 2])
        self.bias = st.sb("bias", [P, NH, 2])
        self.total = st.sb("total", [P, NH, 2])
        (self.s_scores, self.s_bias, self.s_turned, self.s_out, self.s_norm) = (
            st.sem(n) for n in ("scores_ready", "bias_ready", "turned_ready", "out_ready", "norm_ready"))
        self.s_moved = [st.sem("moved_by_dve"), st.sem("moved_by_act")]

    def tiles(self):
        return ((0, slice(0, self.split)), (1, slice(self.split, self.width)))

    def score(self, pe, turn, h, q, k, ident=None, mask=None):
        if h >= IN_FLIGHT:
            pe.wait_ge(self.s_norm, turn + h - IN_FLIGHT + 1)
        for nt, cols in self.tiles():
            into = self.scores[:, h % IN_FLIGHT, cols]
            if self.causal:
                pe.matmul(into, ident, mask[:, cols], start=True, stop=False)
            last = pe.matmul(into, q[:, nt * P:(nt + 1) * P], k[:, 0:cols.stop - cols.start],
                             start=not self.causal, stop=True)
        last.then_inc(self.s_scores, 1)

    def turn(self, pe, turn, h, ident):
        pe.wait_ge(self.s_norm, turn + h + 1)
        if h >= 2:
            pe.wait_ge(self.s_moved[h % 2], turn // 2 + (h - 2) // 2 + 1)
        for n in range(len(self.blocks)):
            last = pe.transpose(self.turned[:, h % 2, n * P:(n + 1) * P], self.probs[:, h % IN_FLIGHT, n * P:(n + 1) * P], ident)
        last.then_inc(self.s_turned, 1)

    def top_of(self, dve, own, turn, h, scale, scales=None):
        dve.wait_ge(self.s_scores, turn + h + 1)
        if self.causal:
            for nt, cols in self.tiles():
                last = dve.tensor_reduce(self.top[:, h, nt:nt + 1], self.scores[:, h % IN_FLIGHT, cols], AX.X, ALU.max)
            own.link(last)
        else:
            own.link(dve.tensor_reduce(self.top[:, h, :], self.scores[:, h % IN_FLIGHT, :].rearrange("p (n k) -> p n k", n=2),
                                       AX.X, ALU.max))
        if scales is None:
            dve.tensor_scalar(self.bias[:, h, :], self.top[:, h, :], -scale, None, ALU.mult).then_inc(self.s_bias, 1)
        else:
            dve.tensor_tensor(self.bias[:, h, :], self.top[:, h, :], scales, ALU.mult).then_inc(self.s_bias, 1)

    def move(self, eng, copy, turn, h):
        eng.wait_ge(self.s_turned, turn + h + 1)
        if h >= IN_FLIGHT:
            eng.wait_ge(self.s_out, turn + h - IN_FLIGHT + 1)
        copy(self.probsT[:, h % IN_FLIGHT, 0:self.width], self.turned[:, h % 2, 0:self.width]).then_inc(self.s_moved[h % 2], 1)

    def exp(self, act, turn, h, scale, ready, scales=None):
        act.wait_ge(self.s_bias, turn + h + 1)
        if h >= IN_FLIGHT:
            act.wait_ge(self.s_turned, turn + h - IN_FLIGHT + 1)
        for nt, cols in self.tiles():
            last = act.activation(self.probs[:, h % IN_FLIGHT, cols], self.scores[:, h % IN_FLIGHT, cols], ACT.Exp, bias=self.bias[:, h, nt:nt + 1],
                                  scale=scale if scales is None else scales[:, nt:nt + 1], accum_out=self.total[:, h, nt:nt + 1])
        last.then_inc(ready, 1)


def attention_small_heads(nc, m, d, name, x, w_qk, w_v, causal, scale, qk_bias=None, lora=None, mean=None):
    with Stage(nc, name) as st:
        banks = st.ps("banks", [P, 7, HALF])
        hd = Heads(st, banks, causal)
        xb = st.sb("xb", [P, CT, T], F32 if mean is None else BF16)
        q, k = st.sb("q", [P, NH, T]), st.sb("k", [P, GROUPS, T])
        v = st.sb("v", [P, 2, NH * 32])
        rtot = st.sb("rtot", [P, NH, 2])
        prj = banks[:, 5:7, :]
        outT = prj.rearrange("p n (g t) -> p (n g) t", t=T)
        kept_outT = st.sb("outT", [P, GROUPS, T])
        s_outT = [st.sem("outT_by_dve"), st.sem("outT_by_act")]
        s_back = st.sem("turned_back")
        own_dve, s_xb, s_prj, s_xfree = (st.sem(n) for n in ("own_dve", "xb_ready", "prj_ready", "x_free"))
        s_low, s_lowready, s_zeroed = st.sem("low_sum"), st.sem("low_ready"), st.sem("zeroed")
        s_kept = [st.sem("kept_even"), st.sem("kept_odd")]
        if mean is not None:
            factor, q_scale, q_minus, v_scale = (st.sb(n, [P, w]) for n, w in (
                ("factor", 1), ("q_scale", 2), ("q_minus", 2), ("v_scale", 2)))
        kept_by_act = (1, 3) if mean is None else (0, 1)
        NB = GROUPS + 1
        low = st.sb("low", [P, T]) if lora else None

        with nc.Block() as block:
            @block.gpsimd
            def _(pool):
                pool.memset(q[:, :, :], 0.0)
                pool.memset(v[:, :, :], 0.0).then_inc(s_zeroed, 1)

            @block.tensor
            def _(pe):
                def batch(b, first):
                    turn = b * NH
                    pe.wait_ge(s_xb, b + 1)
                    if lora:
                        for ct in range(CT):
                            last = pe.matmul(prj[:, 1, 0:T], lora[0][:, ct], xb[:, ct], start=ct == 0, stop=ct == CT - 1)
                        last.then_inc(s_low, 1)
                        pe.wait_ge(s_lowready, b + 1)
                    for n in range(NB):
                        if n >= 2:
                            pe.wait_ge(s_kept[n % 2], b * ((NB + 1 - n % 2) // 2) + (n - 2) // 2 + 1)
                        for half in range(2):
                            into = prj[:, n % 2, half * T:(half + 1) * T]
                            for ct in range(CT):
                                if n < GROUPS:
                                    g = 2 * n + half
                                    last = pe.matmul(into, w_qk[:, ct, g * P:(g + 1) * P], xb[:, ct],
                                                     start=ct == 0, stop=ct == CT - 1 and not lora)
                                else:
                                    last = pe.matmul(into, xb[:, ct, half * P:(half + 1) * P], w_v[:, ct],
                                                     start=ct == 0, stop=ct == CT - 1 and not lora)
                            if lora and n < GROUPS:
                                r = 32 * (g // GROUPS)
                                last = pe.matmul(into, lora[1][r:r + 16, (g % GROUPS) * P:(g % GROUPS + 1) * P],
                                                 low[r:r + 16, :], start=False, stop=True)
                            elif lora:
                                last = pe.matmul(into, low[64:64 + 17, half * P:(half + 1) * P], lora[2][64:64 + 17, :],
                                                 start=False, stop=True)
                        last.then_inc(s_prj, 1)
                    pe.wait_ge(s_kept[0], (b + 1) * ((NB + 1) // 2))
                    pe.wait_ge(s_kept[1], (b + 1) * (NB // 2))
                    if not first:
                        pe.wait_ge(s_xfree, b)

                    def weigh(h):
                        pe.wait_ge(hd.s_moved[h % 2], turn // 2 + h // 2 + 1)
                        into, probsT = outT[32 * (h % HG):32 * (h % HG) + 32, h // HG, :], hd.probsT[:, h % IN_FLIGHT, :]
                        v_h = [v[:, mt, h * 32:(h + 1) * 32] for mt in range(2)]
                        if causal:
                            pe.matmul(into[:, 0:P], v_h[0], probsT[:, 0:P], start=True, stop=True)
                            pe.matmul(into[:, P:T], v_h[0], probsT[:, P:T], start=True, stop=False)
                            last = pe.matmul(into[:, P:T], v_h[1], probsT[:, T:3 * P], start=False, stop=True)
                        else:
                            of = probsT.rearrange("p (n m q) -> p m n q", n=2, m=2)
                            pe.matmul(into.rearrange("p (n q) -> p n q", n=2), v_h[0], of[:, 0], start=True, stop=False)
                            last = pe.matmul(into.rearrange("p (n q) -> p n q", n=2), v_h[1], of[:, 1], start=False, stop=True)
                        last.then_inc(hd.s_out, 1)
                    for i in range(NH + WEIGH):
                        if i < NH:
                            hd.score(pe, turn, i, q[:, i, :], k[:, i // HG, :], m.ident_b[:, :], m.mask_causal)
                        if LAG <= i < NH + LAG:
                            hd.turn(pe, turn, i - LAG, m.ident[:, :])
                        if i >= WEIGH:
                            weigh(i - WEIGH)
                    for by in range(2):
                        pe.wait_ge(s_outT[by], b + 1)
                        pe.wait_ge(hd.s_moved[by], (turn + NH) // 2)
                    for nt in range(2):
                        for g in range(GROUPS):
                            last = pe.transpose(hd.turned[:, nt, g * P:(g + 1) * P], kept_outT[:, g, nt * P:(nt + 1) * P],
                                                m.ident[:, :])
                    last.then_inc(s_back, 1)
                batch(0, True)
                with pe.Fori(1, B, 1) as b:
                    batch(b, False)

            def keep(eng, copy, b, n):
                eng.wait_ge(s_prj, b * NB + n + 1)
                src = prj[:, n % 2, :].rearrange("p (g t) -> p g t", g=2)
                if n < GROUPS // 2:
                    for j in range(HG):
                        rows_j = slice(32 * j, 32 * j + 32)
                        if qk_bias is None:
                            last = copy(q[rows_j, 2 * n * HG:2 * (n + 1) * HG, :].rearrange("p (g h) t -> p h g t", g=2)[:, j],
                                        src[rows_j])
                            continue
                        for half in range(2):
                            g = 2 * n + half
                            into, bias = q[rows_j, g * HG + j, :], qk_bias[rows_j, g:g + 1]
                            last = eng.activation(into, src[rows_j, half], ACT.Identity, bias=bias) if n in kept_by_act else \
                                eng.tensor_scalar(into, src[rows_j, half], bias, None, ALU.add)
                    last.then_inc(s_kept[n % 2], 1)
                elif n < GROUPS:
                    for half in range(2):
                        g = 2 * n + half - GROUPS
                        if mean is not None:
                            last = eng.tensor_tensor(k[:, g, :], src[:, half], m.inv_row[:, bass.ds(b * T, T)], ALU.mult)
                        elif n in kept_by_act:
                            last = eng.activation(k[:, g, :], src[:, half], ACT.Identity, bias=qk_bias[:, GROUPS + g:GROUPS + g + 1])
                        else:
                            last = eng.tensor_scalar(k[:, g, :], src[:, half], qk_bias[:, GROUPS + g:GROUPS + g + 1], None, ALU.add)
                    last.then_inc(s_kept[n % 2], 1)
                else:
                    for mt in range(2):
                        into = v[:, mt, :].rearrange("p (h c) -> p h c", h=NH)[:, :, 0:16]
                        of = src[:, mt].rearrange("p (h c) -> p h c", h=NH)
                        last = copy(into, of) if mean is None else eng.tensor_scalar(into, of, v_scale[:, mt:mt + 1], None, ALU.mult)
                    last.then_inc(s_kept[n % 2], 1)

            @block.scalar
            def _(act):
                def copy(o, i):
                    return nc.scalar.activation(o, i, ACT.Copy)

                def batch(b, first):
                    turn = b * NH
                    if lora:
                        act.wait_ge(s_low, b + 1)
                        act.activation(low[:, :], prj[:, 1, 0:T], ACT.Identity, scale=0.5,
                                       bias=m.low_bias[:, 0:1]).then_inc(s_lowready, 1)
                    for n in kept_by_act:
                        keep(act, copy, b, n)
                    for i in range(NH + LAG):
                        if i < NH:
                            hd.exp(act, turn, i, scale, hd.s_norm, q_scale if mean is not None else None)
                        if i >= LAG and (i - LAG) % 2:
                            hd.move(act, copy, turn, i - LAG)
                    act.wait_ge(hd.s_out, turn + NH)
                    copy(kept_outT[:, 2:4, :], outT[:, 2:4, :]).then_inc(s_outT[1], 1)
                act.wait_ge(s_zeroed, 1)
                batch(0, True)
                with act.Fori(1, B, 1) as b:
                    batch(b, False)

            @block.vector
            def _(dve):
                own = Tally(dve, own_dve)
                dve.wait_ge(s_zeroed, 1)
                if mean is not None:
                    own.link(dve.tensor_scalar(factor[:, :], mean, mean, scale, ALU.mult, ALU.mult))

                def copy(o, i):
                    return nc.vector.tensor_copy(o, i)

                def batch(b, first):
                    turn = b * NH
                    if not first:
                        dve.wait_ge(s_prj, b * NB)
                    dve.tensor_copy(xb[:, :, :], x[:, :, bass.ds(b * T, T)]).then_inc(s_xb, 1)
                    if mean is not None:
                        inv = m.inv[:, bass.ds(2 * b, 2)]
                        dve.tensor_scalar(q_scale[:, :], inv, factor[:, :], None, ALU.mult)
                        dve.tensor_scalar(q_minus[:, :], inv, factor[:, :], -1.0, ALU.mult, ALU.mult)
                        own.link(dve.tensor_scalar(v_scale[:, :], inv, mean, None, ALU.mult))
                    for n in range(NB):
                        if n not in kept_by_act:
                            keep(dve, copy, b, n)
                    for i in range(NH + LAG):
                        if i < NH:
                            hd.top_of(dve, own, turn, i, scale, q_minus[:, :] if mean is not None else None)
                        if i >= LAG and (i - LAG) % 2 == 0:
                            hd.move(dve, copy, turn, i - LAG)
                    dve.wait_ge(hd.s_norm, turn + NH)
                    own.link(dve.reciprocal(rtot[:, :, :], hd.total[:, :, :]))
                    dve.wait_ge(hd.s_out, turn + NH)
                    copy(kept_outT[:, 0:2, :], outT[:, 0:2, :]).then_inc(s_outT[0], 1)
                    dve.wait_ge(s_back, b + 1)
                    for nt in range(2):
                        last = dve.tensor_tensor(m.tok[:, bass.ds(2 * b + nt, 1), :].rearrange("p o (h c) -> p (o h) c", h=NH),
                                                 hd.turned[:, nt, :].rearrange("p (h c) -> p h c", h=NH)[:, :, 0:16],
                                                 rtot[:, :, nt:nt + 1].broadcast_to([P, NH, 16]), ALU.mult)
                    last.then_inc(s_xfree, 1)
                batch(0, True)
                with dve.Fori(1, B, 1) as b:
                    own.enter(b - 1, NH + (1 if mean is None else 2))
                    batch(b, False)
                own.leave(B - 1)


def add_product(nc, m, name, w, x, bias=None, low=None, mean=None):
    kts = w.shape[1]
    with Stage(nc, name) as st:
        acc = st.ps("acc", [P, CT, NT])
        s_sum, own_dve = st.sem("sum"), st.sem("own_dve")
        scaled = st.sb("scaled", [P, 2, HALF])
        with nc.Block() as block:
            @block.tensor
            def _(pe):
                for o in range(CT):
                    for h in range(NT // HALF):
                        t = slice(h * HALF, (h + 1) * HALF)
                        for k in range(kts):
                            last = pe.matmul(acc[:, o, t], w[:, k, o * P:(o + 1) * P], x[:, k, t],
                                             start=k == 0, stop=k == kts - 1 and low is None)
                        if low is not None:
                            last = pe.matmul(acc[:, o, t], low[0][:, o * P:(o + 1) * P], low[1][:, t], start=False, stop=True)
                        last.then_inc(s_sum, 1)

            @block.vector
            def _(dve):
                own = Tally(dve, own_dve)
                for o in range(CT):
                    for h in range(NT // HALF):
                        t = slice(h * HALF, (h + 1) * HALF)
                        dve.wait_ge(s_sum, o * (NT // HALF) + h + 1)
                        if mean is not None:
                            own.link(dve.scalar_tensor_tensor(out=scaled[:, h], in0=acc[:, o, t], scalar=mean,
                                                              in1=m.inv_row[:, t], op0=ALU.mult, op1=ALU.mult))
                            dve.tensor_tensor(m.xT[:, o, t], m.xT[:, o, t], scaled[:, h], ALU.add)
                        elif bias is None:
                            dve.tensor_tensor(m.xT[:, o, t], m.xT[:, o, t], acc[:, o, t], ALU.add)
                        else:
                            dve.scalar_tensor_tensor(out=m.xT[:, o, t], in0=acc[:, o, t], scalar=bias[:, o:o + 1],
                                                     in1=m.xT[:, o, t], op0=ALU.add, op1=ALU.add)



L0_E, L0_R = 8, 64


def argmax_gates(nc, m, d, name, w_g, select, gates):
    with Stage(nc, name) as st:
        lg, ex = st.sb("lg", [P, TT, L0_E]), st.sb("ex", [P, TT, L0_E])
        top, tot = st.sb("top", [P, TT, 1]), st.sb("tot", [P, TT, 1])
        rank = st.sb("rank", [P, L0_E])
        gateT = st.sb("gateT", [L0_E, NT])
        logits = st.ps("logits", [P, TT, L0_E])
        turned = st.ps("turned", [L0_E, NT])
        wide = st.ps("wide", [P, 4, HALF])
        (own_dve, s_logits, s_shift, s_exp, s_gate, s_turned, s_copied, s_wide, loaded) = (st.sem(n) for n in (
            "own_dve", "logits", "shifted", "exp", "gate", "turned", "copied", "wide", "loaded"))
        s_moved = [st.sem("moved_by_dve"), st.sem("moved_by_act")]
        banks = [(g, h) for g in range(4) for h in range(2)]
        with nc.Block() as block:
            @block.sync
            def _(sp):
                sp.dma_start(rank[:, :], d["rank8"]).then_inc(loaded, 16)

            @block.tensor
            def _(pe):
                for j in range(TT):
                    for ct in range(CT):
                        last = pe.matmul(logits[:, j, :], m.hT[:, ct, j * P:(j + 1) * P], w_g[:, ct, :],
                                         start=ct == 0, stop=ct == CT - 1)
                last.then_inc(s_logits, 1)
                pe.wait_ge(s_gate, 1)
                for j in range(TT):
                    last = pe.transpose(turned[:, j * P:(j + 1) * P], ex[:, j, :], m.ident[:, :])
                last.then_inc(s_turned, 1)
                pe.wait_ge(s_copied, 1)
                for n, (g, h) in enumerate(banks):
                    if n >= 4:
                        pe.wait_ge(s_moved[n % 2], (n - 4) // 2 + 1)
                    pe.matmul(wide[:, n % 4, :], select[:, g, :], gateT[:, h * HALF:(h + 1) * HALF],
                              start=True, stop=True).then_inc(s_wide, 1)

            @block.scalar
            def _(act):
                act.wait_ge(s_shift, 1)
                act.activation(ex[:, :, :], lg[:, :, :], ACT.Exp).then_inc(s_exp, 1)
                for n, (g, h) in enumerate(banks):
                    if n % 2:
                        act.wait_ge(s_wide, n + 1)
                        act.activation(gates[:, g, h * HALF:(h + 1) * HALF], wide[:, n % 4, :], ACT.Copy).then_inc(s_moved[1], 1)

            @block.vector
            def _(dve):
                own = Tally(dve, own_dve)
                dve.wait_ge(s_logits, 1)
                own.link(dve.tensor_reduce(top[:, :, :], logits[:, :, :], AX.X, ALU.max))
                dve.tensor_tensor(lg[:, :, :], logits[:, :, :], top[:, :, :].broadcast_to([P, TT, L0_E]),
                                  ALU.subtract).then_inc(s_shift, 1)
                dve.wait_ge(s_exp, 1)
                own.link(dve.tensor_reduce(tot[:, :, :], ex[:, :, :], AX.X, ALU.add))
                own.link(dve.reciprocal(tot[:, :, :], tot[:, :, :]))
                own.link(dve.tensor_scalar(tot[:, :, :], tot[:, :, :], 64.0 / 16.0, None, ALU.mult))
                dve.wait_ge(loaded, 16)
                own.link(dve.tensor_scalar(ex[:, :, :], lg[:, :, :], 0.0, None, ALU.is_equal))
                own.link(dve.tensor_tensor(ex[:, :, :], ex[:, :, :], rank[:, :].unsqueeze(1).broadcast_to([P, TT, L0_E]), ALU.mult))
                own.link(dve.tensor_reduce(top[:, :, :], ex[:, :, :], AX.X, ALU.max))
                own.link(dve.tensor_tensor(ex[:, :, :], ex[:, :, :], top[:, :, :].broadcast_to([P, TT, L0_E]), ALU.is_equal))
                dve.tensor_tensor(ex[:, :, :], ex[:, :, :], tot[:, :, :].broadcast_to([P, TT, L0_E]), ALU.mult).then_inc(s_gate, 1)
                dve.wait_ge(s_turned, 1)
                dve.tensor_copy(gateT[:, :], turned[:, :]).then_inc(s_copied, 1)
                for n, (g, h) in enumerate(banks):
                    if n % 2 == 0:
                        dve.wait_ge(s_wide, n + 1)
                        dve.tensor_copy(gates[:, g, h * HALF:(h + 1) * HALF], wide[:, n % 4, :]).then_inc(s_moved[0], 1)


def gated_inner(nc, m, name, w_a, gates, inner):
    with Stage(nc, name) as st:
        acc = st.ps("acc", [P, 4, HALF])
        s_sum, s_kept = st.sem("sum"), st.sem("kept")
        banks = [(g, h) for g in range(4) for h in range(2)]
        with nc.Block() as block:
            @block.tensor
            def _(pe):
                for n, (g, h) in enumerate(banks):
                    if n >= 4:
                        pe.wait_ge(s_kept, n - 3)
                    for ct in range(CT):
                        last = pe.matmul(acc[:, n % 4, :], w_a[:, ct, g * P:(g + 1) * P],
                                         m.hT[:, ct, h * HALF:(h + 1) * HALF], start=ct == 0, stop=ct == CT - 1)
                    last.then_inc(s_sum, 1)

            @block.vector
            def _(dve):
                for n, (g, h) in enumerate(banks):
                    t = slice(h * HALF, (h + 1) * HALF)
                    dve.wait_ge(s_sum, n + 1)
                    dve.tensor_tensor(inner[:, g, t], acc[:, n % 4, :], gates[:, g, t], ALU.mult).then_inc(s_kept, 1)



L1_CHUNKS = NH * P // HALF


def attention_wide_heads(nc, m, d, name, w_q, w_k, w_v, w_o):
    scale = 128 ** -0.5
    with Stage(nc, name) as st:
        banks = st.ps("banks", [P, 7, HALF])
        hd = Heads(st, banks, True)
        xb = st.sb("xb", [P, CT, T])
        qk = [st.sb("q", [P, NH, T]), st.sb("k", [P, NH, T])]
        v = st.sb("v", [P, 2, NH * P])
        oT = qk[0]
        cos, sin = st.sb("cos", [P, T]), st.sb("sin", [P, T])
        straight, crossed = st.sb("straight", [P, 2, HALF]), st.sb("crossed", [P, 2, HALF])
        rtot = st.sb("rtot", [P, NH, 2])
        prj = banks[:, 5:7, :]
        out = prj
        own_dve, own_act, loaded, s_xb, s_prj, s_rot, s_turned_pos, s_vkept, s_exp, s_okept, s_sum, s_added = (
            st.sem(n) for n in ("own_dve", "own_act", "loaded", "xb_ready", "prj_ready", "rotated_parts", "rotated",
                                "v_kept", "exp_ready", "o_kept", "sum", "added"))
        NR = NH
        NV = 2 * L1_CHUNKS
        with nc.Block() as block:
            @block.sync
            def _(sp):
                sp.dma_start(cos[:, :], d["l1_cos"]).then_inc(loaded, 16)
                sp.dma_start(sin[:, :], d["l1_sin"]).then_inc(loaded, 16)

            @block.tensor
            def _(pe):
                def batch(b, first):
                    turn = b * NH
                    pe.wait_ge(s_xb, b + 1)
                    for n in range(NR):
                        if n >= 2:
                            pe.wait_ge(s_rot, b * NR + n - 1)
                        elif not first:
                            pe.wait_ge(s_added, b)
                        w = w_q if n < NR // 2 else w_k
                        for half in range(2):
                            h = 2 * (n % (NR // 2)) + half
                            for ct in range(CT):
                                last = pe.matmul(prj[:, n % 2, half * T:(half + 1) * T], w[:, ct, h * P:(h + 1) * P],
                                                 xb[:, ct], start=ct == 0, stop=ct == CT - 1)
                        last.then_inc(s_prj, 1)
                    for n in range(NV):
                        if n < 2:
                            pe.wait_ge(s_rot, b * NR + NR - 1 + n)
                        else:
                            pe.wait_ge(s_vkept, b * NV + n - 1)
                        mt, c = n // L1_CHUNKS, n % L1_CHUNKS
                        for ct in range(CT):
                            last = pe.matmul(prj[:, n % 2, :], xb[:, ct, mt * P:(mt + 1) * P],
                                             w_v[:, ct, c * HALF:(c + 1) * HALF], start=ct == 0, stop=ct == CT - 1)
                        last.then_inc(s_prj, 1)
                    pe.wait_ge(s_turned_pos, (b + 1) * NR)
                    pe.wait_ge(s_vkept, (b + 1) * NV)

                    def weigh(h):
                        pe.wait_ge(hd.s_moved[h % 2], turn // 2 + h // 2 + 1)
                        if h >= 2:
                            pe.wait_ge(s_okept, turn + h - 1)
                        for nt in range(2):
                            mine = [(i, mt) for i, (n_, mt) in enumerate(hd.blocks) if n_ == nt]
                            for i, mt in mine:
                                last = pe.matmul(out[:, h % 2, nt * P:(nt + 1) * P], v[:, mt, h * P:(h + 1) * P],
                                                 hd.probsT[:, h % IN_FLIGHT, i * P:(i + 1) * P],
                                                 start=i == mine[0][0], stop=i == mine[-1][0])
                        last.then_inc(hd.s_out, 1)
                    for i in range(NH + WEIGH):
                        if i < NH:
                            hd.score(pe, turn, i, qk[0][:, i, :], qk[1][:, i, :], m.ident_b[:, :], m.mask_window)
                        if LAG <= i < NH + LAG:
                            hd.turn(pe, turn, i - LAG, m.ident[:, :])
                        if i >= WEIGH:
                            weigh(i - WEIGH)
                    pe.wait_ge(s_okept, turn + NH)
                    for o in range(CT):
                        for h in range(NH):
                            last = pe.matmul(out[:, o, 0:T], w_o[:, h, o * P:(o + 1) * P], oT[:, h, :],
                                             start=h == 0, stop=h == NH - 1)
                    last.then_inc(s_sum, 1)
                batch(0, True)
                with pe.Fori(1, B, 1) as b:
                    batch(b, False)

            @block.scalar
            def _(act):
                def copy(o, i):
                    return act.activation(o, i, ACT.Copy)

                def batch(b, first):
                    turn = b * NH
                    for n in range(NV):
                        mt, c = n // L1_CHUNKS, n % L1_CHUNKS
                        act.wait_ge(s_prj, b * (NR + NV) + NR + n + 1)
                        copy(v[:, mt, c * HALF:(c + 1) * HALF], prj[:, n % 2, :]).then_inc(s_vkept, 1)
                    for i in range(NH + WEIGH):
                        if i < NH:
                            hd.exp(act, turn, i, scale, s_exp)
                        if LAG <= i < NH + LAG and (i - LAG) % 2:
                            hd.move(act, copy, turn, i - LAG)
                        if i >= WEIGH:
                            h = i - WEIGH
                            act.wait_ge(hd.s_out, turn + h + 1)
                            copy(oT[:, h, :], out[:, h % 2, 0:T]).then_inc(s_okept, 1)
                batch(0, True)
                with act.Fori(1, B, 1) as b:
                    batch(b, False)

            @block.gpsimd
            def _(pool):
                with pool.Fori(0, B, 1) as b:
                    for n in range(NR):
                        pool.wait_ge(s_rot, b * NR + n + 1)
                        h = 2 * (n % (NR // 2))
                        pool.tensor_tensor(qk[n // (NR // 2)][:, h:h + 2, :], straight[:, n % 2, :].rearrange("p (h t) -> p h t", h=2),
                                           crossed[:, n % 2, :].rearrange("p (h t) -> p h t", h=2), ALU.add).then_inc(s_turned_pos, 1)

            @block.vector
            def _(dve):
                own = Tally(dve, own_dve)
                dve.wait_ge(loaded, 32)

                def copy(o, i):
                    return dve.tensor_copy(o, i)

                def batch(b, first):
                    turn = b * NH
                    dve.tensor_copy(xb[:, :, :], m.hT[:, :, bass.ds(b * T, T)]).then_inc(s_xb, 1)
                    for n in range(NR):
                        dve.wait_ge(s_prj, b * (NR + NV) + n + 1)
                        if n >= 2 or not first:
                            dve.wait_ge(s_turned_pos, b * NR + n - 1)
                        x = prj[:, n % 2, :].rearrange("p (h t) -> p h t", h=2)
                        cr = crossed[:, n % 2, :].rearrange("p (h t) -> p h t", h=2)
                        dve.tensor_tensor(straight[:, n % 2, :].rearrange("p (h t) -> p h t", h=2), x,
                                          cos[:, :].unsqueeze(1).broadcast_to([P, 2, T]), ALU.mult)
                        for src, dst in ((slice(64, P), slice(0, 64)), (slice(0, 64), slice(64, P))):
                            last = dve.tensor_tensor(cr[dst], x[src], sin[src, :].unsqueeze(1).broadcast_to([64, 2, T]), ALU.mult)
                        last.then_inc(s_rot, 1)

                    def normalise(h):
                        dve.wait_ge(s_exp, turn + h + 1)
                        own.link(dve.reciprocal(rtot[:, h, :], hd.total[:, h, :]))
                        for nt, cols in hd.tiles():
                            last = dve.tensor_scalar(hd.probs[:, h % IN_FLIGHT, cols], hd.probs[:, h % IN_FLIGHT, cols], rtot[:, h, nt:nt + 1],
                                                     None, ALU.mult)
                        last.then_inc(hd.s_norm, 1)
                    for i in range(NH + LAG):
                        if i < NH:
                            hd.top_of(dve, own, turn, i, scale)
                        if 1 <= i <= NH:
                            normalise(i - 1)
                        if i >= LAG and (i - LAG) % 2 == 0:
                            hd.move(dve, copy, turn, i - LAG)
                    dve.wait_ge(s_sum, b + 1)
                    for o in range(CT):
                        t = bass.ds(b * T, T)
                        last = dve.tensor_tensor(m.xT[:, o, t], m.xT[:, o, t], out[:, o, 0:T], ALU.add)
                    last.then_inc(s_added, 1)
                batch(0, True)
                with dve.Fori(1, B, 1) as b:
                    own.enter(b - 1, 2 * NH)
                    batch(b, False)
                own.leave(B - 1)



E, GROUPS_E = 64, 8
GE = E // GROUPS_E
TOP_GROUPS = 4
ROUTED_SCALE = 2.5


class Routing:

    def __init__(self, st, K, moves):
        self.K = K
        self.scattered, self.gathered = moves
        self.put = st.sb("slot_put", [P, TT, K], U32)
        self.get = st.sb("slot_get", [P, TT, K], U32)
        self.gate = st.sb("gate", [P, TT, K])


def route(nc, m, d, name, w_g, bias, r, cap, fill):
    K = r.K
    with Stage(nc, name) as st:
        score, biased, masked = (st.sb(n, [P, TT, E]) for n in ("score", "biased", "masked"))
        hi, lo, hi2, lo2, mid = (st.sb(n, [P, TT * GROUPS_E, 4]) for n in ("hi", "lo", "hi2", "lo2", "mid"))
        gsum, gin, pen = (st.sb(n, [P, TT, GROUPS_E]) for n in ("gsum", "gin", "pen"))
        best, idx, idxf = st.sb("best", [P, TT, 8]), st.sb("idx", [P, TT, 8], U32), st.sb("idxf", [P, TT, 8])
        geq = st.sb("geq", [P, TT, TOP_GROUPS, GROUPS_E])
        chosen, prod = st.sb("chosen", [P, TT, K, E]), st.sb("prod", [P, TT, K, E])
        sel = st.sb("sel", [P, TT, E], BF16)
        pos, wk, keep, slot, tmp = (st.sb(n, [P, TT, K]) for n in ("pos", "wk", "keep", "slot", "tmp"))
        wsum = st.sb("wsum", [P, TT, 1])
        logits, before = st.ps("logits", [P, TT, E]), st.ps("before", [P, TT, E])
        own_dve, s_logits, s_score, s_sel, s_before = (st.sem(n) for n in ("own_dve", "logits", "score", "sel", "before"))
        with nc.Block() as block:
            @block.tensor
            def _(pe):
                for j in range(TT):
                    for ct in range(CT):
                        last = pe.matmul(logits[:, j, :], m.hT[:, ct, j * P:(j + 1) * P], w_g[:, ct, :],
                                         start=ct == 0, stop=ct == CT - 1)
                last.then_inc(s_logits, 1)
                pe.wait_ge(s_sel, 1)
                pe.matmul(before[:, :, :], m.earlier[:, :], sel[:, :, :], start=True, stop=False)
                for j in range(TT - 1):
                    last = pe.matmul(before[:, j + 1:, :], m.ones_b[:, :], sel[:, j:j + 1, :].broadcast_to([P, TT - 1 - j, E]),
                                     start=False, stop=j == TT - 2)
                last.then_inc(s_before, 1)

            @block.scalar
            def _(act):
                act.wait_ge(s_logits, 1)
                act.activation(score[:, :, :], logits[:, :, :], ACT.Sigmoid).then_inc(s_score, 1)

            @block.vector
            def _(dve):
                own = Tally(dve, own_dve)

                def both(o, a, b, op):
                    own.link(dve.tensor_tensor(o, a, b, op))
                dve.wait_ge(s_score, 1)
                both(biased[:, :, :], score[:, :, :], bias[:, :].unsqueeze(1).broadcast_to([P, TT, E]), ALU.add)
                v = biased[:, :, :].rearrange("p t (g e) -> p (t g) e", e=GE)
                both(hi[:, :, :], v[:, :, 0:4], v[:, :, 4:8], ALU.max)
                both(lo[:, :, :], v[:, :, 0:4], v[:, :, 4:8], ALU.min)
                h, l, h_, l_ = hi, lo, hi2, lo2
                for n in (2, 1):
                    both(mid[:, :, 0:n], h[:, :, 0:n], h[:, :, n:2 * n], ALU.min)
                    both(h_[:, :, 0:n], h[:, :, 0:n], h[:, :, n:2 * n], ALU.max)
                    both(l_[:, :, 0:n], l[:, :, 0:n], l[:, :, n:2 * n], ALU.max)
                    both(l_[:, :, 0:n], l_[:, :, 0:n], mid[:, :, 0:n], ALU.max)
                    h, l, h_, l_ = h_, l_, h, l
                both(gsum[:, :, :], h[:, :, 0:1].rearrange("p (t g) o -> p t (g o)", g=GROUPS_E),
                     l[:, :, 0:1].rearrange("p (t g) o -> p t (g o)", g=GROUPS_E), ALU.add)
                for j in range(TT):
                    last = dve.max(best[:, j, :], gsum[:, j, :])
                own.link(last)
                for j in range(TT):
                    last = dve.max_index(idx[:, j, :], best[:, j, :], gsum[:, j, :])
                own.link(last)
                own.link(dve.tensor_copy(idxf[:, :, :], idx[:, :, :]))
                both(geq[:, :, :, :], m.iota[:, 0:GROUPS_E].unsqueeze(1).unsqueeze(1).broadcast_to([P, TT, TOP_GROUPS, GROUPS_E]),
                     idxf[:, :, 0:TOP_GROUPS].unsqueeze(3).broadcast_to([P, TT, TOP_GROUPS, GROUPS_E]), ALU.is_equal)
                own.link(dve.tensor_reduce(gin[:, :, :], geq[:, :, :, :].rearrange("p t k g -> p t g k"), AX.X, ALU.add))
                own.link(dve.tensor_scalar(pen[:, :, :], gin[:, :, :], -fill, fill, ALU.mult, ALU.add))
                mk = masked[:, :, :].rearrange("p t (g e) -> p (t g) e", e=GE)
                both(mk, v, gin[:, :, :].rearrange("p t g -> p (t g)").unsqueeze(2).broadcast_to([P, TT * GROUPS_E, GE]), ALU.mult)
                both(mk, mk, pen[:, :, :].rearrange("p t g -> p (t g)").unsqueeze(2).broadcast_to([P, TT * GROUPS_E, GE]), ALU.add)
                for j in range(TT):
                    last = dve.max(best[:, j, :], masked[:, j, :])
                own.link(last)
                for j in range(TT):
                    last = dve.max_index(idx[:, j, :], best[:, j, :], masked[:, j, :])
                own.link(last)
                own.link(dve.tensor_copy(idxf[:, :, :], idx[:, :, :]))
                full = [P, TT, K, E]
                both(chosen[:, :, :, :], m.iota[:, :].unsqueeze(1).unsqueeze(1).broadcast_to(full),
                     idxf[:, :, 0:K].unsqueeze(3).broadcast_to(full), ALU.is_equal)
                dve.tensor_reduce(sel[:, :, :], chosen[:, :, :, :].rearrange("p t k e -> p t e k"), AX.X, ALU.max).then_inc(s_sel, 1)
                both(prod[:, :, :, :], chosen[:, :, :, :], score[:, :, :].unsqueeze(2).broadcast_to(full), ALU.mult)
                own.link(dve.tensor_reduce(wk[:, :, :], prod[:, :, :, :], AX.X, ALU.add))
                dve.wait_ge(s_before, 1)
                both(prod[:, :, :, :], chosen[:, :, :, :], before[:, :, :].unsqueeze(2).broadcast_to(full), ALU.mult)
                own.link(dve.tensor_reduce(pos[:, :, :], prod[:, :, :, :], AX.X, ALU.add))
                own.link(dve.tensor_scalar(keep[:, :, :], pos[:, :, :], float(cap), None, ALU.is_lt))
                own.link(dve.scalar_tensor_tensor(out=slot[:, :, :], in0=idxf[:, :, 0:K], scalar=float(cap), in1=pos[:, :, :],
                                                  op0=ALU.mult, op1=ALU.add))
                own.link(dve.tensor_scalar(tmp[:, :, :], keep[:, :, :], -1048576.0, 1048576.0, ALU.mult, ALU.add))
                both(tmp[:, :, :], tmp[:, :, :], slot[:, :, :], ALU.add)
                own.link(dve.tensor_copy(r.put[:, :, :], tmp[:, :, :]))
                both(slot[:, :, :], slot[:, :, :], keep[:, :, :], ALU.mult)
                dve.tensor_copy(r.get[:, :, :], slot[:, :, :])
                own.link(dve.tensor_reduce(wsum[:, :, :], wk[:, :, :], AX.X, ALU.add))
                own.link(dve.tensor_scalar(wsum[:, :, :], wsum[:, :, :], 1e-20, None, ALU.add))
                own.link(dve.reciprocal(wsum[:, :, :], wsum[:, :, :]))
                both(wk[:, :, :], wk[:, :, :], wsum[:, :, :].broadcast_to([P, TT, K]), ALU.mult)
                dve.scalar_tensor_tensor(out=r.gate[:, :, :], in0=wk[:, :, :], scalar=ROUTED_SCALE, in1=keep[:, :, :],
                                         op0=ALU.mult, op1=ALU.mult)


def dispatch(nc, m, name, r, slots_in, w_up, w_gate, w_down, inner, rows_i):
    n_slots = slots_in.shape[0]
    tiles = w_up.shape[2] // rows_i
    with Stage(nc, name) as st:
        acc, total = st.ps("acc", [P, 4, HALF]), st.ps("total", [P, CT, NT])
        side = st.sb("side", [P, 2, HALF])
        scattered = r.scattered
        s_sum, s_act, s_kept, s_total = (st.sem(n) for n in ("sum", "activated", "kept", "total"))
        banks = [(i, h) for i in range(tiles) for h in range(NT // HALF)]
        with nc.Block() as block:
            @block.gpsimd
            def _(pool):
                for j in range(TT):
                    for k in range(r.K):
                        pool.indirect_dma_start(slots_in, bass.IndirectOffsetOnAxis(ap=r.put[:, j, k:k + 1], axis=0),
                                                m.tok[:, j, :], None, bounds_check=n_slots - 1,
                                                oob_is_err=False).then_inc(scattered, 16)
                pool.wait_ge(scattered, 16 * TT * r.K)

            @block.tensor
            def _(pe):
                for n, (i, h) in enumerate(banks):
                    if n >= 2:
                        pe.wait_ge(s_kept, n - 1)
                    for g, w in enumerate((w_up, w_gate)):
                        for ct in range(CT if w is not None else 0):
                            last = pe.matmul(acc[0:rows_i, 2 * (n % 2) + g, :], w[:, ct, i * rows_i:(i + 1) * rows_i],
                                             m.hT[:, ct, h * HALF:(h + 1) * HALF], start=ct == 0, stop=ct == CT - 1)
                    last.then_inc(s_sum, 1)
                pe.wait_ge(s_kept, len(banks))
                for o in range(CT):
                    for h in range(NT // HALF):
                        t = slice(h * HALF, (h + 1) * HALF)
                        for k in range(tiles):
                            last = pe.matmul(total[:, o, t], w_down[:, k, o * P:(o + 1) * P], inner[0:rows_i, k, t],
                                             start=k == 0, stop=k == tiles - 1)
                        last.then_inc(s_total, 1)

            @block.scalar
            def _(act):
                for n in range(len(banks)):
                    act.wait_ge(s_sum, n + 1)
                    if n >= 2:
                        act.wait_ge(s_kept, n - 1)
                    if w_gate is None:
                        ins = act.activation(side[0:rows_i, n % 2, :], acc[0:rows_i, 2 * (n % 2), :], ACT.Relu)
                    else:
                        ins = act.activation(side[0:rows_i, n % 2, :], acc[0:rows_i, 2 * (n % 2) + 1, :], ACT.Silu)
                    ins.then_inc(s_act, 1)

            @block.vector
            def _(dve):
                for n, (i, h) in enumerate(banks):
                    dve.wait_ge(s_act, n + 1)
                    other = side[0:rows_i, n % 2, :] if w_gate is None else acc[0:rows_i, 2 * (n % 2), :]
                    dve.tensor_tensor(inner[0:rows_i, i, h * HALF:(h + 1) * HALF], side[0:rows_i, n % 2, :], other,
                                      ALU.mult).then_inc(s_kept, 1)
                for o in range(CT):
                    for h in range(NT // HALF):
                        t = slice(h * HALF, (h + 1) * HALF)
                        dve.wait_ge(s_total, o * (NT // HALF) + h + 1)
                        dve.tensor_tensor(m.xT[:, o, t], m.xT[:, o, t], total[:, o, t], ALU.add)


RING = 8
STORES = 4


def experts(nc, m, name, slots_in, slots_out, weights, per, rows_i, gated):
    units = slots_in.shape[0] // P
    cap = P // per
    n_in = 2 if gated else 1
    with Stage(nc, name) as st:
        xs = st.sb("xs", [P, RING, C])
        w_in = per * CT * rows_i
        w = st.sb("w", [P, RING, n_in * w_in + per * C])
        wi = [w[:, :, g * w_in:(g + 1) * w_in].rearrange("p r (e t i) -> p r e t i", e=per, t=CT) for g in range(n_in)]
        wo = w[:, :, n_in * w_in:].rearrange("p r (e c) -> p r e c", e=per)
        xsT = st.sb("xsT", [P, 2, CT, P])
        half = st.sb("half", [P, 2, P])
        inner = st.sb("inner", [P, 2, P])
        y = st.sb("y", [P, STORES, C])
        xs_t, up, ys = st.ps("xs_t", [P, 2, HALF]), st.ps("up", [P, 2, HALF]), st.ps("ys", [P, 2, HALF])
        loaded = [st.sem(f"loaded{i}") for i in range(RING)]
        stored = [st.sem(f"stored{i}") for i in range(STORES)]
        s_turned, s_copied, s_up, s_half, s_inner, s_ys, s_kept = (
            st.sem(n) for n in ("turned", "copied", "up", "half", "inner", "ys", "kept"))
        n_loads = 2

        def pipeline(eng, steps, depth):
            for i in range(RING):
                steps(i, i)
            with eng.Fori(1, units // RING, 1) as it:
                for c in range(RING):
                    steps(it * RING + c, RING + c)
            for i in range(units, units + depth):
                steps(i, i)
        with nc.Block() as block:
            @block.sync
            def _(sp):
                def load_unit(u, r, seen):
                    if seen >= RING:
                        sp.wait_ge(s_ys, u - RING + 1)
                    sp.dma_start(xs[:, r, :], slots_in[bass.ds(u * P, P), :]).then_inc(loaded[r], 16)
                    sp.dma_start(w[:, r], weights[bass.ds(u, 1)]).then_inc(loaded[r], 16)

                def store_unit(u, r):
                    sp.wait_ge(s_kept, u + 1)
                    sp.dma_start(slots_out[bass.ds(u * P, P), :], y[:, r % STORES, :]).then_inc(stored[r % STORES], 16)

                for u in range(RING):
                    load_unit(u, u, u)
                with sp.Fori(1, units // RING, 1) as it:
                    for c in range(RING):
                        store_unit(it * RING + c - RING, c)
                        load_unit(it * RING + c, c, RING)
                for c in range(RING):
                    store_unit(units - RING + c, c)
                for s in stored:
                    sp.wait_ge(s, 16 * units // STORES)

            @block.tensor
            def _(pe):
                def steps(i, seen):
                    c = seen % RING
                    if isinstance(i, int) and i >= units:
                        pass
                    else:
                        pe.wait_ge(loaded[c], 16 * n_loads * (i // RING + 1) if isinstance(i, int) else 16 * n_loads * (i // RING + 1))
                        if seen >= 2:
                            pe.wait_ge(s_copied, i - 1)
                        for ct in range(CT):
                            last = pe.transpose(xs_t[:, c % 2, ct * P:(ct + 1) * P], xs[:, c, ct * P:(ct + 1) * P], m.ident[:, :])
                        last.then_inc(s_turned, 1)
                    if seen >= 1 and not (isinstance(i, int) and i - 1 >= units):
                        r = (c - 1) % RING
                        pe.wait_ge(s_copied, i)
                        if seen >= 3:
                            pe.wait_ge(s_inner, i - 2)
                        for e in range(per):
                            for g in range(n_in):
                                for ct in range(CT):
                                    last = pe.matmul(up[0:rows_i, r % 2, g * P + e * cap:g * P + (e + 1) * cap], wi[g][:, r, e, ct],
                                                     xsT[:, r % 2, ct, e * cap:(e + 1) * cap], start=ct == 0, stop=ct == CT - 1)
                        last.then_inc(s_up, 1)
                    if seen >= 2:
                        r = (c - 2) % RING
                        pe.wait_ge(s_inner, i - 1)
                        if seen >= 4:
                            pe.wait_ge(s_kept, i - 3)
                        for e in range(per):
                            last = pe.matmul(ys[e * cap:(e + 1) * cap, r % 2, 0:C], inner[0:rows_i, r % 2, e * cap:(e + 1) * cap],
                                             wo[0:rows_i, r, e, :], start=True, stop=True)
                        last.then_inc(s_ys, 1)
                pipeline(pe, steps, 2)

            @block.scalar
            def _(act):
                def steps(i, seen):
                    c = seen % RING
                    if not (isinstance(i, int) and i >= units):
                        act.wait_ge(s_turned, i + 1)
                        if seen >= 2:
                            act.wait_ge(s_up, i - 1)
                        act.activation(xsT[:, c % 2].rearrange("p a b -> p (a b)"), xs_t[:, c % 2, 0:C], ACT.Copy).then_inc(s_copied, 1)
                    if seen >= 1:
                        r = (c - 1) % RING
                        act.wait_ge(s_up, i)
                        if seen >= 3:
                            act.wait_ge(s_inner, i - 2)
                        if gated:
                            ins = act.activation(half[0:rows_i, r % 2, :], up[0:rows_i, r % 2, P:2 * P], ACT.Silu)
                        else:
                            ins = act.activation(half[0:rows_i, r % 2, :], up[0:rows_i, r % 2, 0:P], ACT.Relu)
                        ins.then_inc(s_half, 1)
                pipeline(act, steps, 1)

            @block.vector
            def _(dve):
                def steps(i, seen):
                    c = seen % RING
                    if seen >= 1 and not (isinstance(i, int) and i - 1 >= units):
                        r = (c - 1) % RING
                        dve.wait_ge(s_half, i)
                        if seen >= 3:
                            dve.wait_ge(s_ys, i - 2)
                        other = up[0:rows_i, r % 2, 0:P] if gated else half[0:rows_i, r % 2, :]
                        dve.tensor_tensor(inner[0:rows_i, r % 2, :], half[0:rows_i, r % 2, :], other, ALU.mult).then_inc(s_inner, 1)
                    if seen >= 2:
                        r = (c - 2) % RING
                        dve.wait_ge(s_ys, i - 1)
                        if seen >= 2 + STORES:
                            dve.wait_ge(stored[r % STORES], 16 * ((i - 2) // STORES))
                        dve.tensor_copy(y[:, r % STORES, :], ys[:, r % 2, 0:C]).then_inc(s_kept, 1)
                pipeline(dve, steps, 2)


def combine(nc, m, name, r, slots_out):
    with Stage(nc, name) as st:
        got = st.sb("got", [P, TT, C])
        turned = st.ps("turned", [P, CT, NT])
        gathered = r.gathered
        s_added, s_turned = st.sem("added"), st.sem("turned")
        with nc.Block() as block:
            @block.gpsimd
            def _(pool):
                def gather(k, first):
                    for j in range(TT):
                        if not first:
                            pool.wait_ge(s_added, (k - 1) * TT + j + 1)
                        pool.indirect_dma_start(got[:, j, :], None, slots_out,
                                                bass.IndirectOffsetOnAxis(ap=r.get[:, j, k:k + 1], axis=0)
                                                ).then_inc(gathered[j], 16)
                for k in range(r.K):
                    gather(k, k == 0)

            @block.vector
            def _(dve):
                def add(k, first):
                    for j in range(TT):
                        dve.wait_ge(gathered[j], 16 * (k + 1))
                        if first:
                            dve.tensor_scalar(m.tok[:, j, :], got[:, j, :], r.gate[:, j, 0:1], None, ALU.mult).then_inc(s_added, 1)
                        else:
                            dve.wait_ge(s_added, (k - 1) * TT + j + 1)
                            dve.scalar_tensor_tensor(out=m.tok[:, j, :], in0=got[:, j, :], scalar=r.gate[:, j, bass.ds(k, 1)],
                                                     in1=m.tok[:, j, :], op0=ALU.mult, op1=ALU.add).then_inc(s_added, 1)
                add(0, True)
                with dve.Fori(1, r.K, 1) as k:
                    add(k, False)
                for h in range(2):
                    dve.wait_ge(s_turned, h + 1)
                    t = slice(h * HALF, (h + 1) * HALF)
                    for ct in range(CT):
                        dve.tensor_tensor(m.xT[:, ct, t], m.xT[:, ct, t], turned[:, ct, t], ALU.add)

            @block.tensor
            def _(pe):
                for j in range(TT):
                    pe.wait_ge(s_added, (r.K - 1) * TT + j + 1)
                    for ct in range(CT):
                        last = pe.transpose(turned[:, ct, j * P:(j + 1) * P], m.tok[:, j, ct * P:(ct + 1) * P], m.ident[:, :])
                    if j % (TT // 2) == TT // 2 - 1:
                        last.then_inc(s_turned, 1)



L2_H, L2_D = 32, 8
L2_HALF = TT // B


def qkv_tokens(nc, m, name, w, bias, qkv):
    cols = [slice(0, HALF), slice(HALF, 3 * C)]
    with Stage(nc, name) as st:
        acc = st.ps("acc", [P, 4, HALF])
        s_sum, s_kept = st.sem("sum"), st.sem("kept")
        banks = [(j, c) for j in range(TT) for c in cols]
        with nc.Block() as block:
            @block.tensor
            def _(pe):
                for n, (j, c) in enumerate(banks):
                    if n >= 4:
                        pe.wait_ge(s_kept, n - 3)
                    for ct in range(CT):
                        last = pe.matmul(acc[:, n % 4, 0:c.stop - c.start], m.hT[:, ct, j * P:(j + 1) * P], w[:, ct, c],
                                         start=ct == 0, stop=ct == CT - 1)
                    last.then_inc(s_sum, 1)

            @block.vector
            def _(dve):
                for n, (j, c) in enumerate(banks):
                    dve.wait_ge(s_sum, n + 1)
                    dve.tensor_tensor(qkv[:, j, c], acc[:, n % 4, 0:c.stop - c.start], bias[:, c], ALU.add).then_inc(s_kept, 1)


def attention_over_batch(nc, m, d, name, qkv):
    X = L2_HALF * L2_H
    scale = float(np.float32(1) / np.sqrt(np.float32(L2_D)))
    with Stage(nc, name) as st:
        cos, sin = st.sb("cos", [P, B, L2_D]), st.sb("sin", [P, B, L2_D])
        straight, crossed = st.sb("straight", [P, TT, 2 * C]), st.sb("crossed", [P, TT, 2 * C])
        vc = st.sb("vc", [P, TT, C])
        prod = st.sb("prod", [P, 2, B * L2_HALF * C])
        score, top, tot = st.sb("score", [P, B, B, X]), st.sb("top", [P, B, X]), st.sb("tot", [P, B, X])
        (loaded, own_dve, s_straight, s_crossed, s_rot, s_cleared, s_v, s_prod, s_red, s_shift, s_exp, s_norm, s_wprod,
         s_wred) = (st.sem(n) for n in ("loaded", "own_dve", "straight", "crossed", "rotated", "cleared", "v", "prod",
                                        "reduced", "shifted", "exp", "norm", "weighted", "summed"))
        x = qkv[:, :, 0:2 * C].rearrange("p t (h e) -> p t h e", e=L2_D)

        def heads(t):
            return t[:, :, :].rearrange("p t (h e) -> p t h e", e=L2_D)

        def table(t, b, part):
            n = part.stop - part.start
            return t[:, b, part].unsqueeze(1).unsqueeze(1).broadcast_to([P, L2_HALF, 2 * L2_H, n])
        lo, hi, both = slice(0, L2_D // 2), slice(L2_D // 2, L2_D), slice(0, L2_D)
        order = list(range(B))
        with nc.Block() as block:
            @block.sync
            def _(sp):
                sp.dma_start(cos[:, :, :], d["l2_cos"]).then_inc(loaded, 16)
                sp.dma_start(sin[:, :, :], d["l2_sin"]).then_inc(loaded, 16)

            @block.gpsimd
            def _(pool):
                pool.memset(score[:, :, :, :], MASKED).then_inc(s_cleared, 1)
                pool.wait_ge(loaded, 32)
                for b in range(B):
                    j = slice(b * L2_HALF, (b + 1) * L2_HALF)
                    for dst, src in ((lo, hi), (hi, lo)):
                        last = pool.tensor_tensor(heads(crossed)[:, j, :, dst], x[:, j, :, src], table(sin, b, dst), ALU.mult)
                    last.then_inc(s_crossed, 1)
                pool.tensor_copy(vc[:, :, :], qkv[:, :, 2 * C:3 * C]).then_inc(s_v, 1)
                for s in order:
                    pool.wait_ge(s_rot, B)
                    if s >= 2:
                        pool.wait_ge(s_red, s - 1)
                    o = prod[:, s % 2, 0:(s + 1) * L2_HALF * C].rearrange("p (k t c) -> p k t c", t=L2_HALF, c=C)
                    q = straight[:, s * L2_HALF:(s + 1) * L2_HALF, 0:C].unsqueeze(1).broadcast_to([P, s + 1, L2_HALF, C])
                    k = straight[:, 0:(s + 1) * L2_HALF, C:2 * C].rearrange("p (k t) c -> p k t c", t=L2_HALF)
                    pool.tensor_tensor(o, q, k, ALU.mult).then_inc(s_prod, 1)
                pool.wait_ge(s_v, 1)
                pool.wait_ge(s_norm, 1)
                for s in order:
                    if s < 2:
                        pool.wait_ge(s_red, B)
                    else:
                        pool.wait_ge(s_wred, s - 1)
                    o = prod[:, s % 2, 0:(s + 1) * L2_HALF * C].rearrange("p (k x e) -> p k x e", x=X, e=L2_D)
                    v = vc[:, 0:(s + 1) * L2_HALF, :].rearrange("p (k t) (h e) -> p k (t h) e", t=L2_HALF, e=L2_D)
                    p = score[:, s, 0:s + 1, :].unsqueeze(3).broadcast_to([P, s + 1, X, L2_D])
                    pool.tensor_tensor(o, v, p, ALU.mult).then_inc(s_wprod, 1)

            @block.scalar
            def _(act):
                act.wait_ge(s_shift, 1)
                act.activation(score[:, :, :, :], score[:, :, :, :], ACT.Exp, scale=scale).then_inc(s_exp, 1)

            @block.vector
            def _(dve):
                own = Tally(dve, own_dve)
                dve.wait_ge(loaded, 32)
                for b in range(B):
                    j = slice(b * L2_HALF, (b + 1) * L2_HALF)
                    dve.tensor_tensor(heads(straight)[:, j], x[:, j], table(cos, b, both), ALU.mult).then_inc(s_straight, 1)
                for b in range(B):
                    j = slice(b * L2_HALF, (b + 1) * L2_HALF)
                    dve.wait_ge(s_straight, b + 1)
                    dve.wait_ge(s_crossed, b + 1)
                    dve.tensor_tensor(straight[:, j, :], straight[:, j, :], crossed[:, j, :], ALU.add).then_inc(s_rot, 1)
                dve.wait_ge(s_cleared, 1)
                for s in order:
                    dve.wait_ge(s_prod, s + 1)
                    src = prod[:, s % 2, 0:(s + 1) * L2_HALF * C].rearrange("p (k x e) -> p k x e", x=X, e=L2_D)
                    dve.tensor_reduce(score[:, s, 0:s + 1, :], src, AX.X, ALU.add).then_inc(s_red, 1)
                dve.wait_ge(s_red, B)
                own.link(dve.tensor_reduce(top[:, :, :], score[:, :, :, :].rearrange("p s k x -> p s x k"), AX.X, ALU.max))
                full = [P, B, B, X]
                dve.tensor_tensor(score[:, :, :, :], score[:, :, :, :], top[:, :, :].unsqueeze(2).broadcast_to(full),
                                  ALU.subtract).then_inc(s_shift, 1)
                dve.wait_ge(s_exp, 1)
                own.link(dve.tensor_reduce(tot[:, :, :], score[:, :, :, :].rearrange("p s k x -> p s x k"), AX.X, ALU.add))
                own.link(dve.reciprocal(tot[:, :, :], tot[:, :, :]))
                dve.tensor_tensor(score[:, :, :, :], score[:, :, :, :], tot[:, :, :].unsqueeze(2).broadcast_to(full),
                                  ALU.mult).then_inc(s_norm, 1)
                for s in order:
                    dve.wait_ge(s_wprod, s + 1)
                    src = prod[:, s % 2, 0:(s + 1) * L2_HALF * C].rearrange("p (k x) -> p x k", x=L2_HALF * C)
                    out = m.tok[:, s * L2_HALF:(s + 1) * L2_HALF, :].rearrange("p t c -> p (t c)")
                    dve.tensor_reduce(out, src, AX.X, ALU.add).then_inc(s_wred, 1)


def turn_tokens(nc, m, name):
    with Stage(nc, name) as st:
        tp = st.ps("tp", [P, CT, NT])
        s_turned = st.sem("turned")
        with nc.Block() as block:
            @block.tensor
            def _(pe):
                for h in range(NT // HALF):
                    for ct in range(CT):
                        for j in range(h * HALF // P, (h + 1) * HALF // P):
                            last = pe.transpose(tp[:, ct, j * P:(j + 1) * P], m.tok[:, j, ct * P:(ct + 1) * P], m.ident[:, :])
                        last.then_inc(s_turned, 1)

            @block.vector
            def _(dve):
                for h in range(NT // HALF):
                    t = slice(h * HALF, (h + 1) * HALF)
                    dve.wait_ge(s_turned, 2 * h + 1)
                    dve.tensor_copy(m.hT[:, 0, t], tp[:, 0, t])

            @block.scalar
            def _(act):
                for h in range(NT // HALF):
                    t = slice(h * HALF, (h + 1) * HALF)
                    act.wait_ge(s_turned, 2 * h + 2)
                    act.activation(m.hT[:, 1, t], tp[:, 1, t], ACT.Copy)



def low_rank(nc, m, name, w, low):
    with Stage(nc, name) as st:
        acc = st.ps("acc", [16, NT])
        s_sum = st.sem("sum")
        with nc.Block() as block:
            @block.tensor
            def _(pe):
                for h in range(NT // HALF):
                    t = slice(h * HALF, (h + 1) * HALF)
                    for ct in range(CT):
                        last = pe.matmul(acc[:, t], w[:, ct, :], m.hT[:, ct, t], start=ct == 0, stop=ct == CT - 1)
                last.then_inc(s_sum, 1)

            @block.vector
            def _(dve):
                dve.wait_ge(s_sum, 1)
                dve.tensor_scalar(low[:, :], acc[:, :], 0.5, None, ALU.mult)


L3_I = 1024


def swiglu_rms(nc, m, name, x, w_gate, w_up, mean, ln, h):
    with Stage(nc, name) as st:
        gate, up = st.ps("gate", [P, 2, HALF]), st.ps("up", [P, 2, HALF])
        act_out = st.sb("act_out", [P, 2, HALF])
        square = st.sb("square", [P, L3_I])
        ssum, rms, rinv = st.sb("ssum", [P, TT]), st.sb("rms", [P, TT]), st.sb("rinv", [P, TT])
        scales = st.sb("scales", [P, 2, TT])
        own_dve, s_scales, s_sum, s_act, s_h, s_sq, s_var, s_rms = (st.sem(n) for n in ("own_dve", "scales", "sum", "act", "h", "sq", "var", "rms"))
        banks = [(j, c) for j in range(TT) for c in range(L3_I // HALF)]
        with nc.Block() as block:
            @block.tensor
            def _(pe):
                for n, (j, c) in enumerate(banks):
                    if n >= 2:
                        pe.wait_ge(s_h, n - 1)
                    for into, w in ((gate, w_gate), (up, w_up)):
                        for ct in range(CT):
                            last = pe.matmul(into[:, n % 2, :], x[:, ct, j * P:(j + 1) * P], w[:, ct, c * HALF:(c + 1) * HALF],
                                             start=ct == 0, stop=ct == CT - 1)
                    last.then_inc(s_sum, 1)

            @block.scalar
            def _(act):
                act.wait_ge(s_scales, 1)
                for n, (j, c) in enumerate(banks):
                    act.wait_ge(s_sum, n + 1)
                    if n >= 2:
                        act.wait_ge(s_h, n - 1)
                    act.activation(act_out[:, n % 2, :], gate[:, n % 2, :], ACT.Silu, scale=scales[:, 0, j:j + 1]).then_inc(s_act, 1)
                act.wait_ge(s_var, 1)
                act.activation(rms[:, :], rinv[:, :], ACT.Sqrt).then_inc(s_rms, 1)

            @block.vector
            def _(dve):
                own = Tally(dve, own_dve)
                dve.tensor_scalar(scales[:, 0, :], m.inv[:, :], mean[:, 0:1], None, ALU.mult).then_inc(s_scales, 1)
                own.link(dve.tensor_scalar(scales[:, 1, :], m.inv[:, :], mean[:, 1:2], None, ALU.mult))
                for n, (j, c) in enumerate(banks):
                    dve.wait_ge(s_act, n + 1)
                    dve.scalar_tensor_tensor(out=h[:, j, c * HALF:(c + 1) * HALF], in0=up[:, n % 2, :], scalar=scales[:, 1, j:j + 1],
                                             in1=act_out[:, n % 2, :], op0=ALU.mult, op1=ALU.mult).then_inc(s_h, 1)
                for j in range(TT):
                    dve.wait_ge(s_h, 2 * j + 2)
                    own.link(dve.tensor_tensor_reduce(square[:, :], h[:, j, :], h[:, j, :], 1.0, 0.0, ALU.mult, ALU.add, ssum[:, j:j + 1]))
                dve.tensor_scalar(rinv[:, :], ssum[:, :], 1.0 / L3_I, 1e-6, ALU.mult, ALU.add).then_inc(s_var, 1)
                dve.wait_ge(s_rms, 1)
                own.link(dve.reciprocal(rinv[:, :], rms[:, :]))
                for j in range(TT):
                    dve.scalar_tensor_tensor(out=h[:, j, :], in0=h[:, j, :], scalar=rinv[:, j:j + 1], in1=ln[:, :],
                                             op0=ALU.mult, op1=ALU.mult)


def build(nc, m, d, out, stop=8):
    ctx = ExitStack()
    with ctx:
        def sb(name, shape, dt=F32):
            return ctx.enter_context(nc.sbuf_tensor(name, shape, dt))
        m.xT, m.hT = sb("xT", [P, CT, NT]), sb("hT", [P, CT, NT])
        m.tok = sb("tok", [P, TT, C])
        m.inv, m.inv_row = sb("inv", [P, TT]), sb("inv_row", [P, NT])
        m.gain = sb("gain", [P, CONDS, CT, NT])
        m.ident, m.ones = sb("ident", [P, P]), sb("ones", [P, P])
        m.ident_b = sb("ident_b", [P, P], BF16)
        m.mask_causal, m.mask_window = sb("mask_causal", [P, 3 * P], BF16), sb("mask_window", [P, 3 * P], BF16)
        m.ones_b, m.earlier, m.iota = sb("ones_b", [P, P], BF16), sb("earlier", [P, P], BF16), sb("iota", [P, E])
        m.wu, m.condT = sb("wu", [P, 2, 2 * CONDS, CT]), sb("condT", [64, B])
        m.slots_in_1 = nc.dram_tensor("slots_in_1", (64 * 64, C), F32).ap()
        m.slots_in_2 = nc.dram_tensor("slots_in_2", (64 * 128, C), F32).ap()
        m.slots_out_1 = nc.dram_tensor("slots_out_1", (64 * 64, C), F32).ap()
        m.slots_out_2 = nc.dram_tensor("slots_out_2", (64 * 128, C), F32).ap()
        moves = ctx.enter_context(Stage(nc, "moves"))
        m.moves_1, m.moves_2 = ((moves.sem(f"scattered_{n}"), [moves.sem(f"gathered_{n}_{j}") for j in range(TT)]) for n in (1, 2))
        load_constants(nc, m, d)
        condition_gains(nc, m, d, "gains01", 0)
        layer0(nc, m, d, stop)
        layer1(nc, m, d, stop)
        if stop >= 5:
            condition_gains(nc, m, d, "gains23", CONDS)
            layer2(nc, m, d, stop)
        if stop >= 7:
            layer3(nc, m, d, stop)
        with Stage(nc, "end") as st:
            stored = st.sem("stored")
            with nc.Block() as block:
                @block.sync
                def _(sp):
                    sp.dma_start(out, m.xT[:]).then_inc(stored, 16)
                    sp.wait_ge(stored, 16)


def layer0(nc, m, d, stop):
    with ExitStack() as ctx:
        w_qk = ctx.enter_context(nc.sbuf_tensor("l0_w_qk", [P, CT, 2 * GROUPS * P], F32))
        w_v = ctx.enter_context(nc.sbuf_tensor("l0_w_v", [P, CT, C], F32))
        w_o = ctx.enter_context(nc.sbuf_tensor("l0_w_o", [P, CT, C], F32))
        t_qk, t_v, t_o = (ctx.enter_context(nc.sbuf_tensor(f"l0_t_{n}", [P, CT, w], BF16))
                          for n, w in (("qk", 2 * GROUPS * P), ("v", C), ("o", C)))
        mean = ctx.enter_context(nc.sbuf_tensor("l0_mean", [P, 2], F32))
        xq = ctx.enter_context(nc.sbuf_tensor("l0_xq", [P, CT, NT], BF16))
        load(nc, "l0_load", [(w_qk[:], d["l0_w_qk"]), (w_v[:], d["l0_w_v"]), (w_o[:], d["l0_w_o"])])
        quantize_weights(nc, m, "l0_ternary", [([(w_qk[:], t_qk[:]), (w_v[:], t_v[:])], 3 * C * C), ([(w_o[:], t_o[:])], C * C)], mean)
        apply_condition(nc, m, "l0_cond", 0, tok=True)
        quantize_tokens(nc, m, "l0_quant", m.tok, xq, C)
        attention_small_heads(nc, m, d, "l0_attn", xq, t_qk, t_v, True, 16 ** -0.5, mean=mean[:, 0:1])
        quantize_tokens(nc, m, "l0_quant2", m.tok, xq, C)
        add_product(nc, m, "l0_out", t_o, xq, mean=mean[:, 1:2])
    if stop < 2:
        return
    with Stage(nc, "l0f") as st:
        w_g, w_a, w_b = st.sb("w_g", [P, CT, L0_E]), st.sb("w_a", [P, CT, L0_E * L0_R]), st.sb("w_b", [P, 4, C])
        select = st.sb("select", [L0_E, 4, P])
        gates, inner = st.sb("gates", [P, 4, NT]), st.sb("inner", [P, 4, NT])
        load(nc, "l0_load2", [(w_g[:], d["l0_w_g"]), (w_a[:], d["l0_w_a"]), (w_b[:], d["l0_w_b"]), (select[:], d["l0_select"])])
        apply_condition(nc, m, "l0_cond2", 1)
        argmax_gates(nc, m, d, "l0_gates", w_g, select, gates)
        gated_inner(nc, m, "l0_inner", w_a, gates, inner)
        add_product(nc, m, "l0_down", w_b, inner)


L1_SH = 512


def layer1(nc, m, d, stop):
    if stop < 3:
        return
    with Stage(nc, "l1a") as st:
        w_q, w_k, w_v = (st.sb(n, [P, CT, NH * P]) for n in ("w_q", "w_k", "w_v"))
        w_o = st.sb("w_o", [P, NH, C])
        load(nc, "l1_load", [(w_q[:], d["l1_w_q"]), (w_k[:], d["l1_w_k"]), (w_v[:], d["l1_w_v"]), (w_o[:], d["l1_w_o"])])
        apply_condition(nc, m, "l1_cond", 2)
        attention_wide_heads(nc, m, d, "l1_attn", w_q, w_k, w_v, w_o)
    if stop < 4:
        return
    with Stage(nc, "l1f") as st:
        w_g, bias = st.sb("w_g", [P, CT, E]), st.sb("bias", [P, E])
        w_su, w_sd = st.sb("w_su", [P, CT, L1_SH]), st.sb("w_sd", [P, L1_SH // P, C])
        inner = st.sb("inner", [P, L1_SH // P, NT])
        r = Routing(st, 6, m.moves_1)
        load(nc, "l1_load2", [(w_g[:], d["l1_w_g"]), (bias[:], d["l1_bias"]), (w_su[:], d["l1_w_su"]), (w_sd[:], d["l1_w_sd"])])
        apply_condition(nc, m, "l1_cond2", 3, tok=True)
        route(nc, m, d, "l1_route", w_g, bias, r, 64, MASKED)
        dispatch(nc, m, "l1_dispatch", r, m.slots_in_1, w_su, None, w_sd, inner, P)
        experts(nc, m, "l1_experts", m.slots_in_1, m.slots_out_1, d["l1_w_e"], 2, P, False)
        combine(nc, m, "l1_combine", r, m.slots_out_1)


L2_I = 88


def layer2(nc, m, d, stop):
    with Stage(nc, "l2a") as st:
        w, bias, w_o, b_o = st.sb("w", [P, CT, 3 * C]), st.sb("bias", [P, 3 * C]), st.sb("w_o", [P, CT, C]), st.sb("b_o", [P, CT])
        qkv = st.sb("qkv", [P, TT, 3 * C])
        load(nc, "l2_load", [(w[:], d["l2_w"]), (bias[:], d["l2_bias"]), (w_o[:], d["l2_w_o"]), (b_o[:], d["l2_b_o"])])
        apply_condition(nc, m, "l2_cond", 0)
        qkv_tokens(nc, m, "l2_qkv", w, bias, qkv)
        attention_over_batch(nc, m, d, "l2_attn", qkv)
        turn_tokens(nc, m, "l2_turn")
        add_product(nc, m, "l2_out", w_o, m.hT, bias=b_o)
    if stop < 6:
        return
    with Stage(nc, "l2f") as st:
        w_g, bias = st.sb("w_g", [P, CT, E]), st.sb("bias", [P, E])
        w_sg, w_su = st.sb("w_sg", [P, CT, L2_I]), st.sb("w_su", [P, CT, L2_I])
        w_sd, inner = st.sb("w_sd", [L2_I, 1, C]), st.sb("inner", [L2_I, 1, NT])
        r = Routing(st, 8, m.moves_2)
        load(nc, "l2_load2", [(w_g[:], d["l2_w_g"]), (bias[:], d["l2_ebias"]), (w_sg[:], d["l2_w_sg"]), (w_su[:], d["l2_w_su"]),
                              (w_sd[:], d["l2_w_sd"])])
        apply_condition(nc, m, "l2_cond2", 1, tok=True)
        route(nc, m, d, "l2_route", w_g, bias, r, 128, 0.0)
        dispatch(nc, m, "l2_dispatch", r, m.slots_in_2, w_su, w_sg, w_sd, inner, L2_I)
        experts(nc, m, "l2_experts", m.slots_in_2, m.slots_out_2, d["l2_w_e"], 1, L2_I, True)
        combine(nc, m, "l2_combine", r, m.slots_out_2)


def layer3(nc, m, d, stop):
    with Stage(nc, "l3a") as st:
        w_qk, w_v, w_o = st.sb("w_qk", [P, CT, 2 * GROUPS * P]), st.sb("w_v", [P, CT, C]), st.sb("w_o", [P, CT, C])
        low, up_qk, up_v = st.sb("low", [P, CT, P]), st.sb("up_qk", [P, GROUPS * P]), st.sb("up_v", [P, C])
        qk_bias, b_o = st.sb("qk_bias", [P, 2 * GROUPS]), st.sb("b_o", [P, CT])
        low_o, up_o, low_out = st.sb("low_o", [P, CT, 16]), st.sb("up_o", [16, C]), st.sb("low_out", [16, NT])
        m.low_bias = st.sb("low_bias", [P, 1])
        load(nc, "l3_load", [(t[:], d["l3_" + n]) for t, n in (
            (w_qk, "w_qk"), (w_v, "w_v"), (w_o, "w_o"), (low, "low"), (up_qk, "up_qk"), (up_v, "up_v"), (qk_bias, "qk_bias"),
            (b_o, "b_o"), (low_o, "low_o"), (up_o, "up_o"), (m.low_bias, "low_bias"))])
        apply_condition(nc, m, "l3_cond", 2)
        attention_small_heads(nc, m, d, "l3_attn", m.hT, w_qk, w_v, False, 16 ** -0.5, qk_bias, (low, up_qk, up_v))
        turn_tokens(nc, m, "l3_turn")
        low_rank(nc, m, "l3_low", low_o, low_out)
        add_product(nc, m, "l3_out", w_o, m.hT, bias=b_o, low=(up_o, low_out))
    if stop < 8:
        return
    with Stage(nc, "l3f") as st:
        w_g, w_u, w_d = st.sb("w_g", [P, CT, L3_I]), st.sb("w_u", [P, CT, L3_I]), st.sb("w_d", [P, L3_I // P, C])
        ln = st.sb("ln", [P, L3_I])
        t_g, t_u, t_d = (st.sb(n, w.shape, BF16) for n, w in (("t_g", w_g), ("t_u", w_u), ("t_d", w_d)))
        mean, xq = st.sb("mean", [P, 3]), st.sb("xq", [P, CT, NT], BF16)
        h, hq = st.sb("h", [P, TT, L3_I]), st.sb("hq", [P, L3_I // P, NT], BF16)
        load(nc, "l3_load2", [(w_g[:], d["l3_w_g"]), (w_u[:], d["l3_w_u"]), (w_d[:], d["l3_w_d"]), (ln[:], d["l3_ln"])])
        quantize_weights(nc, m, "l3_ternary", [([(w[:], t[:])], L3_I * C) for w, t in ((w_g, t_g), (w_u, t_u), (w_d, t_d))], mean)
        apply_condition(nc, m, "l3_cond2", 3, tok=True)
        quantize_tokens(nc, m, "l3_quant", m.tok, xq, C)
        swiglu_rms(nc, m, "l3_swiglu", xq, t_g, t_u, mean, ln, h)
        quantize_tokens(nc, m, "l3_quant2", h, hq, L3_I)
        add_product(nc, m, "l3_down", t_d, hq, mean=mean[:, 2:3])



def rows(a):
    a = np.asarray(a)
    return np.ascontiguousarray(a.reshape(-1, P, a.shape[-1]).transpose(1, 0, 2))


def spread_heads(wT):
    a = np.zeros((wT.shape[0], NH, 32), wT.dtype)
    a[:, :, :16] = wT.reshape(-1, NH, 16)
    return a.reshape(wT.shape[0], -1)


def at_rows(*blocks):
    a = np.zeros((P, blocks[0][1].shape[1]), np.float32)
    for r, b in blocks:
        a[r:r + b.shape[0]] = b
    return a


def layouts(i):
    conds = [f"L{l}_cond{n}_" for l in range(4) for n in ("", "2")]
    i = {k: np.asarray(v) for k, v in i.items()}
    qkv = i["L0_attn_w_qkv"].T
    row, col = np.arange(P)[:, None], np.arange(P)[None, :]
    bf16 = np.dtype("bfloat16")
    freq = (np.float32(1) / np.float32(10000) ** (np.arange(0, P, 2, dtype=np.float32) / np.float32(P))).astype(np.float32)
    angle = np.tile((np.arange(T, dtype=np.float32)[:, None] * freq).T, (2, 1))
    freq2 = (np.float32(1) / np.float32(10000) ** (np.arange(0, L2_D, 2, dtype=np.float32) / np.float32(L2_D))).astype(np.float32)
    angle2 = np.tile(np.arange(B, dtype=np.float32)[:, None] * freq2, (1, 2))
    causal, window = np.where(col <= row, 0, MASKED), np.where(col > row, 0, MASKED)
    return {
        "xT": rows(i["x"].reshape(NT, C).T),
        "fsideT": rows(i["fside_BxSxS_0"].reshape(NT, C).T),
        "condT": np.ascontiguousarray(i["cond_512"].T),
        "wu": np.ascontiguousarray(np.stack([np.stack([i[c + k].reshape(CT, P).T for c in conds], 1) for k in "wu"], 1)),
        "ident": np.eye(P, dtype=np.float32), "ones": np.ones((P, P), np.float32),
        "ident_b": np.eye(P).astype(bf16),
        "mask_causal": np.concatenate([causal, 0 * causal, causal], 1).astype(bf16),
        "mask_window": np.concatenate([causal, window, causal], 1).astype(bf16),
        "l0_w_qk": rows(np.concatenate([spread_heads(qkv[:, :C]), spread_heads(qkv[:, C:2 * C])], 1)),
        "l0_w_v": rows(qkv[:, 2 * C:]),
        "l0_w_o": rows(i["L0_attn_w_proj"].T),
        "rank8": np.broadcast_to(np.arange(L0_E, 0, -1, dtype=np.float32), (P, L0_E)).copy(),
        "l0_w_g": rows(i["L0_ffn_Wg"].T),
        "l0_w_a": rows(i["L0_ffn_A"].reshape(L0_E * L0_R, C).T),
        "l0_w_b": rows(i["L0_ffn_Bw"].transpose(0, 2, 1).reshape(L0_E * L0_R, C)),
        "l0_select": (np.arange(L0_E)[:, None, None] == 2 * np.arange(4)[None, :, None] + np.arange(P)[None, None, :] // L0_R).astype(np.float32),
        "l1_w_q": rows(i["L1_attn_wq"]), "l1_w_k": rows(i["L1_attn_wk"]), "l1_w_v": rows(i["L1_attn_wv"]),
        "l1_w_o": rows(i["L1_attn_wo"]),
        "ones_b": np.ones((P, P), bf16), "earlier": (row < col).astype(bf16),
        "iota": np.broadcast_to(np.arange(E, dtype=np.float32), (P, E)).copy(),
        "l1_w_g": rows(i["L1_ffn_gate_w"].T), "l1_bias": np.broadcast_to(i["L1_ffn_e_bias"], (P, E)).copy(),
        "l1_w_su": rows(i["L1_ffn_shared_up_w"].T), "l1_w_sd": rows(i["L1_ffn_shared_down_w"].T),
        "l1_w_e": np.concatenate([i["L1_ffn_w1"].reshape(32, 2, P, CT, P).transpose(0, 4, 1, 3, 2).reshape(32, P, -1),
                                  i["L1_ffn_w2"].reshape(32, 2, C, P).transpose(0, 3, 1, 2).reshape(32, P, -1)], 2),
        "l2_w": rows(i["L2_attn_qkv_w"]), "l2_bias": np.broadcast_to(i["L2_attn_qkv_b"], (P, 3 * C)).copy(),
        "l2_w_o": rows(i["L2_attn_out_w"]), "l2_b_o": np.ascontiguousarray(i["L2_attn_out_b"].reshape(CT, P).T),
        "l2_cos": np.broadcast_to(np.cos(angle2).astype(np.float32), (P, B, L2_D)).copy(),
        "l2_sin": np.broadcast_to((np.sin(angle2) * np.repeat([-1, 1], L2_D // 2)).astype(np.float32), (P, B, L2_D)).copy(),
        "l2_w_g": rows(i["L2_ffn_router_weight"].T), "l2_ebias": np.broadcast_to(i["L2_ffn_e_bias"], (P, E)).copy(),
        "l2_w_sg": rows(i["L2_ffn_sh_gate"]), "l2_w_su": rows(i["L2_ffn_sh_up"]), "l2_w_sd": i["L2_ffn_sh_down"][:, None, :],
        "l2_w_e": np.concatenate([i["L2_ffn_w_" + n].reshape(E, CT, P, L2_I).transpose(0, 2, 1, 3).reshape(E, P, -1)
                                  for n in ("up", "gate")] + [np.pad(i["L2_ffn_w_down"], ((0, 0), (0, P - L2_I), (0, 0)))], 2),
        "l3_w_qk": rows(np.concatenate([spread_heads(i["L3_attn_Wq"].T), spread_heads(i["L3_attn_Wk"].T)], 1)),
        "l3_w_v": rows(i["L3_attn_Wv"].T), "l3_w_o": rows(i["L3_attn_Wo"].T),
        "l3_low": rows(np.concatenate([np.pad(i[f"L3_attn_B{k}"].T, ((0, 0), (0, 16))) for k in "qkv"] + [np.zeros((C, 32), np.float32)], 1)),
        "l3_up_qk": at_rows((0, spread_heads(i["L3_attn_Aq"].T)), (32, spread_heads(i["L3_attn_Ak"].T))),
        "l3_up_v": at_rows((64, i["L3_attn_Av"].T), (80, i["L3_attn_bv"][None])),
        "l3_qk_bias": np.concatenate([spread_heads(i[f"L3_attn_b{k}"][None]).reshape(GROUPS, P).T for k in "qk"], 1).copy(),
        "l3_b_o": np.ascontiguousarray(i["L3_attn_bo"].reshape(CT, P).T),
        "l3_low_o": rows(i["L3_attn_Bo"].T), "l3_up_o": np.ascontiguousarray(i["L3_attn_Ao"].T),
        "l3_low_bias": at_rows((80, np.ones((1, 1), np.float32))),
        "l3_w_g": rows(i["L3_ffn_w_gate"].T), "l3_w_u": rows(i["L3_ffn_w_up"].T), "l3_w_d": rows(i["L3_ffn_w_down"].T),
        "l3_ln": np.broadcast_to(i["L3_ffn_ln_weight"], (P, L3_I)).copy(),
        "l1_cos": np.cos(angle).astype(np.float32),
        "l1_sin": np.concatenate([np.sin(angle[:64]), -np.sin(angle[64:])]).astype(np.float32),
    }


def kernel(**inputs):
    import concourse.bacc as bacc
    from concourse.bass_utils import run_bass_kernel_spmd as run
    arrays = layouts(inputs)
    nc = bacc.Bacc("TRN2", target_bir_lowering=False, num_devices=1)
    d = {k: nc.dram_tensor("in_" + k, v.shape, mybir.dt.from_np(v.dtype), kind="ExternalInput").ap()
         for k, v in arrays.items()}
    out = nc.dram_tensor("out", (P, CT, NT), F32, kind="ExternalOutput").ap()
    build(nc, Core(), d, out)
    r = run(nc, [{"in_" + k: v for k, v in arrays.items()}], core_ids=[0])
    return np.ascontiguousarray(r.results[0]["out"].transpose(1, 0, 2).reshape(C, NT).T.reshape(B, T, C))
```

```python
import numpy as np
from contextlib import ExitStack

import concourse.bass as bass
from concourse import mybir

F32 = mybir.dt.float32
BF16 = mybir.dt.bfloat16
U32 = mybir.dt.uint32
ALU = mybir.AluOpType
ACT = mybir.ActivationFunctionType
AX = mybir.AxisListType

P = 128
B, T, C = 4, 256, 256
NT = B * T
CT = C // P
TT = NT // P
HALF = 512
NH = 16
HG = 4
GROUPS = NH // HG
CONDS = 4
ROUND = 1.5 * 2.0 ** 23
MASKED = -1e30
LEAST = 1e-8


class Tally:

    def __init__(self, eng, sem):
        self.eng, self.sem, self.n, self.base = eng, sem, 0, None

    def value(self):
        return self.n if self.base is None else self.base + self.n

    def link(self, ins):
        ins.then_inc(self.sem, 1)
        self.n += 1
        self.eng.wait_ge(self.sem, self.value())

    def enter(self, turn, per):
        self.before, self.per, self.base, self.n = self.n, per, turn * per + self.n, 0

    def leave(self, turns):
        assert self.n == self.per, (self.n, self.per)
        self.base, self.n = None, self.before + turns * self.per


class Stage:

    def __init__(self, nc, name):
        self.nc, self.name, self.stack, self.sems = nc, name, ExitStack(), []

    def __enter__(self):
        return self

    def __exit__(self, *e):
        for s in self.sems:
            self.nc.sync.sem_clear(s)
        self.stack.close()

    def sb(self, name, shape, dt=F32):
        return self.stack.enter_context(self.nc.sbuf_tensor(f"{self.name}_{name}", shape, dt))

    def ps(self, name, shape, dt=F32):
        return self.stack.enter_context(self.nc.psum_tensor(f"{self.name}_{name}", shape, dt))

    def sem(self, name):
        self.sems.append(self.stack.enter_context(self.nc.semaphore(f"{self.name}_{name}")))
        return self.sems[-1]


class Core:
    pass



def load_constants(nc, m, d):
    with Stage(nc, "start") as st:
        loaded = st.sem("loaded")
        pairs = [(m.xT, "xT"), (m.ident, "ident"), (m.ones, "ones"), (m.wu, "wu"), (m.condT, "condT"),
             (m.ident_b, "ident_b"), (m.mask_causal, "mask_causal"), (m.mask_window, "mask_window"),
             (m.ones_b, "ones_b"), (m.earlier, "earlier"), (m.iota, "iota"), (m.rank, "rank8")]
        with nc.Block() as block:
            @block.sync
            def _(sp):
                for tile, name in pairs:
                    sp.dma_start(tile[:], d[name]).then_inc(loaded, 16)
                sp.wait_ge(loaded, 16 * len(pairs))


def condition_gains(nc, m, d, name, first, combining=None):
    with Stage(nc, name) as st:
        if first == 0:
            zeros, zeroed, filled = st.sb("zeros", [P, 1024]), st.sem("zeroed"), st.sem("filled")
        kT, ek, ekv = (st.sb(n, [P, CT, NT]) for n in ("kT", "ek", "ekv"))
        dec, dw, dw2 = st.sb("dec", [P, CONDS, CT, B]), st.sb("dw", [P, CONDS, CT]), st.sb("dw2", [P, CONDS, CT])
        tf, dfac, ofac = st.sb("tf", [P, B]), st.sb("dfac", [P, B]), st.sb("ofac", [P, B])
        eps = st.sb("eps", [P, 2])
        z, zv, rd, seed = (st.sb(n, [P, 2, NT]) for n in ("z", "zv", "rd", "seed"))
        sc = st.sb("sc", [P, 2, 4, NT])
        num, den = st.ps("num", [P, 2, NT]), st.ps("den", [P, 2, NT])
        (loaded, own_dve, capped, ek_ready, dw_ready, w_ready, tf_sum, tf_ready, uk_ready, euk_ready,
         z_ready, zv_ready, scans_ready, sums_ready, eps_ready, seeded, gain_ready, own_act) = (
            st.sem(n) for n in ("loaded", "own_dve", "capped", "ek", "dw", "w", "tf_sum", "tf", "uk", "euk",
                                "z", "zv", "scans", "sums", "eps", "seeded", "gain", "own_act"))
        w = m.wu[:, 0, first:first + CONDS, :]
        with nc.Block() as block:
            @block.sync
            def _(sp):
                sp.dma_start(kT[:], d["fsideT"]).then_inc(loaded, 16)
                if first == 0:
                    sp.wait_ge(zeroed, 1)
                    n = 0
                    for slots in (m.slots_in_1, m.slots_in_2):
                        flat = slots.rearrange("(p r) c -> p (r c)", p=P)
                        for c in range(0, flat.shape[1], zeros.shape[1]):
                            sp.dma_start(flat[:, c:c + zeros.shape[1]], zeros[:, :]).then_inc(filled, 16)
                            n += 1
                    sp.wait_ge(filled, 16 * n)

            @block.tensor
            def _(pe):
                nc.tensor.matmul(num[:, 0, 0:B], m.ones[0:64, :], m.condT[:, :], start=True, stop=True).then_inc(tf_sum, 1)
                pe.wait_ge(tf_ready, 1)

                def add_up(i, ct, early):
                    s = i * CT + ct
                    pe.wait_ge(scans_ready, s + 1)
                    pe.wait_ge(zv_ready, s + 1)
                    if not early:
                        pe.wait_ge(gain_ready, s - 1)
                    for acc, terms in ((num, (sc[:, ct, 0], sc[:, ct, 1], zv[:, ct])),
                                       (den, (sc[:, ct, 2], sc[:, ct, 3], z[:, ct]))):
                        for c in range(0, NT, HALF):
                            for n, t in enumerate(terms):
                                last = nc.tensor.matmul(acc[:, ct, c:c + HALF], m.ident[:, :], t[:, c:c + HALF],
                                                        start=n == 0, stop=n == 2)
                    last.then_inc(sums_ready, 1)
                add_up(0, 0, True)
                add_up(0, 1, True)
                with pe.Fori(1, CONDS, 1) as i:
                    add_up(i, 0, False)
                    add_up(i, 1, False)
                if combining:
                    pe.wait_ge(gain_ready, CONDS * CT)
                    combining.turn(pe, num)

            @block.scalar
            def _(act):
                nc.scalar.activation(dw[:, :, :], w, ACT.Exp).then_inc(dw_ready, 1)
                act.wait_ge(dw_ready, 1)
                nc.scalar.activation(dw2[:, :, :], dw[:, :, :], ACT.Exp, scale=-1.0).then_inc(w_ready, 1)
                act.wait_ge(tf_sum, 1)
                nc.scalar.activation(tf[:, :], num[:, 0, 0:B], ACT.Sigmoid).then_inc(tf_ready, 1)
                act.wait_ge(capped, 1)
                act.wait_ge(eps_ready, 1)
                nc.scalar.activation(ek[:, :, :], ek[:, :, :], ACT.Exp).then_inc(ek_ready, 1)

                def exp_uk(i, ct, early):
                    s = i * CT + ct
                    act.wait_ge(uk_ready, s + 1)
                    nc.scalar.activation(z[:, ct], z[:, ct], ACT.Exp).then_inc(euk_ready, 1)

                def seed_inverse(i, ct):
                    s = i * CT + ct
                    act.wait_ge(sums_ready, s + 1)
                    nc.scalar.activation(rd[:, ct], den[:, ct], ACT.Relu, bias=eps[:, 0:1]).then_inc(own_act, 1)
                    act.wait_ge(own_act, 2 * s + 1)
                    nc.scalar.activation(seed[:, ct], rd[:, ct], ACT.Ln, bias=eps[:, 1:2]).then_inc(own_act, 1)
                    act.wait_ge(own_act, 2 * s + 2)
                    nc.scalar.activation(seed[:, ct], seed[:, ct], ACT.Exp, scale=-1.0).then_inc(seeded, 1)
                exp_uk(0, 0, True)
                exp_uk(0, 1, True)
                with act.Fori(1, CONDS, 1) as i:
                    seed_inverse(i - 1, 0)
                    exp_uk(i, 0, False)
                    seed_inverse(i - 1, 1)
                    exp_uk(i, 1, False)
                seed_inverse(CONDS - 1, 0)
                seed_inverse(CONDS - 1, 1)

            @block.gpsimd
            def _(pool):
                if first == 0:
                    nc.gpsimd.memset(zeros[:, :], 0.0).then_inc(zeroed, 1)
                if combining:
                    combining.gather(pool, 0)
                pool.wait_ge(ek_ready, 1)

                def own_token(i, ct, early):
                    s = i * CT + ct
                    pool.wait_ge(euk_ready, s + 1)
                    if not early:
                        pool.wait_ge(sums_ready, s - 1)
                    nc.gpsimd.tensor_tensor(z[:, ct], z[:, ct], ek[:, ct], ALU.subtract).then_inc(z_ready, 1)
                    pool.wait_ge(z_ready, s + 1)
                    nc.gpsimd.tensor_tensor(zv[:, ct], z[:, ct], kT[:, ct], ALU.mult).then_inc(zv_ready, 1)
                own_token(0, 0, True)
                own_token(0, 1, True)
                if combining:
                    combining.gather(pool, 1)
                    for i in range(1, CONDS):
                        for ct in range(CT):
                            own_token(i, ct, False)
                            if 2 * i + ct < combining.K:
                                combining.gather(pool, 2 * i + ct)
                else:
                    with pool.Fori(1, CONDS, 1) as i:
                        own_token(i, 0, False)
                        own_token(i, 1, False)

            @block.vector
            def _(dve):
                own = Tally(dve, own_dve)
                dve.memset(eps[:, 0:1], -LEAST)
                dve.memset(eps[:, 1:2], LEAST).then_inc(eps_ready, 1)
                if combining:
                    assert combining.K == CT * (CONDS - 1)
                    combining.clear(dve)
                dve.wait_ge(loaded, 16)
                nc.vector.tensor_scalar(ek[:, :, :], kT[:, :, :], 30.0, None, ALU.min).then_inc(capped, 1)
                dve.wait_ge(tf_ready, 1)
                nc.vector.tensor_scalar(ofac[:, :], tf[:, :], 0.2, 0.8, ALU.mult, ALU.add)
                own.link(nc.vector.tensor_scalar(dfac[:, :], tf[:, :], 0.5, 0.5, ALU.mult, ALU.add))
                dve.wait_ge(w_ready, 1)
                for b in range(B):
                    last = nc.vector.tensor_scalar(dec[:, :, :, b], dw2[:, :, :], dfac[:, b:b + 1], None, ALU.mult)
                own.link(last)
                dve.wait_ge(ek_ready, 1)
                own.link(nc.vector.tensor_tensor(ekv[:, :, :], ek[:, :, :], kT[:, :, :], ALU.mult))

                def scans(i, ct, early):
                    s = i * CT + ct
                    if not early:
                        dve.wait_ge(sums_ready, s - 1)
                    nc.vector.tensor_scalar(z[:, ct], kT[:, ct], m.wu[:, 1, bass.ds(first + i, 1), ct], 30.0,
                                            ALU.add, ALU.min).then_inc(uk_ready, 1)
                    for b in range(B):
                        decay = dec[:, bass.ds(i, 1), ct, b].broadcast_to([P, T])
                        ahead = slice(b * T, b * T + T)
                        back = slice(b * T + T - 1, b * T - 1 if b else None, -1)
                        for n, src in enumerate((ekv, ek)):
                            nc.vector.tensor_tensor_scan(sc[:, ct, 2 * n, ahead], decay, src[:, ct, ahead], 0.0,
                                                         ALU.mult, ALU.add)
                            last = nc.vector.tensor_tensor_scan(sc[:, ct, 2 * n + 1, back], decay, src[:, ct, back],
                                                                0.0, ALU.mult, ALU.add)
                    last.then_inc(scans_ready, 1)

                def gains(i, ct):
                    s = i * CT + ct
                    dve.wait_ge(seeded, s + 1)
                    own.link(nc.vector.scalar_tensor_tensor(out=rd[:, ct], in0=rd[:, ct], scalar=LEAST, in1=seed[:, ct],
                                                            op0=ALU.add, op1=ALU.mult))
                    own.link(nc.vector.scalar_tensor_tensor(out=rd[:, ct], in0=rd[:, ct], scalar=2.0, in1=seed[:, ct],
                                                            op0=ALU.subtract, op1=ALU.mult))
                    for b in range(B):
                        t = slice(b * T, b * T + T)
                        last = nc.vector.scalar_tensor_tensor(
                            out=m.gain[:, bass.ds(i, 1), ct, t], in0=num[:, ct, t], scalar=ofac[:, b:b + 1],
                            in1=rd[:, ct, t], op0=ALU.mult, op1=ALU.mult)
                    last.then_inc(gain_ready, 1)
                own.link(nc.vector.tensor_scalar(ofac[:, :], ofac[:, :], -1.0, None, ALU.mult))
                scans(0, 0, True)
                scans(0, 1, True)
                with dve.Fori(1, CONDS, 1) as i:
                    own.enter(i - 1, 4)
                    scans(i, 0, False)
                    gains(i - 1, 0)
                    if combining:
                        combining.add(dve, 2 * i - 2, i, 0)
                    scans(i, 1, False)
                    gains(i - 1, 1)
                    if combining:
                        combining.add(dve, 2 * i - 1, i, 1)
                own.leave(CONDS - 1)
                gains(CONDS - 1, 0)
                gains(CONDS - 1, 1)
                if combining:
                    combining.finish(dve, num)


def apply_condition(nc, m, name, i, tok=False):
    with Stage(nc, name) as st:
        sig = st.sb("sig", [P, CT, NT])
        sig_ready, h_ready, turned = st.sem("sig"), st.sem("h"), st.sem("turned")
        tp = st.ps("tp", [P, TT, C]) if tok else None
        with nc.Block() as block:
            @block.scalar
            def _(act):
                for ct in range(CT):
                    nc.scalar.activation(sig[:, ct], m.xT[:, ct], ACT.Sigmoid).then_inc(sig_ready, 1)
                if tok:
                    for half in range(2):
                        act.wait_ge(turned, half + 1)
                        j = slice(half * TT // 2, (half + 1) * TT // 2)
                        nc.scalar.activation(m.tok[:, j, :], tp[:, j, :], ACT.Copy)

            @block.vector
            def _(dve):
                for ct in range(CT):
                    dve.wait_ge(sig_ready, ct + 1)
                    nc.vector.tensor_tensor(m.hT[:, ct], sig[:, ct], m.gain[:, i, ct], ALU.mult).then_inc(h_ready, 1)

            @block.tensor
            def _(pe):
                if tok:
                    pe.wait_ge(h_ready, CT)
                    for j in range(TT):
                        for ct in range(CT):
                            last = nc.tensor.transpose(tp[:, j, ct * P:(ct + 1) * P], m.hT[:, ct, j * P:(j + 1) * P],
                                                       m.ident[:, :])
                        if j % (TT // 2) == TT // 2 - 1:
                            last.then_inc(turned, 1)



def quantize_tokens(nc, m, name, tok, qT, feats, known=None):
    KT = feats // P
    per = HALF // P
    with Stage(nc, name) as st:
        amax, s = st.sb("amax", [P, TT]), st.sb("s", [P, TT])
        tp, row = st.ps("tp", [P, 4, HALF]), st.ps("row", [P, NT])
        own_dve, s_inv, s_row, quantized, turned = (st.sem(n) for n in ("own_dve", "inv", "row", "quantized", "turned"))
        moved = [st.sem("moved_by_dve"), st.sem("moved_by_act")]
        banks = [(k, h) for h in range(TT // per) for k in range(KT)]
        with nc.Block() as block:
            @block.vector
            def _(dve):
                own = Tally(dve, own_dve)
                if known is None:
                    own.link(nc.vector.tensor_reduce(amax[:, :], tok[:, :, :], AX.X, ALU.max, apply_absolute_value=True))
                else:
                    own.link(nc.vector.tensor_tensor(amax[:, :], known[0][:, :], known[1][:, :], ALU.mult))
                own.link(nc.vector.tensor_scalar(amax[:, :], amax[:, :], 1e-5, None, ALU.max))
                nc.vector.tensor_scalar(m.inv[:, :], amax[:, :], 1.0 / 127.0, None, ALU.mult).then_inc(s_inv, 1)
                own.link(nc.vector.reciprocal(s[:, :], amax[:, :]))
                own.link(nc.vector.tensor_scalar(s[:, :], s[:, :], 127.0, None, ALU.mult))
                if known is not None:
                    own.link(nc.vector.tensor_tensor(s[:, :], s[:, :], known[1][:, :], ALU.mult))
                for j in range(TT):
                    nc.vector.tensor_scalar(tok[:, j, :], tok[:, j, :], s[:, j:j + 1], ROUND, ALU.mult,
                                            ALU.add).then_inc(quantized, 1)
                for n, (k, h) in enumerate(banks):
                    if n % 2 == 0:
                        dve.wait_ge(turned, n + 1)
                        nc.vector.tensor_scalar(qT[:, k, h * HALF:(h + 1) * HALF], tp[:, n % 4, :], ROUND, None,
                                                ALU.subtract).then_inc(moved[0], 1)

            @block.scalar
            def _(act):
                act.wait_ge(s_row, 1)
                nc.scalar.activation(m.inv_row[:, :], row[:, :], ACT.Copy)
                for n, (k, h) in enumerate(banks):
                    if n % 2:
                        act.wait_ge(turned, n + 1)
                        nc.scalar.activation(qT[:, k, h * HALF:(h + 1) * HALF], tp[:, n % 4, :], ACT.Copy,
                                             bias=-ROUND).then_inc(moved[1], 1)

            @block.tensor
            def _(pe):
                pe.wait_ge(s_inv, 1)
                for j in range(TT):
                    last = nc.tensor.matmul(row[:, j * P:(j + 1) * P], m.inv[:, j:j + 1].broadcast_to([P, P]), m.ident[:, :],
                                            start=True, stop=True)
                last.then_inc(s_row, 1)
                for n, (k, h) in enumerate(banks):
                    pe.wait_ge(quantized, (h + 1) * per)
                    if n >= 4:
                        pe.wait_ge(moved[n % 2], (n - 4) // 2 + 1)
                    for j in range(per):
                        last = nc.tensor.transpose(tp[:, n % 4, j * P:(j + 1) * P],
                                                   tok[:, h * per + j, k * P:(k + 1) * P], m.ident[:, :])
                    last.then_inc(turned, 1)


class Ternary:

    def __init__(self, st, m, groups, mean):
        self.m, self.groups, self.mean = m, groups, mean
        self.views = [(w, wq, g) for g, (ws, _) in enumerate(groups) for w, wq in ws]
        self.part = st.sb("part", [P, len(self.views)])
        self.s = st.sb("s", [P, len(groups)])
        self.total = st.ps("total", [P, len(groups)])
        self.own_dve, self.parts, self.summed = (st.sem(k) for k in ("own_dve", "parts", "summed"))

    def quantize(self, dve):
        own, s, mean = Tally(dve, self.own_dve), self.s, self.mean
        for i, (w, _, _) in enumerate(self.views):
            last = dve.tensor_reduce(self.part[:, i:i + 1], w, AX.XY, ALU.add, apply_absolute_value=True)
        last.then_inc(self.parts, 1)
        dve.wait_ge(self.summed, 1)
        for g, (_, count) in enumerate(self.groups):
            last = dve.tensor_scalar(mean[:, g:g + 1], self.total[:, g:g + 1], 1.0 / count, 1e-5, ALU.mult, ALU.max)
        own.link(last)
        own.link(dve.reciprocal(s[:, :], mean[:, :]))
        for step in range(3):
            for w, wq, g in self.views:
                if step == 0:
                    last = dve.tensor_scalar(w, w, s[:, g:g + 1], ROUND, ALU.mult, ALU.add)
                elif step == 1:
                    last = dve.tensor_scalar(w, w, ROUND, 1.0, ALU.subtract, ALU.min)
                else:
                    last = dve.tensor_scalar(wq, w, -1.0, None, ALU.max)
            own.link(last)

    def add_up(self, pe):
        pe.wait_ge(self.parts, 1)
        for g in range(len(self.groups)):
            mine = [i for i, (_, _, g_) in enumerate(self.views) if g_ == g]
            for i in mine:
                last = pe.matmul(self.total[:, g:g + 1], self.m.ones[:, :], self.part[:, i:i + 1], start=i == mine[0],
                                 stop=i == mine[-1])
        last.then_inc(self.summed, 1)


def quantize_weights(nc, m, name, groups, mean):
    with Stage(nc, name) as st:
        t = Ternary(st, m, groups, mean)
        with nc.Block() as block:
            @block.vector
            def _(dve):
                t.quantize(dve)

            @block.tensor
            def _(pe):
                t.add_up(pe)


class Weights(Stage):

    def start(self, *pairs):
        self.loaded = [self.sem(f"loaded{i}") for i in range(len(pairs))]
        with self.nc.Block() as block:
            @block.sync
            def _(sp):
                for (tile, src), loaded in zip(pairs, self.loaded):
                    sp.dma_start(tile, src).then_inc(loaded, 16)

    def arrive(self):
        with self.nc.Block() as block:
            @block.sync
            def _(sp):
                for loaded in self.loaded:
                    sp.wait_ge(loaded, 16)





IN_FLIGHT = 3
LAG = 2
WEIGH = 4


class Heads:

    def __init__(self, st, banks, causal):
        self.blocks = [(0, 0), (1, 0), (1, 1)] if causal else [(0, 0), (0, 1), (1, 0), (1, 1)]
        self.causal = causal
        self.split = P if causal else 2 * P
        self.width = len(self.blocks) * P
        self.turned, self.scores = banks[:, 0:2, :], banks[:, 2:2 + IN_FLIGHT, :]
        self.probs = st.sb("probs", [P, IN_FLIGHT, self.width])
        self.probsT = st.sb("probsT", [P, IN_FLIGHT, self.width])
        self.top, self.bias, self.total = (st.sb(n, [P, 2 * NH, 2]) for n in ("top", "bias", "total"))
        (self.s_scores, self.s_bias, self.s_turned, self.s_out, self.s_norm) = (
            st.sem(n) for n in ("scores_ready", "bias_ready", "turned_ready", "out_ready", "norm_ready"))
        self.s_moved = [st.sem("moved_by_dve"), st.sem("moved_by_act")]

    def tiles(self):
        return ((0, slice(0, self.split)), (1, slice(self.split, self.width)))

    def score(self, pe, turn, h, q, k, ident=None, mask=None):
        if h >= IN_FLIGHT:
            pe.wait_ge(self.s_norm, turn + h - IN_FLIGHT + 1)
        for nt, cols in self.tiles():
            into = self.scores[:, h % IN_FLIGHT, cols]
            if self.causal:
                pe.matmul(into, ident, mask[:, cols], start=True, stop=False)
            last = pe.matmul(into, q[:, nt * P:(nt + 1) * P], k[:, 0:cols.stop - cols.start],
                             start=not self.causal, stop=True)
        last.then_inc(self.s_scores, 1)

    def turn(self, pe, turn, h, ident):
        pe.wait_ge(self.s_norm, turn + h + 1)
        if h >= 2:
            pe.wait_ge(self.s_moved[h % 2], turn // 2 + (h - 2) // 2 + 1)
        for n in range(len(self.blocks)):
            last = pe.transpose(self.turned[:, h % 2, n * P:(n + 1) * P], self.probs[:, h % IN_FLIGHT, n * P:(n + 1) * P], ident)
        last.then_inc(self.s_turned, 1)

    def top_of(self, dve, own, turn, h, scale, scales=None):
        dve.wait_ge(self.s_scores, turn + h + 1)
        if self.causal:
            for nt, cols in self.tiles():
                last = dve.tensor_reduce(self.top[:, h % (2 * NH), nt:nt + 1], self.scores[:, h % IN_FLIGHT, cols], AX.X, ALU.max)
            own.link(last)
        else:
            own.link(dve.tensor_reduce(self.top[:, h % (2 * NH), :], self.scores[:, h % IN_FLIGHT, :].rearrange("p (n k) -> p n k", n=2),
                                       AX.X, ALU.max))
        if scales is None:
            dve.tensor_scalar(self.bias[:, h % (2 * NH), :], self.top[:, h % (2 * NH), :], -scale, None, ALU.mult).then_inc(self.s_bias, 1)
        else:
            dve.tensor_tensor(self.bias[:, h % (2 * NH), :], self.top[:, h % (2 * NH), :], scales, ALU.mult).then_inc(self.s_bias, 1)

    def move(self, eng, copy, turn, h):
        eng.wait_ge(self.s_turned, turn + h + 1)
        if h >= IN_FLIGHT:
            eng.wait_ge(self.s_out, turn + h - IN_FLIGHT + 1)
        copy(self.probsT[:, h % IN_FLIGHT, 0:self.width], self.turned[:, h % 2, 0:self.width]).then_inc(self.s_moved[h % 2], 1)

    def exp(self, act, turn, h, scale, ready, scales=None):
        act.wait_ge(self.s_bias, turn + h + 1)
        if h >= IN_FLIGHT:
            act.wait_ge(self.s_turned, turn + h - IN_FLIGHT + 1)
        for nt, cols in self.tiles():
            last = act.activation(self.probs[:, h % IN_FLIGHT, cols], self.scores[:, h % IN_FLIGHT, cols], ACT.Exp, bias=self.bias[:, h % (2 * NH), nt:nt + 1],
                                  scale=scale if scales is None else scales[:, nt:nt + 1], accum_out=self.total[:, h % (2 * NH), nt:nt + 1])
        last.then_inc(ready, 1)


def attention_small_heads(nc, m, name, x, w_qk, w_v, causal, scale, qk_bias=None, v_bias=None, mean=None):
    with Stage(nc, name) as st:
        banks = st.ps("banks", [P, 8, HALF])
        hd = Heads(st, banks, causal)
        xb = st.sb("xb", [P, CT, T], F32 if mean is None else BF16)
        q, k = st.sb("q", [P, 2, NH, T]), st.sb("k", [P, 2, GROUPS, T])
        together = st.sb("together", [P, GROUPS, T])
        v = st.sb("v", [P, 2, 2, NH * 32])
        rtot = st.sb("rtot", [P, NH, 2])
        outT = banks[:, 5:7, :].rearrange("p n (g t) -> p (n g) t", t=T)
        kept_outT = st.sb("outT", [P, GROUPS, T])
        s_outT = [st.sem("outT_by_dve"), st.sem("outT_by_act")]
        own_dve, s_xb, s_job, s_zeroed, s_scales, s_spread = (
            st.sem(n) for n in ("own_dve", "xb_ready", "job_ready", "zeroed", "scales", "spread"))
        s_read = {"dve": st.sem("job_read_by_dve"), "act": st.sem("job_read_by_act")}
        if mean is not None:
            factor = st.sb("factor", [P, 1])
            q_scale, q_minus, v_scale = (st.sb(n, [P, TT]) for n in ("q_scale", "q_minus", "v_scale"))
        kept_by_act = (1, 3) if mean is None else (0, 1)
        NB = GROUPS + 1
        jobs = [(-1, "project", 0, n, 5 + n % 3, "act" if n in kept_by_act else "dve") for n in range(NB)]
        for b in range(B):
            if b + 1 < B:
                jobs += [(NH * b + at, "project", b + 1, n, 7, "act" if n in kept_by_act else "dve")
                         for n, at in enumerate((1, 3, 9, 11, 13))]
            jobs += [(NH * b + NH + WEIGH + 1 + 2 * nt, "back", b, nt, 7, "dve") for nt in range(2)]
        jobs.sort(key=lambda job: job[0])
        steps = range(NH * B + WEIGH + 5)

        def wait_read(eng, index):
            who = jobs[index][5]
            eng.wait_ge(s_read[who], sum(job[5] == who for job in jobs[:index + 1]))

        def wait_turned_back(eng, b):
            wait_read(eng, max(i for i, job in enumerate(jobs) if job[1:3] == ("back", b)))

        with nc.Block() as block:
            @block.gpsimd
            def _(pool):
                for half in range(2):
                    pool.memset(q[:, half], 0.0)
                    pool.memset(v[:, half], 0.0).then_inc(s_zeroed, 1)
                pool.wait_ge(s_zeroed, 2)
                for index, (_, what, b, n, _, _) in enumerate(jobs):
                    if what != "project" or n >= GROUPS // 2 or b == 0:
                        continue
                    wait_read(pool, index)
                    for j in range(HG):
                        rows_j = slice(32 * j, 32 * j + 32)
                        last = pool.tensor_copy(q[rows_j, b % 2, 2 * n * HG:2 * (n + 1) * HG, :].rearrange(
                            "p (g h) t -> p h g t", g=2)[:, j], together[rows_j, 2 * n:2 * n + 2, :])
                    last.then_inc(s_spread, 1)

            @block.tensor
            def _(pe):
                def project(b, n, bank):
                    for half in range(2):
                        into = banks[:, bank, half * T:(half + 1) * T]
                        for ct in range(CT):
                            if n < GROUPS:
                                g = 2 * n + half
                                last = pe.matmul(into, w_qk[:, ct, g * P:(g + 1) * P], xb[:, ct], start=ct == 0, stop=ct == CT - 1)
                            else:
                                last = pe.matmul(into, xb[:, ct, half * P:(half + 1) * P], w_v[:, ct], start=ct == 0, stop=ct == CT - 1)
                    return last

                def turn_back(nt, bank):
                    for g in range(GROUPS):
                        last = pe.transpose(banks[:, bank, g * P:(g + 1) * P], kept_outT[:, g, nt * P:(nt + 1) * P], m.ident[:, :])
                    return last

                def weigh(i):
                    b, h = i // NH, i % NH
                    pe.wait_ge(hd.s_moved[i % 2], i // 2 + 1)
                    if b and h % (NH // 2) == 0:
                        pe.wait_ge(s_outT[h // (NH // 2)], b)
                    into, probsT = outT[32 * (h % HG):32 * (h % HG) + 32, h // HG, :], hd.probsT[:, i % IN_FLIGHT, :]
                    v_h = [v[:, b % 2, mt, h * 32:(h + 1) * 32] for mt in range(2)]
                    if causal:
                        pe.matmul(into[:, 0:P], v_h[0], probsT[:, 0:P], start=True, stop=True)
                        pe.matmul(into[:, P:T], v_h[0], probsT[:, P:T], start=True, stop=False)
                        last = pe.matmul(into[:, P:T], v_h[1], probsT[:, T:3 * P], start=False, stop=True)
                    else:
                        of = probsT.rearrange("p (n m q) -> p m n q", n=2, m=2)
                        pe.matmul(into.rearrange("p (n q) -> p n q", n=2), v_h[0], of[:, 0], start=True, stop=False)
                        last = pe.matmul(into.rearrange("p (n q) -> p n q", n=2), v_h[1], of[:, 1], start=False, stop=True)
                    last.then_inc(hd.s_out, 1)

                def do_jobs(step):
                    for index, (at, what, b, n, bank, _) in enumerate(jobs):
                        if at != step:
                            continue
                        before = [j for j in range(index) if jobs[j][4] == bank]
                        if before:
                            wait_read(pe, before[-1])
                        if what == "project" and n == 0:
                            pe.wait_ge(s_xb, b + 1)
                        if what == "back":
                            for by in range(2):
                                pe.wait_ge(s_outT[by], b + 1)
                        (project(b, n, bank) if what == "project" else turn_back(n, bank)).then_inc(s_job, 1)
                do_jobs(-1)
                for i in steps:
                    if i < NH * B:
                        b, h = i // NH, i % NH
                        if h == 0:
                            if b:
                                pe.wait_ge(s_spread, GROUPS // 2 * b)
                            for index, (_, what, of, _, _, _) in enumerate(jobs):
                                if what == "project" and of == b:
                                    wait_read(pe, index)
                        hd.score(pe, 0, i, q[:, b % 2, h, :], k[:, b % 2, h // HG, :], m.ident_b[:, :], m.mask_causal)
                    if LAG <= i < NH * B + LAG:
                        hd.turn(pe, 0, i - LAG, m.ident[:, :])
                    if WEIGH <= i < NH * B + WEIGH:
                        weigh(i - WEIGH)
                    do_jobs(i)

            def keep(eng, copy, b, n, bank, by_act):
                s, t = b % 2, slice(b * T, (b + 1) * T)
                src = banks[:, bank, :].rearrange("p (g t) -> p g t", g=2)
                if n < GROUPS // 2:
                    if b == 0:
                        for j in range(HG):
                            rows_j = slice(32 * j, 32 * j + 32)
                            into = q[rows_j, s, 2 * n * HG:2 * (n + 1) * HG, :].rearrange("p (g h) t -> p h g t", g=2)[:, j]
                            if qk_bias is None:
                                last = copy(into, src[rows_j])
                                continue
                            for half in range(2):
                                bias = qk_bias[rows_j, 2 * n + half:2 * n + half + 1]
                                last = eng.activation(into[:, half], src[rows_j, half], ACT.Identity, bias=bias) if by_act else \
                                    eng.tensor_scalar(into[:, half], src[rows_j, half], bias, None, ALU.add)
                        return last
                    if b > 1:
                        eng.wait_ge(s_spread, GROUPS // 2 * (b - 2) + n + 1)
                    if qk_bias is None:
                        return copy(together[:, 2 * n:2 * n + 2, :], src)
                    for half in range(2):
                        g = 2 * n + half
                        into, bias = together[:, g, :], qk_bias[:, g:g + 1]
                        last = eng.activation(into, src[:, half], ACT.Identity, bias=bias) if by_act else \
                            eng.tensor_scalar(into, src[:, half], bias, None, ALU.add)
                elif n < GROUPS:
                    for half in range(2):
                        g = 2 * n + half - GROUPS
                        if mean is not None:
                            last = eng.tensor_tensor(k[:, s, g, :], src[:, half], m.inv_row[:, t], ALU.mult)
                        elif by_act:
                            last = eng.activation(k[:, s, g, :], src[:, half], ACT.Identity, bias=qk_bias[:, GROUPS + g:GROUPS + g + 1])
                        else:
                            last = eng.tensor_scalar(k[:, s, g, :], src[:, half], qk_bias[:, GROUPS + g:GROUPS + g + 1], None, ALU.add)
                else:
                    for mt in range(2):
                        into = v[:, s, mt, :].rearrange("p (h c) -> p h c", h=NH)[:, :, 0:16]
                        of = src[:, mt].rearrange("p (h c) -> p h c", h=NH)
                        last = eng.tensor_tensor(into, of, v_bias[:, :].rearrange("p (h c) -> p h c", h=NH), ALU.add) if mean is None \
                            else eng.tensor_scalar(into, of, v_scale[:, 2 * b + mt:2 * b + mt + 1], None, ALU.mult)
                return last

            def read_jobs(eng, copy, who, step, normalise=None):
                for index, (at, what, b, n, bank, by) in enumerate(jobs):
                    if at != step or by != who:
                        continue
                    eng.wait_ge(s_job, index + 1)
                    if what == "project":
                        eng.wait_ge(s_zeroed, min(b, 1) + 1)
                        keep(eng, copy, b, n, bank, who == "act").then_inc(s_read[who], 1)
                    else:
                        normalise(b, n, bank).then_inc(s_read[who], 1)

            @block.scalar
            def _(act):
                def copy(o, i):
                    return act.activation(o, i, ACT.Copy)
                read_jobs(act, copy, "act", -1)
                if mean is not None:
                    act.wait_ge(s_scales, 1)
                for i in steps:
                    if i < NH * B:
                        b = i // NH
                        hd.exp(act, 0, i, scale, hd.s_norm, q_scale[:, 2 * b:2 * b + 2] if mean is not None else None)
                    if LAG <= i < NH * B + LAG and (i - LAG) % 2:
                        hd.move(act, copy, 0, i - LAG)
                    if i % NH == WEIGH and i > NH:
                        b = i // NH - 1
                        act.wait_ge(hd.s_out, NH * (b + 1))
                        if b:
                            wait_turned_back(act, b - 1)
                        copy(kept_outT[:, 2:4, :], outT[:, 2:4, :]).then_inc(s_outT[1], 1)
                    read_jobs(act, copy, "act", i - 1 if i else None)

            @block.vector
            def _(dve):
                own = Tally(dve, own_dve)

                def copy(o, i):
                    return dve.tensor_copy(o, i)

                def take(b):
                    if b:
                        last_use = max(i for i, job in enumerate(jobs) if job[1:3] == ("project", b - 1))
                        dve.wait_ge(s_job, last_use + 1)
                    dve.tensor_copy(xb[:, :, :], x[:, :, b * T:(b + 1) * T]).then_inc(s_xb, 1)

                def normalise(b, nt, bank):
                    return dve.tensor_tensor(m.tok[:, 2 * b + nt, :].rearrange("p (h c) -> p h c", h=NH),
                                             banks[:, bank, :].rearrange("p (h c) -> p h c", h=NH)[:, :, 0:16],
                                             rtot[:, :, nt:nt + 1].broadcast_to([P, NH, 16]), ALU.mult)
                take(0)
                if mean is not None:
                    own.link(dve.tensor_scalar(factor[:, :], mean, mean, scale, ALU.mult, ALU.mult))
                    own.link(dve.tensor_scalar(v_scale[:, :], m.inv[:, :], mean, None, ALU.mult))
                    own.link(dve.tensor_scalar(q_minus[:, :], m.inv[:, :], factor[:, :], -1.0, ALU.mult, ALU.mult))
                    dve.tensor_scalar(q_scale[:, :], m.inv[:, :], factor[:, :], None, ALU.mult).then_inc(s_scales, 1)
                read_jobs(dve, copy, "dve", -1)
                for i in steps:
                    b = i // NH
                    if i < NH * B:
                        hd.top_of(dve, own, 0, i, scale, q_minus[:, 2 * b:2 * b + 2] if mean is not None else None)
                        if i % NH == 0 and b + 1 < B:
                            take(b + 1)
                    if LAG <= i < NH * B + LAG and (i - LAG) % 2 == 0:
                        hd.move(dve, copy, 0, i - LAG)
                    if i % NH == NH // 2 + WEIGH and i < NH * B:
                        dve.wait_ge(hd.s_out, NH * b + NH // 2)
                        if b:
                            wait_turned_back(dve, b - 1)
                        copy(kept_outT[:, 0:2, :], outT[:, 0:2, :]).then_inc(s_outT[0], 1)
                    if i % NH == WEIGH and b:
                        dve.wait_ge(hd.s_norm, NH * b)
                        own.link(dve.reciprocal(rtot[:, :, :], hd.total[:, (b - 1) % 2 * NH:(b - 1) % 2 * NH + NH, :]))
                    read_jobs(dve, copy, "dve", i - 1 if i else None, normalise)


def add_product(nc, m, name, w, x, bias=None, mean=None):
    kts = w.shape[1]
    with Stage(nc, name) as st:
        acc = st.ps("acc", [P, CT, NT])
        s_sum, own_dve = st.sem("sum"), st.sem("own_dve")
        scaled = st.sb("scaled", [P, 2, HALF])
        with nc.Block() as block:
            @block.tensor
            def _(pe):
                for o in range(CT):
                    for h in range(NT // HALF):
                        t = slice(h * HALF, (h + 1) * HALF)
                        for k in range(kts):
                            last = pe.matmul(acc[:, o, t], w[:, k, o * P:(o + 1) * P], x[:, k, t],
                                             start=k == 0, stop=k == kts - 1)
                        last.then_inc(s_sum, 1)

            @block.vector
            def _(dve):
                own = Tally(dve, own_dve)
                for o in range(CT):
                    for h in range(NT // HALF):
                        t = slice(h * HALF, (h + 1) * HALF)
                        dve.wait_ge(s_sum, o * (NT // HALF) + h + 1)
                        if mean is not None:
                            own.link(dve.scalar_tensor_tensor(out=scaled[:, h], in0=acc[:, o, t], scalar=mean,
                                                              in1=m.inv_row[:, t], op0=ALU.mult, op1=ALU.mult))
                            dve.tensor_tensor(m.xT[:, o, t], m.xT[:, o, t], scaled[:, h], ALU.add)
                        elif bias is None:
                            dve.tensor_tensor(m.xT[:, o, t], m.xT[:, o, t], acc[:, o, t], ALU.add)
                        else:
                            dve.scalar_tensor_tensor(out=m.xT[:, o, t], in0=acc[:, o, t], scalar=bias[:, o:o + 1],
                                                     in1=m.xT[:, o, t], op0=ALU.add, op1=ALU.add)



L0_E, L0_R = 8, 64


def argmax_gates(nc, m, name, w_g, select, gates):
    with Stage(nc, name) as st:
        lg, ex = st.sb("lg", [P, TT, L0_E]), st.sb("ex", [P, TT, L0_E])
        top, tot = st.sb("top", [P, TT, 1]), st.sb("tot", [P, TT, 1])
        gateT = st.sb("gateT", [L0_E, NT])
        logits = st.ps("logits", [P, TT, L0_E])
        turned = st.ps("turned", [L0_E, NT])
        wide = st.ps("wide", [P, 4, HALF])
        (own_dve, s_logits, s_shift, s_exp, s_gate, s_turned, s_copied, s_wide) = (st.sem(n) for n in (
            "own_dve", "logits", "shifted", "exp", "gate", "turned", "copied", "wide"))
        s_moved = [st.sem("moved_by_dve"), st.sem("moved_by_act")]
        banks = [(g, h) for g in range(4) for h in range(2)]
        with nc.Block() as block:
            @block.tensor
            def _(pe):
                for j in range(TT):
                    for ct in range(CT):
                        last = pe.matmul(logits[:, j, :], m.hT[:, ct, j * P:(j + 1) * P], w_g[:, ct, :],
                                         start=ct == 0, stop=ct == CT - 1)
                last.then_inc(s_logits, 1)
                pe.wait_ge(s_gate, 1)
                for j in range(TT):
                    last = pe.transpose(turned[:, j * P:(j + 1) * P], ex[:, j, :], m.ident[:, :])
                last.then_inc(s_turned, 1)
                pe.wait_ge(s_copied, 1)
                for n, (g, h) in enumerate(banks):
                    if n >= 4:
                        pe.wait_ge(s_moved[n % 2], (n - 4) // 2 + 1)
                    pe.matmul(wide[:, n % 4, :], select[:, g, :], gateT[:, h * HALF:(h + 1) * HALF],
                              start=True, stop=True).then_inc(s_wide, 1)

            @block.scalar
            def _(act):
                act.wait_ge(s_shift, 1)
                act.activation(ex[:, :, :], lg[:, :, :], ACT.Exp).then_inc(s_exp, 1)
                for n, (g, h) in enumerate(banks):
                    if n % 2:
                        act.wait_ge(s_wide, n + 1)
                        act.activation(gates[:, g, h * HALF:(h + 1) * HALF], wide[:, n % 4, :], ACT.Copy).then_inc(s_moved[1], 1)

            @block.vector
            def _(dve):
                own = Tally(dve, own_dve)
                dve.wait_ge(s_logits, 1)
                own.link(dve.tensor_reduce(top[:, :, :], logits[:, :, :], AX.X, ALU.max))
                dve.tensor_tensor(lg[:, :, :], logits[:, :, :], top[:, :, :].broadcast_to([P, TT, L0_E]),
                                  ALU.subtract).then_inc(s_shift, 1)
                dve.wait_ge(s_exp, 1)
                own.link(dve.tensor_reduce(tot[:, :, :], ex[:, :, :], AX.X, ALU.add))
                own.link(dve.reciprocal(tot[:, :, :], tot[:, :, :]))
                own.link(dve.tensor_scalar(tot[:, :, :], tot[:, :, :], 64.0 / 16.0, None, ALU.mult))
                own.link(dve.tensor_scalar(ex[:, :, :], lg[:, :, :], 0.0, None, ALU.is_equal))
                own.link(dve.tensor_tensor(ex[:, :, :], ex[:, :, :], m.rank[:, :].unsqueeze(1).broadcast_to([P, TT, L0_E]), ALU.mult))
                own.link(dve.tensor_reduce(top[:, :, :], ex[:, :, :], AX.X, ALU.max))
                own.link(dve.tensor_tensor(ex[:, :, :], ex[:, :, :], top[:, :, :].broadcast_to([P, TT, L0_E]), ALU.is_equal))
                dve.tensor_tensor(ex[:, :, :], ex[:, :, :], tot[:, :, :].broadcast_to([P, TT, L0_E]), ALU.mult).then_inc(s_gate, 1)
                dve.wait_ge(s_turned, 1)
                dve.tensor_copy(gateT[:, :], turned[:, :]).then_inc(s_copied, 1)
                for n, (g, h) in enumerate(banks):
                    if n % 2 == 0:
                        dve.wait_ge(s_wide, n + 1)
                        dve.tensor_copy(gates[:, g, h * HALF:(h + 1) * HALF], wide[:, n % 4, :]).then_inc(s_moved[0], 1)


def gated_inner(nc, m, name, w_a, gates, inner):
    with Stage(nc, name) as st:
        acc = st.ps("acc", [P, 4, HALF])
        s_sum, s_kept = st.sem("sum"), st.sem("kept")
        banks = [(g, h) for g in range(4) for h in range(2)]
        with nc.Block() as block:
            @block.tensor
            def _(pe):
                for n, (g, h) in enumerate(banks):
                    if n >= 4:
                        pe.wait_ge(s_kept, n - 3)
                    for ct in range(CT):
                        last = pe.matmul(acc[:, n % 4, :], w_a[:, ct, g * P:(g + 1) * P],
                                         m.hT[:, ct, h * HALF:(h + 1) * HALF], start=ct == 0, stop=ct == CT - 1)
                    last.then_inc(s_sum, 1)

            @block.vector
            def _(dve):
                for n, (g, h) in enumerate(banks):
                    t = slice(h * HALF, (h + 1) * HALF)
                    dve.wait_ge(s_sum, n + 1)
                    dve.tensor_tensor(inner[:, g, t], acc[:, n % 4, :], gates[:, g, t], ALU.mult).then_inc(s_kept, 1)



L1_CHUNKS = NH * P // HALF


def attention_wide_heads(nc, m, d, name, weights):
    scale = 128 ** -0.5
    w_q, w_k, w_v, w_o = weights.w_q, weights.w_k, weights.w_v, weights.w_o
    wq_loaded, wv_loaded, wk_loaded, wo_loaded = weights.loaded
    with Stage(nc, name) as st:
        banks = st.ps("banks", [P, 8, HALF])
        hd = Heads(st, banks, True)
        xb = st.sb("xb", [P, CT, T])
        qk = [st.sb("q", [P, NH, T]), st.sb("k", [P, NH, T])]
        v = st.sb("v", [P, 2, NH * P])
        oT = qk[0]
        cos, sin = st.sb("cos", [P, T]), st.sb("sin", [P, T])
        straight, crossed = st.sb("straight", [P, 2, HALF]), st.sb("crossed", [P, 2, HALF])
        rtot = st.sb("rtot", [P, NH, 2])
        prj = banks[:, 5:8, :]
        out = prj
        own_dve, own_act, loaded, s_xb, s_prj, s_rot, s_turned_pos, s_vkept, s_exp, s_okept, s_sum, s_added = (
            st.sem(n) for n in ("own_dve", "own_act", "loaded", "xb_ready", "prj_ready", "rotated_parts", "rotated",
                                "v_kept", "exp_ready", "o_kept", "sum", "added"))
        NR = NH
        NV = 2 * L1_CHUNKS
        sequence = [(True, i // 3 * 2 + i % 3) if i % 3 < 2 else (False, i // 3) for i in range(NR + NV)]
        with nc.Block() as block:
            @block.sync
            def _(sp):
                sp.dma_start(cos[:, :], d["l1_cos"]).then_inc(loaded, 16)
                sp.dma_start(sin[:, :], d["l1_sin"]).then_inc(loaded, 16)

            @block.tensor
            def _(pe):
                def batch(b, first):
                    turn = b * NH
                    pe.wait_ge(s_xb, b + 1)
                    for p, (rotated, n) in enumerate(sequence):
                        bank = p % 3
                        if p >= 3:
                            before, i = sequence[p - 3]
                            pe.wait_ge(s_rot if before else s_vkept, b * (NR if before else NV) + i + 1)
                        elif not first:
                            pe.wait_ge(s_added, b)
                        if not rotated:
                            mt, c = n // L1_CHUNKS, n % L1_CHUNKS
                            if first and n == 0:
                                pe.wait_ge(wv_loaded, 16)
                            for ct in range(CT):
                                last = pe.matmul(prj[:, bank, :], xb[:, ct, mt * P:(mt + 1) * P],
                                                 w_v[:, ct, c * HALF:(c + 1) * HALF], start=ct == 0, stop=ct == CT - 1)
                            last.then_inc(s_prj, 1)
                            continue
                        w = w_q if n < NR // 2 else w_k
                        if first and n % (NR // 2) == 0:
                            pe.wait_ge(wk_loaded if n else wq_loaded, 16)
                        for half in range(2):
                            h = 2 * (n % (NR // 2)) + half
                            for ct in range(CT):
                                last = pe.matmul(prj[:, bank, half * T:(half + 1) * T], w[:, ct, h * P:(h + 1) * P],
                                                 xb[:, ct], start=ct == 0, stop=ct == CT - 1)
                        last.then_inc(s_prj, 1)
                    pe.wait_ge(s_turned_pos, (b + 1) * NR)
                    pe.wait_ge(s_vkept, (b + 1) * NV)

                    def weigh(h):
                        pe.wait_ge(hd.s_moved[h % 2], turn // 2 + h // 2 + 1)
                        if h >= 2:
                            pe.wait_ge(s_okept, turn + h - 1)
                        for nt in range(2):
                            mine = [(i, mt) for i, (n_, mt) in enumerate(hd.blocks) if n_ == nt]
                            for i, mt in mine:
                                last = pe.matmul(out[:, h % 2, nt * P:(nt + 1) * P], v[:, mt, h * P:(h + 1) * P],
                                                 hd.probsT[:, h % IN_FLIGHT, i * P:(i + 1) * P],
                                                 start=i == mine[0][0], stop=i == mine[-1][0])
                        last.then_inc(hd.s_out, 1)
                    for i in range(NH + WEIGH):
                        if i < NH:
                            hd.score(pe, turn, i, qk[0][:, i, :], qk[1][:, i, :], m.ident_b[:, :], m.mask_window)
                        if LAG <= i < NH + LAG:
                            hd.turn(pe, turn, i - LAG, m.ident[:, :])
                        if i >= WEIGH:
                            weigh(i - WEIGH)
                    pe.wait_ge(s_okept, turn + NH)
                    if first:
                        pe.wait_ge(wo_loaded, 16)
                    for o in range(CT):
                        for h in range(NH):
                            last = pe.matmul(out[:, o, 0:T], w_o[:, h, o * P:(o + 1) * P], oT[:, h, :],
                                             start=h == 0, stop=h == NH - 1)
                    last.then_inc(s_sum, 1)
                batch(0, True)
                with pe.Fori(1, B, 1) as b:
                    batch(b, False)

            @block.scalar
            def _(act):
                def copy(o, i):
                    return act.activation(o, i, ACT.Copy)

                def batch(b, first):
                    turn = b * NH
                    for n in range(NV):
                        mt, c = n // L1_CHUNKS, n % L1_CHUNKS
                        p = sequence.index((False, n))
                        act.wait_ge(s_prj, b * (NR + NV) + p + 1)
                        copy(v[:, mt, c * HALF:(c + 1) * HALF], prj[:, p % 3, :]).then_inc(s_vkept, 1)
                    for i in range(NH + WEIGH):
                        if i < NH:
                            hd.exp(act, turn, i, scale, s_exp)
                        if LAG <= i < NH + LAG and (i - LAG) % 2:
                            hd.move(act, copy, turn, i - LAG)
                        if i >= WEIGH:
                            h = i - WEIGH
                            act.wait_ge(hd.s_out, turn + h + 1)
                            copy(oT[:, h, :], out[:, h % 2, 0:T]).then_inc(s_okept, 1)
                batch(0, True)
                with act.Fori(1, B, 1) as b:
                    batch(b, False)

            @block.gpsimd
            def _(pool):
                with pool.Fori(0, B, 1) as b:
                    for n in range(NR):
                        pool.wait_ge(s_rot, b * NR + n + 1)
                        h = 2 * (n % (NR // 2))
                        pool.tensor_tensor(qk[n // (NR // 2)][:, h:h + 2, :], straight[:, n % 2, :].rearrange("p (h t) -> p h t", h=2),
                                           crossed[:, n % 2, :].rearrange("p (h t) -> p h t", h=2), ALU.add).then_inc(s_turned_pos, 1)

            @block.vector
            def _(dve):
                own = Tally(dve, own_dve)
                dve.wait_ge(loaded, 32)

                def copy(o, i):
                    return dve.tensor_copy(o, i)

                def batch(b, first):
                    turn = b * NH
                    dve.tensor_copy(xb[:, :, :], m.hT[:, :, bass.ds(b * T, T)]).then_inc(s_xb, 1)
                    for n in range(NR):
                        p = sequence.index((True, n))
                        dve.wait_ge(s_prj, b * (NR + NV) + p + 1)
                        if n >= 2 or not first:
                            dve.wait_ge(s_turned_pos, b * NR + n - 1)
                        x = prj[:, p % 3, :].rearrange("p (h t) -> p h t", h=2)
                        cr = crossed[:, n % 2, :].rearrange("p (h t) -> p h t", h=2)
                        dve.tensor_tensor(straight[:, n % 2, :].rearrange("p (h t) -> p h t", h=2), x,
                                          cos[:, :].unsqueeze(1).broadcast_to([P, 2, T]), ALU.mult)
                        for src, dst in ((slice(64, P), slice(0, 64)), (slice(0, 64), slice(64, P))):
                            last = dve.tensor_tensor(cr[dst], x[src], sin[src, :].unsqueeze(1).broadcast_to([64, 2, T]), ALU.mult)
                        last.then_inc(s_rot, 1)

                    def normalise(h):
                        dve.wait_ge(s_exp, turn + h + 1)
                        own.link(dve.reciprocal(rtot[:, h, :], hd.total[:, h, :]))
                        for nt, cols in hd.tiles():
                            last = dve.tensor_scalar(hd.probs[:, h % IN_FLIGHT, cols], hd.probs[:, h % IN_FLIGHT, cols], rtot[:, h, nt:nt + 1],
                                                     None, ALU.mult)
                        last.then_inc(hd.s_norm, 1)
                    for i in range(NH + LAG):
                        if i < NH:
                            hd.top_of(dve, own, turn, i, scale)
                        if 1 <= i <= NH:
                            normalise(i - 1)
                        if i >= LAG and (i - LAG) % 2 == 0:
                            hd.move(dve, copy, turn, i - LAG)
                    dve.wait_ge(s_sum, b + 1)
                    for o in range(CT):
                        t = bass.ds(b * T, T)
                        last = dve.tensor_tensor(m.xT[:, o, t], m.xT[:, o, t], out[:, o, 0:T], ALU.add)
                    last.then_inc(s_added, 1)
                batch(0, True)
                with dve.Fori(1, B, 1) as b:
                    own.enter(b - 1, 2 * NH)
                    batch(b, False)
                own.leave(B - 1)



E, GROUPS_E = 64, 8
GE = E // GROUPS_E
TOP_GROUPS = 4
ROUTED_SCALE = 2.5


class Routing:

    def __init__(self, st, K, moves):
        self.K = K
        self.scattered, self.gathered = moves
        self.put = st.sb("slot_put", [P, TT, K], U32)
        self.get = st.sb("slot_get", [P, TT, K], U32)
        self.gate = st.sb("gate", [P, TT, K])


def route(nc, m, name, w_g, bias, r, cap, fill):
    K = r.K
    with Stage(nc, name) as st:
        score, biased, masked = (st.sb(n, [P, TT, E]) for n in ("score", "biased", "masked"))
        hi, lo, hi2, lo2, mid = (st.sb(n, [P, TT * GROUPS_E, 4]) for n in ("hi", "lo", "hi2", "lo2", "mid"))
        gsum, gin, pen = (st.sb(n, [P, TT, GROUPS_E]) for n in ("gsum", "gin", "pen"))
        best, idx, idxf = st.sb("best", [P, TT, 8]), st.sb("idx", [P, TT, 8], U32), st.sb("idxf", [P, TT, 8])
        geq = st.sb("geq", [P, TT, TOP_GROUPS, GROUPS_E])
        chosen, prod = st.sb("chosen", [P, TT, K, E]), st.sb("prod", [P, TT, K, E])
        sel = st.sb("sel", [P, TT, E], BF16)
        pos, wk, keep, slot, tmp = (st.sb(n, [P, TT, K]) for n in ("pos", "wk", "keep", "slot", "tmp"))
        wsum = st.sb("wsum", [P, TT, 1])
        logits, before = st.ps("logits", [P, TT, E]), st.ps("before", [P, TT, E])
        own_dve, s_logits, s_score, s_sel, s_before = (st.sem(n) for n in ("own_dve", "logits", "score", "sel", "before"))
        with nc.Block() as block:
            @block.tensor
            def _(pe):
                for j in range(TT):
                    for ct in range(CT):
                        last = pe.matmul(logits[:, j, :], m.hT[:, ct, j * P:(j + 1) * P], w_g[:, ct, :],
                                         start=ct == 0, stop=ct == CT - 1)
                last.then_inc(s_logits, 1)
                pe.wait_ge(s_sel, 1)
                pe.matmul(before[:, :, :], m.earlier[:, :], sel[:, :, :], start=True, stop=False)
                for j in range(TT - 1):
                    last = pe.matmul(before[:, j + 1:, :], m.ones_b[:, :], sel[:, j:j + 1, :].broadcast_to([P, TT - 1 - j, E]),
                                     start=False, stop=j == TT - 2)
                last.then_inc(s_before, 1)

            @block.scalar
            def _(act):
                act.wait_ge(s_logits, 1)
                act.activation(score[:, :, :], logits[:, :, :], ACT.Sigmoid).then_inc(s_score, 1)

            @block.vector
            def _(dve):
                own = Tally(dve, own_dve)

                def both(o, a, b, op):
                    own.link(dve.tensor_tensor(o, a, b, op))
                dve.wait_ge(s_score, 1)
                both(biased[:, :, :], score[:, :, :], bias[:, :].unsqueeze(1).broadcast_to([P, TT, E]), ALU.add)
                v = biased[:, :, :].rearrange("p t (g e) -> p (t g) e", e=GE)
                both(hi[:, :, :], v[:, :, 0:4], v[:, :, 4:8], ALU.max)
                both(lo[:, :, :], v[:, :, 0:4], v[:, :, 4:8], ALU.min)
                h, l, h_, l_ = hi, lo, hi2, lo2
                for n in (2, 1):
                    both(mid[:, :, 0:n], h[:, :, 0:n], h[:, :, n:2 * n], ALU.min)
                    both(h_[:, :, 0:n], h[:, :, 0:n], h[:, :, n:2 * n], ALU.max)
                    both(l_[:, :, 0:n], l[:, :, 0:n], l[:, :, n:2 * n], ALU.max)
                    both(l_[:, :, 0:n], l_[:, :, 0:n], mid[:, :, 0:n], ALU.max)
                    h, l, h_, l_ = h_, l_, h, l
                both(gsum[:, :, :], h[:, :, 0:1].rearrange("p (t g) o -> p t (g o)", g=GROUPS_E),
                     l[:, :, 0:1].rearrange("p (t g) o -> p t (g o)", g=GROUPS_E), ALU.add)
                for j in range(TT):
                    last = dve.max(best[:, j, :], gsum[:, j, :])
                own.link(last)
                for j in range(TT):
                    last = dve.max_index(idx[:, j, :], best[:, j, :], gsum[:, j, :])
                own.link(last)
                own.link(dve.tensor_copy(idxf[:, :, :], idx[:, :, :]))
                both(geq[:, :, :, :], m.iota[:, 0:GROUPS_E].unsqueeze(1).unsqueeze(1).broadcast_to([P, TT, TOP_GROUPS, GROUPS_E]),
                     idxf[:, :, 0:TOP_GROUPS].unsqueeze(3).broadcast_to([P, TT, TOP_GROUPS, GROUPS_E]), ALU.is_equal)
                own.link(dve.tensor_reduce(gin[:, :, :], geq[:, :, :, :].rearrange("p t k g -> p t g k"), AX.X, ALU.add))
                own.link(dve.tensor_scalar(pen[:, :, :], gin[:, :, :], -fill, fill, ALU.mult, ALU.add))
                mk = masked[:, :, :].rearrange("p t (g e) -> p (t g) e", e=GE)
                both(mk, v, gin[:, :, :].rearrange("p t g -> p (t g)").unsqueeze(2).broadcast_to([P, TT * GROUPS_E, GE]), ALU.mult)
                both(mk, mk, pen[:, :, :].rearrange("p t g -> p (t g)").unsqueeze(2).broadcast_to([P, TT * GROUPS_E, GE]), ALU.add)
                for j in range(TT):
                    last = dve.max(best[:, j, :], masked[:, j, :])
                own.link(last)
                for j in range(TT):
                    last = dve.max_index(idx[:, j, :], best[:, j, :], masked[:, j, :])
                own.link(last)
                own.link(dve.tensor_copy(idxf[:, :, :], idx[:, :, :]))
                full = [P, TT, K, E]
                both(chosen[:, :, :, :], m.iota[:, :].unsqueeze(1).unsqueeze(1).broadcast_to(full),
                     idxf[:, :, 0:K].unsqueeze(3).broadcast_to(full), ALU.is_equal)
                dve.tensor_reduce(sel[:, :, :], chosen[:, :, :, :].rearrange("p t k e -> p t e k"), AX.X, ALU.max).then_inc(s_sel, 1)
                both(prod[:, :, :, :], chosen[:, :, :, :], score[:, :, :].unsqueeze(2).broadcast_to(full), ALU.mult)
                own.link(dve.tensor_reduce(wk[:, :, :], prod[:, :, :, :], AX.X, ALU.add))
                dve.wait_ge(s_before, 1)
                both(prod[:, :, :, :], chosen[:, :, :, :], before[:, :, :].unsqueeze(2).broadcast_to(full), ALU.mult)
                own.link(dve.tensor_reduce(pos[:, :, :], prod[:, :, :, :], AX.X, ALU.add))
                own.link(dve.tensor_scalar(keep[:, :, :], pos[:, :, :], float(cap), None, ALU.is_lt))
                own.link(dve.scalar_tensor_tensor(out=slot[:, :, :], in0=idxf[:, :, 0:K], scalar=float(cap), in1=pos[:, :, :],
                                                  op0=ALU.mult, op1=ALU.add))
                own.link(dve.tensor_scalar(tmp[:, :, :], keep[:, :, :], -1048576.0, 1048576.0, ALU.mult, ALU.add))
                both(tmp[:, :, :], tmp[:, :, :], slot[:, :, :], ALU.add)
                own.link(dve.tensor_copy(r.put[:, :, :], tmp[:, :, :]))
                both(slot[:, :, :], slot[:, :, :], keep[:, :, :], ALU.mult)
                dve.tensor_copy(r.get[:, :, :], slot[:, :, :])
                own.link(dve.tensor_reduce(wsum[:, :, :], wk[:, :, :], AX.X, ALU.add))
                own.link(dve.tensor_scalar(wsum[:, :, :], wsum[:, :, :], 1e-20, None, ALU.add))
                own.link(dve.reciprocal(wsum[:, :, :], wsum[:, :, :]))
                both(wk[:, :, :], wk[:, :, :], wsum[:, :, :].broadcast_to([P, TT, K]), ALU.mult)
                dve.scalar_tensor_tensor(out=r.gate[:, :, :], in0=wk[:, :, :], scalar=ROUTED_SCALE, in1=keep[:, :, :],
                                         op0=ALU.mult, op1=ALU.mult)


def dispatch(nc, m, name, r, slots_in, w_up, w_gate, w_down, inner, rows_i):
    n_slots = slots_in.shape[0]
    tiles = w_up.shape[2] // rows_i
    with Stage(nc, name) as st:
        acc, total = st.ps("acc", [P, 4, HALF]), st.ps("total", [P, CT, NT])
        side = st.sb("side", [P, 2, HALF])
        scattered = r.scattered
        s_sum, s_act, s_kept, s_total = (st.sem(n) for n in ("sum", "activated", "kept", "total"))
        banks = [(i, h) for i in range(tiles) for h in range(NT // HALF)]
        with nc.Block() as block:
            @block.gpsimd
            def _(pool):
                for j in range(TT):
                    for k in range(r.K):
                        pool.indirect_dma_start(slots_in, bass.IndirectOffsetOnAxis(ap=r.put[:, j, k:k + 1], axis=0),
                                                m.tok[:, j, :], None, bounds_check=n_slots - 1,
                                                oob_is_err=False).then_inc(scattered, 16)
                pool.wait_ge(scattered, 16 * TT * r.K)

            @block.tensor
            def _(pe):
                for n, (i, h) in enumerate(banks):
                    if n >= 2:
                        pe.wait_ge(s_kept, n - 1)
                    for g, w in enumerate((w_up, w_gate)):
                        for ct in range(CT if w is not None else 0):
                            last = pe.matmul(acc[0:rows_i, 2 * (n % 2) + g, :], w[:, ct, i * rows_i:(i + 1) * rows_i],
                                             m.hT[:, ct, h * HALF:(h + 1) * HALF], start=ct == 0, stop=ct == CT - 1)
                    last.then_inc(s_sum, 1)
                pe.wait_ge(s_kept, len(banks))
                for o in range(CT):
                    for h in range(NT // HALF):
                        t = slice(h * HALF, (h + 1) * HALF)
                        for k in range(tiles):
                            last = pe.matmul(total[:, o, t], w_down[:, k, o * P:(o + 1) * P], inner[0:rows_i, k, t],
                                             start=k == 0, stop=k == tiles - 1)
                        last.then_inc(s_total, 1)

            @block.scalar
            def _(act):
                for n in range(len(banks)):
                    act.wait_ge(s_sum, n + 1)
                    if n >= 2:
                        act.wait_ge(s_kept, n - 1)
                    if w_gate is None:
                        ins = act.activation(side[0:rows_i, n % 2, :], acc[0:rows_i, 2 * (n % 2), :], ACT.Relu)
                    else:
                        ins = act.activation(side[0:rows_i, n % 2, :], acc[0:rows_i, 2 * (n % 2) + 1, :], ACT.Silu)
                    ins.then_inc(s_act, 1)

            @block.vector
            def _(dve):
                for n, (i, h) in enumerate(banks):
                    dve.wait_ge(s_act, n + 1)
                    other = side[0:rows_i, n % 2, :] if w_gate is None else acc[0:rows_i, 2 * (n % 2), :]
                    dve.tensor_tensor(inner[0:rows_i, i, h * HALF:(h + 1) * HALF], side[0:rows_i, n % 2, :], other,
                                      ALU.mult).then_inc(s_kept, 1)
                for o in range(CT):
                    for h in range(NT // HALF):
                        t = slice(h * HALF, (h + 1) * HALF)
                        dve.wait_ge(s_total, o * (NT // HALF) + h + 1)
                        dve.tensor_tensor(m.xT[:, o, t], m.xT[:, o, t], total[:, o, t], ALU.add)


RING = 8
STORES = 4


def experts(nc, m, name, slots_in, slots_out, weights, per, rows_i, gated):
    units = slots_in.shape[0] // P
    cap = P // per
    n_in = 2 if gated else 1
    with Stage(nc, name) as st:
        xs = st.sb("xs", [P, RING, C])
        w_in = per * CT * rows_i
        w = st.sb("w", [P, RING, n_in * w_in + per * C])
        wi = [w[:, :, g * w_in:(g + 1) * w_in].rearrange("p r (e t i) -> p r e t i", e=per, t=CT) for g in range(n_in)]
        wo = w[:, :, n_in * w_in:].rearrange("p r (e c) -> p r e c", e=per)
        xsT = st.sb("xsT", [P, 2, CT, P])
        half = st.sb("half", [P, 2, P])
        inner = st.sb("inner", [P, 2, P])
        y = st.sb("y", [P, STORES, C])
        xs_t, up, ys = st.ps("xs_t", [P, 2, HALF]), st.ps("up", [P, 2, HALF]), st.ps("ys", [P, 2, HALF])
        loaded = [st.sem(f"loaded{i}") for i in range(RING)]
        stored = [st.sem(f"stored{i}") for i in range(STORES)]
        s_turned, s_copied, s_up, s_half, s_inner, s_ys, s_kept = (
            st.sem(n) for n in ("turned", "copied", "up", "half", "inner", "ys", "kept"))
        n_loads = 2

        def pipeline(eng, steps, depth):
            for i in range(RING):
                steps(i, i)
            with eng.Fori(1, units // RING, 1) as it:
                for c in range(RING):
                    steps(it * RING + c, RING + c)
            for i in range(units, units + depth):
                steps(i, i)
        with nc.Block() as block:
            @block.sync
            def _(sp):
                def load_unit(u, r, seen):
                    if seen >= RING:
                        sp.wait_ge(s_ys, u - RING + 1)
                    sp.dma_start(xs[:, r, :], slots_in[bass.ds(u * P, P), :]).then_inc(loaded[r], 16)
                    sp.dma_start(w[:, r], weights[bass.ds(u, 1)]).then_inc(loaded[r], 16)

                def store_unit(u, r):
                    sp.wait_ge(s_kept, u + 1)
                    sp.dma_start(slots_out[bass.ds(u * P, P), :], y[:, r % STORES, :]).then_inc(stored[r % STORES], 16)

                for u in range(RING):
                    load_unit(u, u, u)
                with sp.Fori(1, units // RING, 1) as it:
                    for c in range(RING):
                        store_unit(it * RING + c - RING, c)
                        load_unit(it * RING + c, c, RING)
                for c in range(RING):
                    store_unit(units - RING + c, c)
                for s in stored:
                    sp.wait_ge(s, 16 * units // STORES)

            @block.tensor
            def _(pe):
                def steps(i, seen):
                    c = seen % RING
                    if isinstance(i, int) and i >= units:
                        pass
                    else:
                        pe.wait_ge(loaded[c], 16 * n_loads * (i // RING + 1))
                        if seen >= 2:
                            pe.wait_ge(s_copied, i - 1)
                        for ct in range(CT):
                            last = pe.transpose(xs_t[:, c % 2, ct * P:(ct + 1) * P], xs[:, c, ct * P:(ct + 1) * P], m.ident[:, :])
                        last.then_inc(s_turned, 1)
                    if seen >= 1 and not (isinstance(i, int) and i - 1 >= units):
                        r = (c - 1) % RING
                        pe.wait_ge(s_copied, i)
                        if seen >= 3:
                            pe.wait_ge(s_inner, i - 2)
                        for e in range(per):
                            for g in range(n_in):
                                for ct in range(CT):
                                    last = pe.matmul(up[0:rows_i, r % 2, g * P + e * cap:g * P + (e + 1) * cap], wi[g][:, r, e, ct],
                                                     xsT[:, r % 2, ct, e * cap:(e + 1) * cap], start=ct == 0, stop=ct == CT - 1)
                        last.then_inc(s_up, 1)
                    if seen >= 2:
                        r = (c - 2) % RING
                        pe.wait_ge(s_inner, i - 1)
                        if seen >= 4:
                            pe.wait_ge(s_kept, i - 3)
                        for e in range(per):
                            last = pe.matmul(ys[e * cap:(e + 1) * cap, r % 2, 0:C], inner[0:rows_i, r % 2, e * cap:(e + 1) * cap],
                                             wo[0:rows_i, r, e, :], start=True, stop=True)
                        last.then_inc(s_ys, 1)
                pipeline(pe, steps, 2)

            @block.scalar
            def _(act):
                def steps(i, seen):
                    c = seen % RING
                    if not (isinstance(i, int) and i >= units):
                        act.wait_ge(s_turned, i + 1)
                        if seen >= 2:
                            act.wait_ge(s_up, i - 1)
                        act.activation(xsT[:, c % 2].rearrange("p a b -> p (a b)"), xs_t[:, c % 2, 0:C], ACT.Copy).then_inc(s_copied, 1)
                    if seen >= 1:
                        r = (c - 1) % RING
                        act.wait_ge(s_up, i)
                        if seen >= 3:
                            act.wait_ge(s_inner, i - 2)
                        if gated:
                            ins = act.activation(half[0:rows_i, r % 2, :], up[0:rows_i, r % 2, P:2 * P], ACT.Silu)
                        else:
                            ins = act.activation(half[0:rows_i, r % 2, :], up[0:rows_i, r % 2, 0:P], ACT.Relu)
                        ins.then_inc(s_half, 1)
                pipeline(act, steps, 1)

            @block.vector
            def _(dve):
                def steps(i, seen):
                    c = seen % RING
                    if seen >= 1 and not (isinstance(i, int) and i - 1 >= units):
                        r = (c - 1) % RING
                        dve.wait_ge(s_half, i)
                        if seen >= 3:
                            dve.wait_ge(s_ys, i - 2)
                        other = up[0:rows_i, r % 2, 0:P] if gated else half[0:rows_i, r % 2, :]
                        dve.tensor_tensor(inner[0:rows_i, r % 2, :], half[0:rows_i, r % 2, :], other, ALU.mult).then_inc(s_inner, 1)
                    if seen >= 2:
                        r = (c - 2) % RING
                        dve.wait_ge(s_ys, i - 1)
                        if seen >= 2 + STORES:
                            dve.wait_ge(stored[r % STORES], 16 * ((i - 2) // STORES))
                        dve.tensor_copy(y[:, r % STORES, :], ys[:, r % 2, 0:C]).then_inc(s_kept, 1)
                pipeline(dve, steps, 2)


class Combining:

    def __init__(self, st, m, r, slots_out):
        self.m, self.r, self.K, self.slots_out = m, r, r.K, slots_out
        self.got = st.sb("got", [P, 2, TT, C])
        self.s_added, self.s_turned = st.sem("added"), st.sem("back_turned")

    def gather(self, pool, k):
        for j in range(TT):
            if k >= 2:
                pool.wait_ge(self.s_added, (k - 1) * TT + j + 1)
            pool.indirect_dma_start(self.got[:, k % 2, j, :], None, self.slots_out,
                                    bass.IndirectOffsetOnAxis(ap=self.r.get[:, j, k:k + 1], axis=0)
                                    ).then_inc(self.r.gathered[k % 2][j], 16)

    def clear(self, dve):
        for j in range(TT):
            dve.memset(self.m.tok[:, j, :], 0.0).then_inc(self.s_added, 1)

    def add(self, dve, k, nth, odd):
        for j in range(TT):
            dve.wait_ge(self.r.gathered[odd][j], 16 * nth)
            dve.wait_ge(self.s_added, k * TT + j + 1)
            dve.scalar_tensor_tensor(out=self.m.tok[:, j, :], in0=self.got[:, odd, j, :], scalar=self.r.gate[:, j, bass.ds(k, 1)],
                                     in1=self.m.tok[:, j, :], op0=ALU.mult, op1=ALU.add).then_inc(self.s_added, 1)

    def turn(self, pe, turned):
        for j in range(TT):
            pe.wait_ge(self.s_added, self.K * TT + j + 1)
            for ct in range(CT):
                last = pe.transpose(turned[:, ct, j * P:(j + 1) * P], self.m.tok[:, j, ct * P:(ct + 1) * P], self.m.ident[:, :])
            if j % (TT // 2) == TT // 2 - 1:
                last.then_inc(self.s_turned, 1)

    def finish(self, dve, turned):
        for h in range(2):
            dve.wait_ge(self.s_turned, h + 1)
            t = slice(h * HALF, (h + 1) * HALF)
            for ct in range(CT):
                dve.tensor_tensor(self.m.xT[:, ct, t], self.m.xT[:, ct, t], turned[:, ct, t], ALU.add)


class LowRank:

    BANKS = 3

    def __init__(self, st, low, up, parts):
        self.low, self.up, self.parts = low, up, parts
        self.banks = st.ps("banks", [P, self.BANKS, HALF])
        self.s_term, self.s_added = st.sem("term"), st.sem("term_added")
        firsts = np.cumsum([0] + [w.shape[2] for w in parts])
        self.terms = [(i, int(firsts[i]), ct) for i in range(len(parts)) for ct in range(CT)]

    def into(self, n):
        return self.banks[:, n % self.BANKS, 0:self.parts[self.terms[n][0]].shape[2]]

    def multiply(self, pe):
        for n, (i, at, ct) in enumerate(self.terms):
            if n >= self.BANKS:
                pe.wait_ge(self.s_added, n - self.BANKS + 1)
            pe.matmul(self.into(n), self.low[:, i, ct * P:(ct + 1) * P], self.up[:, at:at + self.parts[i].shape[2]],
                      start=True, stop=True).then_inc(self.s_term, 1)

    def add(self, dve):
        for n, (i, _, ct) in enumerate(self.terms):
            dve.wait_ge(self.s_term, n + 1)
            dve.scalar_tensor_tensor(out=self.parts[i][:, ct], in0=self.into(n), scalar=0.5, in1=self.parts[i][:, ct],
                                     op0=ALU.mult, op1=ALU.add).then_inc(self.s_added, 1)


def combine(nc, m, name, r, slots_out, groups, mean, low_rank):
    with Stage(nc, name) as st:
        low = LowRank(st, *low_rank)
        t = Ternary(st, m, groups, mean)
        c = Combining(st, m, r, slots_out)
        turned = st.ps("turned", [P, CT, NT])
        with nc.Block() as block:
            @block.gpsimd
            def _(pool):
                for k in range(c.K):
                    c.gather(pool, k)

            @block.vector
            def _(dve):
                c.clear(dve)
                t.quantize(dve)
                c.add(dve, 0, 1, 0)
                c.add(dve, 1, 1, 1)
                low.add(dve)
                with dve.Fori(1, c.K // 2, 1) as i:
                    c.add(dve, 2 * i, i + 1, 0)
                    c.add(dve, 2 * i + 1, i + 1, 1)
                c.finish(dve, turned)

            @block.tensor
            def _(pe):
                t.add_up(pe)
                low.multiply(pe)
                c.turn(pe, turned)



L2_H, L2_D = 32, 8
L2_HALF = TT // B


def qkv_tokens(nc, m, name, w, bias, qkv):
    cols = [slice(0, HALF), slice(HALF, 3 * C)]
    with Stage(nc, name) as st:
        acc = st.ps("acc", [P, 4, HALF])
        s_sum, s_kept = st.sem("sum"), st.sem("kept")
        banks = [(j, c) for j in range(TT) for c in cols]
        with nc.Block() as block:
            @block.tensor
            def _(pe):
                for n, (j, c) in enumerate(banks):
                    if n >= 4:
                        pe.wait_ge(s_kept, n - 3)
                    for ct in range(CT):
                        last = pe.matmul(acc[:, n % 4, 0:c.stop - c.start], m.hT[:, ct, j * P:(j + 1) * P], w[:, ct, c],
                                         start=ct == 0, stop=ct == CT - 1)
                    last.then_inc(s_sum, 1)

            @block.vector
            def _(dve):
                for n, (j, c) in enumerate(banks):
                    dve.wait_ge(s_sum, n + 1)
                    dve.tensor_tensor(qkv[:, j, c], acc[:, n % 4, 0:c.stop - c.start], bias[:, c], ALU.add).then_inc(s_kept, 1)


def attention_over_batch(nc, m, d, name, qkv):
    X = L2_HALF * L2_H
    scale = float(np.float32(1) / np.sqrt(np.float32(L2_D)))
    with Stage(nc, name) as st:
        cos, sin = st.sb("cos", [P, B, L2_D]), st.sb("sin", [P, B, L2_D])
        straight, crossed = st.sb("straight", [P, TT, 2 * C]), st.sb("crossed", [P, TT, 2 * C])
        vc = st.sb("vc", [P, TT, C])
        prod = st.sb("prod", [P, 3, B * L2_HALF * C])
        score, top, tot = st.sb("score", [P, B, B, X]), st.sb("top", [P, B, X]), st.sb("tot", [P, B, X])
        (loaded, own_dve, s_straight, s_crossed, s_rot, s_cleared, s_v, s_prod, s_red, s_shift, s_exp, s_norm, s_wprod,
         s_wred) = (st.sem(n) for n in ("loaded", "own_dve", "straight", "crossed", "rotated", "cleared", "v", "prod",
                                        "reduced", "shifted", "exp", "norm", "weighted", "summed"))
        x = qkv[:, :, 0:2 * C].rearrange("p t (h e) -> p t h e", e=L2_D)

        def heads(t):
            return t[:, :, :].rearrange("p t (h e) -> p t h e", e=L2_D)

        def table(t, b, part):
            n = part.stop - part.start
            return t[:, b, part].unsqueeze(1).unsqueeze(1).broadcast_to([P, L2_HALF, 2 * L2_H, n])
        lo, hi, both = slice(0, L2_D // 2), slice(L2_D // 2, L2_D), slice(0, L2_D)
        third = [0, 1, 0, 2]
        LAST = B - 1

        def products(eng, s):
            o = prod[:, third[s], 0:(s + 1) * L2_HALF * C].rearrange("p (k t c) -> p k t c", t=L2_HALF, c=C)
            q = straight[:, s * L2_HALF:(s + 1) * L2_HALF, 0:C].unsqueeze(1).broadcast_to([P, s + 1, L2_HALF, C])
            k = straight[:, 0:(s + 1) * L2_HALF, C:2 * C].rearrange("p (k t) c -> p k t c", t=L2_HALF)
            return eng.tensor_tensor(o, q, k, ALU.mult)

        def weighted(eng, s):
            o = prod[:, third[s], 0:(s + 1) * L2_HALF * C].rearrange("p (k x e) -> p k x e", x=X, e=L2_D)
            v = vc[:, 0:(s + 1) * L2_HALF, :].rearrange("p (k t) (h e) -> p k (t h) e", t=L2_HALF, e=L2_D)
            p = score[:, s, 0:s + 1, :].unsqueeze(3).broadcast_to([P, s + 1, X, L2_D])
            return eng.tensor_tensor(o, v, p, ALU.mult)
        with nc.Block() as block:
            @block.sync
            def _(sp):
                sp.dma_start(cos[:, :, :], d["l2_cos"]).then_inc(loaded, 16)
                sp.dma_start(sin[:, :, :], d["l2_sin"]).then_inc(loaded, 16)

            @block.gpsimd
            def _(pool):
                pool.memset(score[:, :, :, :], MASKED).then_inc(s_cleared, 1)
                pool.wait_ge(loaded, 32)
                for b in range(B):
                    j = slice(b * L2_HALF, (b + 1) * L2_HALF)
                    for dst, src in ((lo, hi), (hi, lo)):
                        last = pool.tensor_tensor(heads(crossed)[:, j, :, dst], x[:, j, :, src], table(sin, b, dst), ALU.mult)
                    last.then_inc(s_crossed, 1)
                pool.wait_ge(s_rot, B)
                for s in range(LAST):
                    if s >= 2:
                        pool.wait_ge(s_red, s)
                    products(pool, s).then_inc(s_prod, 1)
                pool.wait_ge(s_v, 1)
                pool.wait_ge(s_norm, 1)
                pool.wait_ge(s_red, B)
                for s in range(LAST):
                    if s >= 2:
                        pool.wait_ge(s_wred, s)
                    weighted(pool, s).then_inc(s_wprod, 1)

            @block.scalar
            def _(act):
                act.activation(vc[:, :, :], qkv[:, :, 2 * C:3 * C], ACT.Copy).then_inc(s_v, 1)
                act.wait_ge(s_shift, 1)
                act.activation(score[:, :, :, :], score[:, :, :, :], ACT.Exp, scale=scale).then_inc(s_exp, 1)

            @block.vector
            def _(dve):
                own = Tally(dve, own_dve)
                dve.wait_ge(loaded, 32)
                for b in range(B):
                    j = slice(b * L2_HALF, (b + 1) * L2_HALF)
                    dve.tensor_tensor(heads(straight)[:, j], x[:, j], table(cos, b, both), ALU.mult).then_inc(s_straight, 1)
                for b in range(B):
                    j = slice(b * L2_HALF, (b + 1) * L2_HALF)
                    dve.wait_ge(s_straight, b + 1)
                    dve.wait_ge(s_crossed, b + 1)
                    dve.tensor_tensor(straight[:, j, :], straight[:, j, :], crossed[:, j, :], ALU.add).then_inc(s_rot, 1)
                dve.wait_ge(s_cleared, 1)
                dve.wait_ge(s_rot, B)
                own.link(products(dve, LAST))
                for s in (LAST, *range(LAST)):
                    if s < LAST:
                        dve.wait_ge(s_prod, s + 1)
                    src = prod[:, third[s], 0:(s + 1) * L2_HALF * C].rearrange("p (k x e) -> p k x e", x=X, e=L2_D)
                    dve.tensor_reduce(score[:, s, 0:s + 1, :], src, AX.X, ALU.add).then_inc(s_red, 1)
                dve.wait_ge(s_red, B)
                own.link(dve.tensor_reduce(top[:, :, :], score[:, :, :, :].rearrange("p s k x -> p s x k"), AX.X, ALU.max))
                full = [P, B, B, X]
                dve.tensor_tensor(score[:, :, :, :], score[:, :, :, :], top[:, :, :].unsqueeze(2).broadcast_to(full),
                                  ALU.subtract).then_inc(s_shift, 1)
                dve.wait_ge(s_exp, 1)
                own.link(dve.tensor_reduce(tot[:, :, :], score[:, :, :, :].rearrange("p s k x -> p s x k"), AX.X, ALU.add))
                own.link(dve.reciprocal(tot[:, :, :], tot[:, :, :]))
                dve.tensor_tensor(score[:, :, :, :], score[:, :, :, :], tot[:, :, :].unsqueeze(2).broadcast_to(full),
                                  ALU.mult).then_inc(s_norm, 1)
                dve.wait_ge(s_norm, 1)
                dve.wait_ge(s_v, 1)
                own.link(weighted(dve, LAST))
                for s in (LAST, *range(LAST)):
                    if s < LAST:
                        dve.wait_ge(s_wprod, s + 1)
                    src = prod[:, third[s], 0:(s + 1) * L2_HALF * C].rearrange("p (k x) -> p x k", x=L2_HALF * C)
                    out = m.tok[:, s * L2_HALF:(s + 1) * L2_HALF, :].rearrange("p t c -> p (t c)")
                    dve.tensor_reduce(out, src, AX.X, ALU.add).then_inc(s_wred, 1)


def turn_tokens(nc, m, name):
    with Stage(nc, name) as st:
        tp = st.ps("tp", [P, CT, NT])
        s_turned = st.sem("turned")
        with nc.Block() as block:
            @block.tensor
            def _(pe):
                for h in range(NT // HALF):
                    for ct in range(CT):
                        for j in range(h * HALF // P, (h + 1) * HALF // P):
                            last = pe.transpose(tp[:, ct, j * P:(j + 1) * P], m.tok[:, j, ct * P:(ct + 1) * P], m.ident[:, :])
                        last.then_inc(s_turned, 1)

            @block.vector
            def _(dve):
                for h in range(NT // HALF):
                    t = slice(h * HALF, (h + 1) * HALF)
                    dve.wait_ge(s_turned, 2 * h + 1)
                    dve.tensor_copy(m.hT[:, 0, t], tp[:, 0, t])

            @block.scalar
            def _(act):
                for h in range(NT // HALF):
                    t = slice(h * HALF, (h + 1) * HALF)
                    act.wait_ge(s_turned, 2 * h + 2)
                    act.activation(m.hT[:, 1, t], tp[:, 1, t], ACT.Copy)



L3_I = 1024


def swiglu_rms(nc, m, name, x, w_gate, w_up, mean, ln, h, top, rinv):
    with Stage(nc, name) as st:
        gate, up = st.ps("gate", [P, 2, HALF]), st.ps("up", [P, 2, HALF])
        act_out = st.sb("act_out", [P, 2, HALF])
        product, square = st.sb("product", [P, 2, L3_I]), st.sb("square", [P, L3_I])
        ssum, rms = st.sb("ssum", [P, TT]), st.sb("rms", [P, TT])
        scales = st.sb("scales", [P, 2, TT])
        own_dve, s_scales, s_sum, s_act, s_product, s_sq, s_h, s_var, s_rms = (
            st.sem(n) for n in ("own_dve", "scales", "sum", "act", "product", "sq", "h", "var", "rms"))
        CH = L3_I // HALF
        banks = [(j, c) for j in range(TT) for c in range(CH)]
        with nc.Block() as block:
            @block.tensor
            def _(pe):
                for n, (j, c) in enumerate(banks):
                    if n >= 2:
                        pe.wait_ge(s_product, n - 1)
                    for into, w in ((gate, w_gate), (up, w_up)):
                        for ct in range(CT):
                            last = pe.matmul(into[:, n % 2, :], x[:, ct, j * P:(j + 1) * P], w[:, ct, c * HALF:(c + 1) * HALF],
                                             start=ct == 0, stop=ct == CT - 1)
                    last.then_inc(s_sum, 1)

            @block.scalar
            def _(act):
                act.wait_ge(s_scales, 1)

                def squares(j):
                    act.wait_ge(s_product, CH * (j + 1))
                    if j:
                        act.wait_ge(s_sq, j)
                    act.activation(square[:, :], product[:, j % 2, :], ACT.Square, accum_out=ssum[:, j:j + 1]).then_inc(s_sq, 1)
                for n, (j, c) in enumerate(banks):
                    act.wait_ge(s_sum, n + 1)
                    if n >= 2:
                        act.wait_ge(s_product, n - 1)
                    act.activation(act_out[:, n % 2, :], gate[:, n % 2, :], ACT.Silu, scale=scales[:, 0, j:j + 1]).then_inc(s_act, 1)
                    if c == 0 and j:
                        squares(j - 1)
                squares(TT - 1)
                act.wait_ge(s_var, 1)
                act.activation(rms[:, :], rinv[:, :], ACT.Sqrt).then_inc(s_rms, 1)

            @block.gpsimd
            def _(pool):
                for j in range(TT):
                    pool.wait_ge(s_product, CH * (j + 1))
                    pool.tensor_tensor(h[:, j, :], product[:, j % 2, :], ln[:, :], ALU.mult).then_inc(s_h, 1)

            @block.vector
            def _(dve):
                own = Tally(dve, own_dve)
                dve.tensor_scalar(scales[:, 0, :], m.inv[:, :], mean[:, 0:1], None, ALU.mult).then_inc(s_scales, 1)
                own.link(dve.tensor_scalar(scales[:, 1, :], m.inv[:, :], mean[:, 1:2], None, ALU.mult))

                def maximum(j):
                    dve.wait_ge(s_h, j + 1)
                    dve.tensor_reduce(top[:, j:j + 1], h[:, j, :], AX.X, ALU.max, apply_absolute_value=True)
                for n, (j, c) in enumerate(banks):
                    dve.wait_ge(s_act, n + 1)
                    if j >= 2 and c == 0:
                        dve.wait_ge(s_h, j - 1)
                        dve.wait_ge(s_sq, j - 1)
                    dve.scalar_tensor_tensor(out=product[:, j % 2, c * HALF:(c + 1) * HALF], in0=up[:, n % 2, :],
                                             scalar=scales[:, 1, j:j + 1], in1=act_out[:, n % 2, :],
                                             op0=ALU.mult, op1=ALU.mult).then_inc(s_product, 1)
                    if j >= 2 and c == 0:
                        maximum(j - 2)
                dve.wait_ge(s_sq, TT)
                dve.tensor_scalar(rinv[:, :], ssum[:, :], 1.0 / L3_I, 1e-6, ALU.mult, ALU.add).then_inc(s_var, 1)
                maximum(TT - 2)
                maximum(TT - 1)
                dve.wait_ge(s_rms, 1)
                dve.reciprocal(rinv[:, :], rms[:, :])


def build(nc, m, d, out):
    ctx = ExitStack()
    with ctx:
        def sb(name, shape, dt=F32):
            return ctx.enter_context(nc.sbuf_tensor(name, shape, dt))
        m.xT, m.hT = sb("xT", [P, CT, NT]), sb("hT", [P, CT, NT])
        m.tok = sb("tok", [P, TT, C])
        m.inv, m.inv_row = sb("inv", [P, TT]), sb("inv_row", [P, NT])
        m.gain = sb("gain", [P, CONDS, CT, NT])
        m.ident, m.ones = sb("ident", [P, P]), sb("ones", [P, P])
        m.ident_b = sb("ident_b", [P, P], BF16)
        m.mask_causal, m.mask_window = sb("mask_causal", [P, 3 * P], BF16), sb("mask_window", [P, 3 * P], BF16)
        m.ones_b, m.earlier, m.iota = sb("ones_b", [P, P], BF16), sb("earlier", [P, P], BF16), sb("iota", [P, E])
        m.rank = sb("rank", [P, L0_E])
        m.wu, m.condT = sb("wu", [P, 2, 2 * CONDS, CT]), sb("condT", [64, B])
        m.slots_in_1 = nc.dram_tensor("slots_in_1", (64 * 64, C), F32).ap()
        m.slots_in_2 = nc.dram_tensor("slots_in_2", (64 * 128, C), F32).ap()
        m.slots_out_1 = nc.dram_tensor("slots_out_1", (64 * 64, C), F32).ap()
        m.slots_out_2 = nc.dram_tensor("slots_out_2", (64 * 128, C), F32).ap()
        moves = ctx.enter_context(Stage(nc, "moves"))
        m.moves_1, m.moves_2 = ((moves.sem(f"scattered_{n}"), [[moves.sem(f"gathered_{n}_{odd}_{j}") for j in range(TT)] for odd in (0, 1)])
                                for n in (1, 2))
        load_constants(nc, m, d)
        with weights_l0(nc, d) as w:
            condition_gains(nc, m, d, "gains01", 0)
            w.arrive()
            layer0(nc, m, w)
        with weights_l1(nc, d) as w:
            with weights_l0f(nc, d) as w_ffn:
                w.start(*w.pairs)
                layer0_ffn(nc, m, w_ffn)
            layer1(nc, m, d, w)
        layers123(nc, m, d)
        with Stage(nc, "end") as st:
            stored = st.sem("stored")
            with nc.Block() as block:
                @block.sync
                def _(sp):
                    sp.dma_start(out, m.xT[:]).then_inc(stored, 16)
                    sp.wait_ge(stored, 16)


def layers123(nc, m, d):
    with weights_l2f(nc, d) as w_ffn:
        with weights_l2(nc, d) as w:
            with Stage(nc, "l1h") as st:
                r = Routing(st, 6, m.moves_1)
                with weights_l1f(nc, d) as w1:
                    layer1_ffn(nc, m, d, w1, r)
                condition_gains(nc, m, d, "gains23", CONDS, Combining(st, m, r, m.slots_out_1))
            w.arrive()
            w_ffn.arrive()
            layer2(nc, m, d, w)
        with weights_l3(nc, d) as w, weights_l3f(nc, d) as w3:
            layer2_ffn(nc, m, d, w_ffn, w, w3)
            layer3(nc, m, w)
            layer3_ffn(nc, m, w3)


def weights_l0(nc, d):
    st = Weights(nc, "l0")
    st.w_qk, st.w_v, st.w_o = st.sb("w_qk", [P, CT, 2 * GROUPS * P]), st.sb("w_v", [P, CT, C]), st.sb("w_o", [P, CT, C])
    st.start((st.w_qk[:], d["l0_w_qk"]), (st.w_v[:], d["l0_w_v"]), (st.w_o[:], d["l0_w_o"]))
    return st


def layer0(nc, m, w):
    with Stage(nc, "l0a") as st:
        t_qk, t_v, t_o = (st.sb(n, t.shape, BF16) for n, t in (("t_qk", w.w_qk), ("t_v", w.w_v), ("t_o", w.w_o)))
        mean, xq = st.sb("mean", [P, 2]), st.sb("xq", [P, CT, NT], BF16)
        quantize_weights(nc, m, "l0_ternary", [([(w.w_qk[:], t_qk[:]), (w.w_v[:], t_v[:])], 3 * C * C), ([(w.w_o[:], t_o[:])], C * C)],
                         mean)
        apply_condition(nc, m, "l0_cond", 0, tok=True)
        quantize_tokens(nc, m, "l0_quant", m.tok, xq, C)
        attention_small_heads(nc, m, "l0_attn", xq, t_qk, t_v, True, 16 ** -0.5, mean=mean[:, 0:1])
        quantize_tokens(nc, m, "l0_quant2", m.tok, xq, C)
        add_product(nc, m, "l0_out", t_o, xq, mean=mean[:, 1:2])


def weights_l0f(nc, d):
    st = Weights(nc, "l0f")
    st.w_g, st.w_a, st.w_b = st.sb("w_g", [P, CT, L0_E]), st.sb("w_a", [P, CT, L0_E * L0_R]), st.sb("w_b", [P, 4, C])
    st.select = st.sb("select", [L0_E, 4, P])
    st.start((st.w_g[:], d["l0_w_g"]), (st.w_a[:], d["l0_w_a"]), (st.w_b[:], d["l0_w_b"]), (st.select[:], d["l0_select"]))
    return st


def layer0_ffn(nc, m, w):
    with Stage(nc, "l0g") as st:
        gates, inner = st.sb("gates", [P, 4, NT]), st.sb("inner", [P, 4, NT])
        apply_condition(nc, m, "l0_cond2", 1)
        w.arrive()
        argmax_gates(nc, m, "l0_gates", w.w_g, w.select, gates)
        gated_inner(nc, m, "l0_inner", w.w_a, gates, inner)
        add_product(nc, m, "l0_down", w.w_b, inner)


def weights_l1(nc, d):
    st = Weights(nc, "l1a")
    st.w_q, st.w_k, st.w_v = (st.sb(n, [P, CT, NH * P]) for n in ("w_q", "w_k", "w_v"))
    st.w_o = st.sb("w_o", [P, NH, C])
    st.pairs = ((st.w_q[:], d["l1_w_q"]), (st.w_v[:], d["l1_w_v"]), (st.w_k[:], d["l1_w_k"]), (st.w_o[:], d["l1_w_o"]))
    return st


def layer1(nc, m, d, w):
    apply_condition(nc, m, "l1_cond", 2)
    attention_wide_heads(nc, m, d, "l1_attn", w)


L1_SH = 512


def weights_l1f(nc, d):
    st = Weights(nc, "l1f")
    st.w_g, st.bias = st.sb("w_g", [P, CT, E]), st.sb("bias", [P, E])
    st.w_su, st.w_sd = st.sb("w_su", [P, CT, L1_SH]), st.sb("w_sd", [P, L1_SH // P, C])
    st.start((st.w_g[:], d["l1_w_g"]), (st.bias[:], d["l1_bias"]), (st.w_su[:], d["l1_w_su"]), (st.w_sd[:], d["l1_w_sd"]))
    return st


def layer1_ffn(nc, m, d, w, r):
    with Stage(nc, "l1g") as st:
        inner = st.sb("inner", [P, L1_SH // P, NT])
        apply_condition(nc, m, "l1_cond2", 3, tok=True)
        w.arrive()
        route(nc, m, "l1_route", w.w_g, w.bias, r, 64, MASKED)
        dispatch(nc, m, "l1_dispatch", r, m.slots_in_1, w.w_su, None, w.w_sd, inner, P)
        experts(nc, m, "l1_experts", m.slots_in_1, m.slots_out_1, d["l1_w_e"], 2, P, False)


L2_I = 88


def weights_l2(nc, d):
    st = Weights(nc, "l2a")
    st.w, st.bias, st.w_o, st.b_o = st.sb("w", [P, CT, 3 * C]), st.sb("bias", [P, 3 * C]), st.sb("w_o", [P, CT, C]), st.sb("b_o", [P, CT])
    st.start((st.w[:], d["l2_w"]), (st.bias[:], d["l2_bias"]), (st.w_o[:], d["l2_w_o"]), (st.b_o[:], d["l2_b_o"]))
    return st


def layer2(nc, m, d, w):
    with Stage(nc, "l2b") as st:
        qkv = st.sb("qkv", [P, TT, 3 * C])
        apply_condition(nc, m, "l2_cond", 0)
        qkv_tokens(nc, m, "l2_qkv", w.w, w.bias, qkv)
        attention_over_batch(nc, m, d, "l2_attn", qkv)
        turn_tokens(nc, m, "l2_turn")
        add_product(nc, m, "l2_out", w.w_o, m.hT, bias=w.b_o)


def weights_l2f(nc, d):
    st = Weights(nc, "l2f")
    st.w_g, st.bias = st.sb("w_g", [P, CT, E]), st.sb("bias", [P, E])
    st.w_sg, st.w_su, st.w_sd = st.sb("w_sg", [P, CT, L2_I]), st.sb("w_su", [P, CT, L2_I]), st.sb("w_sd", [L2_I, 1, C])
    st.start((st.w_g[:], d["l2_w_g"]), (st.bias[:], d["l2_ebias"]), (st.w_sg[:], d["l2_w_sg"]), (st.w_su[:], d["l2_w_su"]),
             (st.w_sd[:], d["l2_w_sd"]))
    return st


def layer2_ffn(nc, m, d, w, w3a, w3):
    with Stage(nc, "l2g") as st:
        inner = st.sb("inner", [L2_I, 1, NT])
        r = Routing(st, 8, m.moves_2)
        apply_condition(nc, m, "l2_cond2", 1, tok=True)
        route(nc, m, "l2_route", w.w_g, w.bias, r, 128, 0.0)
        dispatch(nc, m, "l2_dispatch", r, m.slots_in_2, w.w_su, w.w_sg, w.w_sd, inner, L2_I)
        experts(nc, m, "l2_experts", m.slots_in_2, m.slots_out_2, d["l2_w_e"], 1, L2_I, True)
        w3a.arrive()
        w3.arrive()
        combine(nc, m, "l2_combine", r, m.slots_out_2, [([(a[:], t[:])], L3_I * C) for a, t in w3.ternary], w3.mean,
                (w3a.low, w3a.up, [w3a.w_qk[:, :, 0:GROUPS * P], w3a.w_qk[:, :, GROUPS * P:], w3a.w_v[:], w3a.w_o[:]]))


def weights_l3(nc, d):
    st = Weights(nc, "l3a")
    st.w_qk, st.w_v, st.w_o = st.sb("w_qk", [P, CT, 2 * GROUPS * P]), st.sb("w_v", [P, CT, C]), st.sb("w_o", [P, CT, C])
    st.low, st.up = st.sb("low", [16, 4, C]), st.sb("up", [16, 2 * GROUPS * P + 2 * C])
    st.qk_bias, st.v_bias, st.b_o = st.sb("qk_bias", [P, 2 * GROUPS]), st.sb("v_bias", [P, C]), st.sb("b_o", [P, CT])
    st.start(*((t[:], d["l3_" + n]) for t, n in (
        (st.w_qk, "w_qk"), (st.w_v, "w_v"), (st.w_o, "w_o"), (st.low, "low"), (st.up, "up"),
        (st.qk_bias, "qk_bias"), (st.v_bias, "v_bias"), (st.b_o, "b_o"))))
    return st


def layer3(nc, m, w):
    apply_condition(nc, m, "l3_cond", 2)
    attention_small_heads(nc, m, "l3_attn", m.hT, w.w_qk, w.w_v, False, 16 ** -0.5, w.qk_bias, w.v_bias)
    turn_tokens(nc, m, "l3_turn")
    add_product(nc, m, "l3_out", w.w_o, m.hT, bias=w.b_o)


def weights_l3f(nc, d):
    st = Weights(nc, "l3f")
    st.w_g, st.w_u, st.w_d = st.sb("w_g", [P, CT, L3_I]), st.sb("w_u", [P, CT, L3_I]), st.sb("w_d", [P, L3_I // P, C])
    st.ln = st.sb("ln", [P, L3_I])
    st.t_g, st.t_u, st.t_d = (st.sb(n, t.shape, BF16) for n, t in (("t_g", st.w_g), ("t_u", st.w_u), ("t_d", st.w_d)))
    st.ternary, st.mean = ((st.w_g, st.t_g), (st.w_u, st.t_u), (st.w_d, st.t_d)), st.sb("mean", [P, 3])
    st.start((st.w_g[:], d["l3_w_g"]), (st.w_u[:], d["l3_w_u"]), (st.w_d[:], d["l3_w_d"]), (st.ln[:], d["l3_ln"]))
    return st


def layer3_ffn(nc, m, w):
    with Stage(nc, "l3g") as st:
        mean, xq = w.mean, st.sb("xq", [P, CT, NT], BF16)
        h, hq = st.sb("h", [P, TT, L3_I]), st.sb("hq", [P, L3_I // P, NT], BF16)
        apply_condition(nc, m, "l3_cond2", 3, tok=True)
        quantize_tokens(nc, m, "l3_quant", m.tok, xq, C)
        top, rinv = st.sb("top", [P, TT]), st.sb("rinv", [P, TT])
        swiglu_rms(nc, m, "l3_swiglu", xq, w.t_g, w.t_u, mean, w.ln, h, top, rinv)
        quantize_tokens(nc, m, "l3_quant2", h, hq, L3_I, (top, rinv))
        add_product(nc, m, "l3_down", w.t_d, hq, mean=mean[:, 2:3])



def rows(a):
    a = np.asarray(a)
    return np.ascontiguousarray(a.reshape(-1, P, a.shape[-1]).transpose(1, 0, 2))


def spread_heads(wT):
    a = np.zeros((wT.shape[0], NH, 32), wT.dtype)
    a[:, :, :16] = wT.reshape(-1, NH, 16)
    return a.reshape(wT.shape[0], -1)


def layouts(i):
    conds = [f"L{l}_cond{n}_" for l in range(4) for n in ("", "2")]
    i = {k: np.asarray(v) for k, v in i.items()}
    qkv = i["L0_attn_w_qkv"].T
    row, col = np.arange(P)[:, None], np.arange(P)[None, :]
    bf16 = np.dtype("bfloat16")
    freq = (np.float32(1) / np.float32(10000) ** (np.arange(0, P, 2, dtype=np.float32) / np.float32(P))).astype(np.float32)
    angle = np.tile((np.arange(T, dtype=np.float32)[:, None] * freq).T, (2, 1))
    freq2 = (np.float32(1) / np.float32(10000) ** (np.arange(0, L2_D, 2, dtype=np.float32) / np.float32(L2_D))).astype(np.float32)
    angle2 = np.tile(np.arange(B, dtype=np.float32)[:, None] * freq2, (1, 2))
    causal, window = np.where(col <= row, 0, MASKED), np.where(col > row, 0, MASKED)
    return {
        "xT": rows(i["x"].reshape(NT, C).T),
        "fsideT": rows(i["fside_BxSxS_0"].reshape(NT, C).T),
        "condT": np.ascontiguousarray(i["cond_512"].T),
        "wu": np.ascontiguousarray(np.stack([np.stack([i[c + k].reshape(CT, P).T for c in conds], 1) for k in "wu"], 1)),
        "ident": np.eye(P, dtype=np.float32), "ones": np.ones((P, P), np.float32),
        "ident_b": np.eye(P).astype(bf16),
        "mask_causal": np.concatenate([causal, 0 * causal, causal], 1).astype(bf16),
        "mask_window": np.concatenate([causal, window, causal], 1).astype(bf16),
        "l0_w_qk": rows(np.concatenate([spread_heads(qkv[:, :C]), spread_heads(qkv[:, C:2 * C])], 1)),
        "l0_w_v": rows(qkv[:, 2 * C:]),
        "l0_w_o": rows(i["L0_attn_w_proj"].T),
        "rank8": np.broadcast_to(np.arange(L0_E, 0, -1, dtype=np.float32), (P, L0_E)).copy(),
        "l0_w_g": rows(i["L0_ffn_Wg"].T),
        "l0_w_a": rows(i["L0_ffn_A"].reshape(L0_E * L0_R, C).T),
        "l0_w_b": rows(i["L0_ffn_Bw"].transpose(0, 2, 1).reshape(L0_E * L0_R, C)),
        "l0_select": (np.arange(L0_E)[:, None, None] == 2 * np.arange(4)[None, :, None] + np.arange(P)[None, None, :] // L0_R).astype(np.float32),
        "l1_w_q": rows(i["L1_attn_wq"]), "l1_w_k": rows(i["L1_attn_wk"]), "l1_w_v": rows(i["L1_attn_wv"]),
        "l1_w_o": rows(i["L1_attn_wo"]),
        "ones_b": np.ones((P, P), bf16), "earlier": (row < col).astype(bf16),
        "iota": np.broadcast_to(np.arange(E, dtype=np.float32), (P, E)).copy(),
        "l1_w_g": rows(i["L1_ffn_gate_w"].T), "l1_bias": np.broadcast_to(i["L1_ffn_e_bias"], (P, E)).copy(),
        "l1_w_su": rows(i["L1_ffn_shared_up_w"].T), "l1_w_sd": rows(i["L1_ffn_shared_down_w"].T),
        "l1_w_e": np.concatenate([i["L1_ffn_w1"].reshape(32, 2, P, CT, P).transpose(0, 4, 1, 3, 2).reshape(32, P, -1),
                                  i["L1_ffn_w2"].reshape(32, 2, C, P).transpose(0, 3, 1, 2).reshape(32, P, -1)], 2),
        "l2_w": rows(i["L2_attn_qkv_w"]), "l2_bias": np.broadcast_to(i["L2_attn_qkv_b"], (P, 3 * C)).copy(),
        "l2_w_o": rows(i["L2_attn_out_w"]), "l2_b_o": np.ascontiguousarray(i["L2_attn_out_b"].reshape(CT, P).T),
        "l2_cos": np.broadcast_to(np.cos(angle2).astype(np.float32), (P, B, L2_D)).copy(),
        "l2_sin": np.broadcast_to((np.sin(angle2) * np.repeat([-1, 1], L2_D // 2)).astype(np.float32), (P, B, L2_D)).copy(),
        "l2_w_g": rows(i["L2_ffn_router_weight"].T), "l2_ebias": np.broadcast_to(i["L2_ffn_e_bias"], (P, E)).copy(),
        "l2_w_sg": rows(i["L2_ffn_sh_gate"]), "l2_w_su": rows(i["L2_ffn_sh_up"]), "l2_w_sd": i["L2_ffn_sh_down"][:, None, :],
        "l2_w_e": np.concatenate([i["L2_ffn_w_" + n].reshape(E, CT, P, L2_I).transpose(0, 2, 1, 3).reshape(E, P, -1)
                                  for n in ("up", "gate")] + [np.pad(i["L2_ffn_w_down"], ((0, 0), (0, P - L2_I), (0, 0)))], 2),
        "l3_w_qk": rows(np.concatenate([spread_heads(i["L3_attn_Wq"].T), spread_heads(i["L3_attn_Wk"].T)], 1)),
        "l3_w_v": rows(i["L3_attn_Wv"].T), "l3_w_o": rows(i["L3_attn_Wo"].T),
        "l3_low": np.stack([i[f"L3_attn_B{k}"] for k in "qkvo"], 1),
        "l3_up": np.concatenate([spread_heads(i["L3_attn_Aq"].T), spread_heads(i["L3_attn_Ak"].T), i["L3_attn_Av"].T, i["L3_attn_Ao"].T], 1),
        "l3_qk_bias": np.concatenate([spread_heads(i[f"L3_attn_b{k}"][None]).reshape(GROUPS, P).T for k in "qk"], 1).copy(),
        "l3_v_bias": np.broadcast_to(i["L3_attn_bv"], (P, C)).copy(),
        "l3_b_o": np.ascontiguousarray(i["L3_attn_bo"].reshape(CT, P).T),
        "l3_w_g": rows(i["L3_ffn_w_gate"].T), "l3_w_u": rows(i["L3_ffn_w_up"].T), "l3_w_d": rows(i["L3_ffn_w_down"].T),
        "l3_ln": np.broadcast_to(i["L3_ffn_ln_weight"], (P, L3_I)).copy(),
        "l1_cos": np.cos(angle).astype(np.float32),
        "l1_sin": np.concatenate([np.sin(angle[:64]), -np.sin(angle[64:])]).astype(np.float32),
    }


def kernel(**inputs):
    import concourse.bacc as bacc
    from concourse.bass_utils import run_bass_kernel_spmd as run
    arrays = layouts(inputs)
    nc = bacc.Bacc("TRN2", target_bir_lowering=False, num_devices=1)
    d = {k: nc.dram_tensor("in_" + k, v.shape, mybir.dt.from_np(v.dtype), kind="ExternalInput").ap()
         for k, v in arrays.items()}
    out = nc.dram_tensor("out", (P, CT, NT), F32, kind="ExternalOutput").ap()
    build(nc, Core(), d, out)
    r = run(nc, [{"in_" + k: v for k, v in arrays.items()}], core_ids=[0])
    return np.ascontiguousarray(r.results[0]["out"].transpose(1, 0, 2).reshape(C, NT).T.reshape(B, T, C))
```
